# Optimizing a Trainium2 kernel written in Bass

```python
import numpy as np
import jax
import jax.numpy as jnp

def _softmax(x, axis=-1):
    return jax.nn.softmax(x, axis=axis)

def _gelu(x):
    return jax.nn.gelu(x, approximate=True)

def _silu(x):
    return jax.nn.silu(x)

def _sigmoid(x):
    return jax.nn.sigmoid(x)

def _layernorm(x, axis=-1, eps=1e-05):
    m = jnp.mean(x, axis=axis, keepdims=True)
    v = jnp.var(x, axis=axis, keepdims=True)
    return (x - m) / jnp.sqrt(v + eps)

def _scatter_add(tgt, idx, src, axis=0):
    return tgt.at[idx].add(src)

def _segment_sum(src, seg, n):
    return jax.ops.segment_sum(src, seg, n)
kernel_name = 'mk_gnn_preln_d2_gnn_r32_72d554'

def setup_inputs(seed: int=0):
    np.random.seed(seed)
    _w = jnp.asarray

    def _rec_inputs():
        import jax
        import jax.numpy as jnp
        _gk = jax.random.key(seed)
        x = 0.0001755 + 0.9998 * jax.random.normal(jax.random.fold_in(_gk, 1), (3125, 256), jnp.float32)
        _s = jax.random.randint(jax.random.fold_in(_gk, 2), (25000,), 0, 3125, jnp.int32)
        _d = jax.random.randint(jax.random.fold_in(_gk, 3), (25000,), 0, 3125, jnp.int32)
        _loop = jnp.arange(3125, dtype=jnp.int32)
        src = jnp.concatenate([_s, _d, _loop])
        dst = jnp.concatenate([_d, _s, _loop])
        _o = jnp.argsort(dst, stable=True)
        src = src[_o]
        dst = dst[_o]
        edge_attr_64 = jax.random.uniform(jax.random.fold_in(_gk, 12), (53125, 64), jnp.float32, 0.0, 1)
        return (x, src, dst, edge_attr_64)
    x, src, dst, edge_attr_64 = _rec_inputs()

    def _L0_gnn_setup():
        import jax, jax.numpy as jnp
        import numpy as np
        N, E, HID, NRBF = (10000, 10000, 256, 64)
        key = jax.random.key(seed)
        ks = jax.random.split(key, 12)

        def lin(k, fin, fout):
            bound = 1.0 / np.sqrt(fin)
            kw, kb = jax.random.split(k)
            W = jax.random.uniform(kw, (fin, fout), jnp.float32, -bound, bound)
            b = jax.random.uniform(kb, (fout,), jnp.float32, -bound, bound)
            return (W, b)
        W1, b1 = lin(ks[0], NRBF, HID)
        W2, b2 = lin(ks[1], HID, HID)
        U1, c1 = lin(ks[2], 2 * HID, HID)
        U2, c2 = lin(ks[3], HID, HID)
        h = jax.random.normal(ks[4], (N, HID), jnp.float32)
        edge_index = jax.random.randint(ks[5], (2, E), 0, N, jnp.int64)
        rbf = jax.random.uniform(ks[6], (E, NRBF), jnp.float32)
        return {'h': h, 'edge_index': edge_index, 'rbf': rbf, 'W1': W1, 'b1': b1, 'W2': W2, 'b2': b2, 'U1': U1, 'c1': c1, 'U2': U2, 'c2': c2}
    _L0_gnn_all = _L0_gnn_setup()
    _L0_gnn_in = {k: v for k, v in _L0_gnn_all.items() if k in ('W1', 'b1', 'W2', 'b2', 'U1', 'c1', 'U2', 'c2')}
    del _L0_gnn_all

    def _L1_gnn_setup():
        import jax, jax.numpy as jnp
        import numpy as np
        N_NODES = 50000
        N_EDGES = 25000
        D_IN = 256
        D_HID = 256
        D_OUT = 256
        GAMMA = 0.0
        K_STEPS = 6

        def _spmm(h, src, dst, inv_deg):
            msg = h[src]
            agg = jax.ops.segment_sum(msg, dst, num_segments=h.shape[0])
            return agg * inv_deg[:, None]

        def _linear_diffusion(h, src, dst, gamma=GAMMA, k=K_STEPS):
            n = h.shape[0]
            deg = jax.ops.segment_sum(jnp.ones((src.shape[0],), h.dtype), dst, num_segments=n)
            inv_deg = 1.0 / jnp.clip(deg, 1.0)
            out = h
            term = h
            for i in range(1, k + 1):
                term = (_spmm(term, src, dst, inv_deg) + gamma * term) / float(i)
                out = out + term
            return out
        key = jax.random.key(seed)
        ks = jax.random.split(key, 8)
        h = jax.random.normal(ks[0], (N_NODES, D_IN), dtype=jnp.float32)
        src = jax.random.randint(ks[1], (N_EDGES,), 0, N_NODES, dtype=jnp.int64)
        dst = jax.random.randint(ks[2], (N_EDGES,), 0, N_NODES, dtype=jnp.int64)
        s_in = 1.0 / np.sqrt(D_IN)
        s_hid = 1.0 / np.sqrt(D_HID)
        W_in = jax.random.uniform(ks[3], (D_HID, D_IN), jnp.float32, -s_in, s_in)
        b_in = jax.random.uniform(ks[4], (D_HID,), jnp.float32, -s_in, s_in)
        W_out = jax.random.uniform(ks[5], (D_OUT, D_HID), jnp.float32, -s_hid, s_hid)
        b_out = jax.random.uniform(ks[6], (D_OUT,), jnp.float32, -s_hid, s_hid)
        return {'h': h, 'src': src, 'dst': dst, 'W_in': W_in, 'b_in': b_in, 'W_out': W_out, 'b_out': b_out}
    _L1_gnn_all = _L1_gnn_setup()
    _L1_gnn_in = {k: v for k, v in _L1_gnn_all.items() if k in ('W_in', 'b_in', 'W_out', 'b_out')}
    del _L1_gnn_all
    return {'x': x, 'src': src, 'dst': dst, 'edge_attr_64': edge_attr_64, 'L0_gnn_W1': _L0_gnn_in['W1'], 'L0_gnn_b1': _L0_gnn_in['b1'], 'L0_gnn_W2': _L0_gnn_in['W2'], 'L0_gnn_b2': _L0_gnn_in['b2'], 'L0_gnn_U1': _L0_gnn_in['U1'], 'L0_gnn_c1': _L0_gnn_in['c1'], 'L0_gnn_U2': _L0_gnn_in['U2'], 'L0_gnn_c2': _L0_gnn_in['c2'], 'L1_gnn_W_in': _L1_gnn_in['W_in'], 'L1_gnn_b_in': _L1_gnn_in['b_in'], 'L1_gnn_W_out': _L1_gnn_in['W_out'], 'L1_gnn_b_out': _L1_gnn_in['b_out']}

def reference(x, src, dst, edge_attr_64, L0_gnn_W1, L0_gnn_b1, L0_gnn_W2, L0_gnn_b2, L0_gnn_U1, L0_gnn_c1, L0_gnn_U2, L0_gnn_c2, L1_gnn_W_in, L1_gnn_b_in, L1_gnn_W_out, L1_gnn_b_out):
    import jax
    import jax.numpy as jnp

    def _L0_gnn_ref(h, edge_index, rbf, W1, b1, W2, b2, U1, c1, U2, c2):
        import jax, jax.numpy as jnp
        import numpy as np
        N, E, HID, NRBF = (10000, 10000, 256, 64)
        src, dst = (edge_index[0], edge_index[1])
        gate = jax.nn.sigmoid(jax.nn.silu(rbf @ W1 + b1) @ W2 + b2)
        msg = gate * h[src]
        aggr = jax.ops.segment_sum(msg, dst, num_segments=h.shape[0])
        upd = jax.nn.silu(jnp.concatenate([h, aggr], axis=-1) @ U1 + c1) @ U2 + c2
        return h + upd

    def _L1_gnn_ref(h, src, dst, W_in, b_in, W_out, b_out):
        import jax, jax.numpy as jnp
        import numpy as np
        N_NODES = 50000
        N_EDGES = 25000
        D_IN = 256
        D_HID = 256
        D_OUT = 256
        GAMMA = 0.0
        K_STEPS = 6

        def _spmm(h, src, dst, inv_deg):
            msg = h[src]
            agg = jax.ops.segment_sum(msg, dst, num_segments=h.shape[0])
            return agg * inv_deg[:, None]

        def _linear_diffusion(h, src, dst, gamma=GAMMA, k=K_STEPS):
            n = h.shape[0]
            deg = jax.ops.segment_sum(jnp.ones((src.shape[0],), h.dtype), dst, num_segments=n)
            inv_deg = 1.0 / jnp.clip(deg, 1.0)
            out = h
            term = h
            for i in range(1, k + 1):
                term = (_spmm(term, src, dst, inv_deg) + gamma * term) / float(i)
                out = out + term
            return out
        x = h @ W_in.T + b_in
        x = jax.nn.silu(x)
        x = _linear_diffusion(x, src, dst)
        x = x @ W_out.T + b_out
        return x
    edge_index = jnp.stack([src, dst])
    h = jnp.maximum(_layernorm(x, axis=-1), 0.0)
    x = x + _L0_gnn_ref(h, edge_index, edge_attr_64, L0_gnn_W1, L0_gnn_b1, L0_gnn_W2, L0_gnn_b2, L0_gnn_U1, L0_gnn_c1, L0_gnn_U2, L0_gnn_c2)
    h = jnp.maximum(_layernorm(x, axis=-1), 0.0)
    x = x + _L1_gnn_ref(h, src, dst, L1_gnn_W_in, L1_gnn_b_in, L1_gnn_W_out, L1_gnn_b_out)
    return x

_drawn_inputs = setup_inputs


def setup_inputs(seed=0):
    import zlib

    import numpy as np

    out = dict(_drawn_inputs(seed))
    spreads = {}
    factors = {'edge_attr_64': 8.0,
     'L0_gnn_W1': 3.922,
     'L0_gnn_b1': 8.0,
     'L0_gnn_W2': 3.744,
     'L0_gnn_b2': 63.355,
     'L0_gnn_c1': 8.0,
     'L1_gnn_b_in': 3.187,
     'L0_gnn_c2': 2.694,
     'L1_gnn_b_out': 2.726}
    for name, (base, spread) in spreads.items():
        noise = np.random.default_rng([zlib.crc32(name.encode()), seed]).standard_normal(out[name].shape)
        drawn = base * np.exp(spread * noise) if base else spread * noise
        out[name] = jnp.asarray(drawn.astype(out[name].dtype))
    for name, factor in factors.items():
        out[name] = (out[name] * factor).astype(out[name].dtype)
    return out
```

```python
import concourse.bass as bass
from concourse import mybir
from contextlib import ExitStack

FP32 = mybir.dt.float32
FP16 = mybir.dt.float16
BF16 = mybir.dt.bfloat16
I32 = mybir.dt.int32
U32 = mybir.dt.uint32
ALU = mybir.AluOpType
ACT = mybir.ActivationFunctionType
AX = mybir.AxisListType

N_NODES = 3125
N_EDGES = 53125
D = 256
R = 64
P = 125
NT = N_NODES // P
EC = N_EDGES // P
NSTEPS = 6
EPS = 1e-5

WIN = 128
NW = 4
GRP = WIN * NW
NG = (N_EDGES - NT) // GRP + NT + 1
NG += 1 - NG % 2
CHK = 114
SLOT = 25
NCH = EC // SLOT
MAGIC = 1.5 * 2.0 ** 23
HALF = D // 2
LOW = 2048.0


class Link:

    def __init__(self, eng, sem):
        self.eng, self.sem, self.n = eng, sem, 0

    def __call__(self, ins):
        self.n += 1
        ins.then_inc(self.sem, 1)
        self.eng.wait_ge(self.sem, self.n)


def constants_and_node_norm(nc, t, x, h_dram):
    with ExitStack() as ctx:
        sb = lambda n, s, d: ctx.enter_context(nc.sbuf_tensor(n, s, d))
        sem = lambda n: ctx.enter_context(nc.semaphore(n))
        xs = sb("xs", [P, NT, D], FP32)
        hs = sb("hs", [P, NT, D], FP32)
        stats = sb("stats", [P, NT, 6], FP32)
        mv = sb("mv", [P, NT, 2], FP32)
        rstd = sb("rstd", [P, NT], FP32)
        nmr = sb("nmr", [P, NT], FP32)
        x_in, made, chain, var_ready, std_ready, norm_ready, h_ready, h_out = (
            sem(n) for n in ("x_in", "made", "norm_chain", "var_ready", "std_ready", "norm_ready", "h_ready", "h_out"))
        block = ctx.enter_context(nc.Block())

        @block.sync
        def _(sp):
            sp.dma_start(xs[:, :, :], x.rearrange("(n p) d -> p n d", p=P)).then_inc(x_in, 16)
            sp.wait_ge(h_ready, 1)
            sp.dma_start(h_dram.rearrange("(n p) d -> p n d", p=P), hs[:, :, :]).then_inc(h_out, 16)
            sp.wait_ge(h_out, 16)

        @block.gpsimd
        def _(pool):
            pool.memset(t.ident[:, :], 0.0).then_inc(made, 1)
            pool.memset(t.before[:, :], 1.0).then_inc(made, 1)
            pool.memset(t.ones[:, :], 1.0).then_inc(made, 1)
            pool.memset(t.ones_h[:, :], 1.0).then_inc(made, 1)
            pool.iota(t.cols_i[:, :], pattern=[[1, 500]], base=0, channel_multiplier=0).then_inc(made, 1)
            pool.wait_ge(made, 5)
            pool.affine_select(out=t.ident[:, :], in_=t.ident[:, :], compare_op=ALU.not_equal, fill=1.0,
                               base=0, pattern=[[-1, 128]], channel_multiplier=1).then_inc(made, 1)
            pool.affine_select(out=t.before[:, :], in_=t.before[:, :], compare_op=ALU.is_gt, fill=0.0,
                               base=0, pattern=[[1, 128]], channel_multiplier=-1).then_inc(made, 1)
            pool.tensor_copy(t.cols[:, :], t.cols_i[:, :]).then_inc(made, 1)
            pool.wait_ge(made, 8)

        @block.vector
        def _(dve):
            link = Link(dve, chain)
            dve.wait_ge(x_in, 16)
            for n in range(NT):
                last = nc.vector.bn_stats(stats[:, n, :], xs[:, n, :])
            link(last)
            for n in range(NT):
                last = nc.vector.bn_aggr(mv[:, n, :], stats[:, n, :])
            link(last)
            link(nc.vector.tensor_scalar(rstd[:, :], mv[:, :, 1], EPS, None, ALU.add))
            nc.vector.reciprocal(nmr[:, :], rstd[:, :]).then_inc(var_ready, 1)
            dve.wait_ge(std_ready, 1)
            nc.vector.scalar_tensor_tensor(out=nmr[:, :], in0=mv[:, :, 0], scalar=-1.0, in1=rstd[:, :],
                                           op0=ALU.mult, op1=ALU.mult).then_inc(norm_ready, 1)

        @block.scalar
        def _(act):
            act.wait_ge(var_ready, 1)
            nc.scalar.activation(rstd[:, :], nmr[:, :], ACT.Sqrt).then_inc(std_ready, 1)
            act.wait_ge(norm_ready, 1)
            for n in range(NT):
                last = nc.scalar.activation(hs[:, n, :], xs[:, n, :], ACT.Relu, bias=nmr[:, n:n + 1],
                                            scale=rstd[:, n:n + 1])
            last.then_inc(h_ready, 1)


def edge_tables(nc, t, src, dst):
    with ExitStack() as ctx:
        sb = lambda n, s, d: ctx.enter_context(nc.sbuf_tensor(n, s, d))
        sem = lambda n: ctx.enter_context(nc.semaphore(n))
        here = sb("here", [CHK, (N_EDGES - 1) // CHK], I32)
        after = sb("after", [CHK, (N_EDGES - 1) // CHK], I32)
        falls = sb("falls", [CHK, 1], FP32)
        hot = sb("hot", [P, 2, EC], FP32)
        cnt = sb("cnt", [P, NT], FP32)
        tot = sb("tot", [128, NT], FP32)
        tab = sb("tab", [128, 5, NT], FP32)
        jump = sb("jump", [128, 2, NG], FP32)
        row_f = sb("row_f", [128, NG], FP32)
        ps = ctx.enter_context(nc.psum_tensor("ps_sort", [128, 512], FP32))
        ids_in, next_in, chain, counted, totals = (sem(n) for n in ("ids_in", "next_in", "tables_chain", "counted", "totals"))
        block = ctx.enter_context(nc.Block())

        @block.sync
        def _(sp):
            sp.dma_start(t.dst_i[:, :], dst.rearrange("(p c) -> p c", p=P)).then_inc(ids_in, 16)
            sp.dma_start(here[:, :], dst[0:N_EDGES - 1].rearrange("(p c) -> p c", p=CHK)).then_inc(next_in, 16)
            sp.dma_start(after[:, :], dst[1:N_EDGES].rearrange("(p c) -> p c", p=CHK)).then_inc(next_in, 16)

        @block.tensor
        def _(pe):
            pe.wait_ge(counted, 1)
            nc.tensor.matmul(ps[0:128, 0:NT], t.before[0:P, :], cnt[:, :], start=True, stop=True)
            nc.tensor.matmul(ps[0:128, 64:64 + NT], t.ones[0:P, :], cnt[:, :], start=True, stop=True)
            nc.tensor.matmul(ps[0:128, 128:129], t.ones[0:CHK, :], falls[:, :], start=True, stop=True).then_inc(totals, 1)

        @block.vector
        def _(dve):
            link = Link(dve, chain)
            v = nc.vector
            dve.wait_ge(ids_in, 16)
            link(v.tensor_copy(t.dst_f[:, :], t.dst_i[:, :]))
            link(v.tensor_scalar(t.bucket[:, :], t.dst_f[:, :], -float(P // 2), 1.0 / P, ALU.add, ALU.mult))
            link(v.tensor_scalar(t.bucket[:, :], t.bucket[:, :], MAGIC, None, ALU.add))
            link(v.tensor_scalar(t.bucket[:, :], t.bucket[:, :], MAGIC, None, ALU.subtract))
            n0 = link.n
            with dve.Fori(0, NT) as b:
                v.tensor_scalar(hot[:, 0, :], t.bucket[:, :], t.cols[0:P, bass.ds(b, 1)], None, ALU.is_equal).then_inc(chain, 1)
                dve.wait_ge(chain, b * 2 + (n0 + 1))
                v.tensor_reduce(cnt[:, bass.ds(b, 1)], hot[:, 0, :], AX.X, ALU.add).then_inc(chain, 1)
                dve.wait_ge(chain, b * 2 + (n0 + 2))
            link.n = n0 + 2 * NT
            dve.wait_ge(next_in, 32)
            wide = hot[0:CHK, :, :].rearrange("p a b -> p (a b)")[:, 0:(N_EDGES - 1) // CHK]
            link(v.tensor_tensor(wide, after[:, :], here[:, :], ALU.is_lt))
            v.tensor_reduce(falls[:, :], wide, AX.X, ALU.add).then_inc(counted, 1)
            dve.wait_ge(totals, 1)
            link(v.tensor_copy(t.unsorted[:, :], ps[:, 128:129]))
            link(v.tensor_copy(tot[:, :], ps[:, 64:64 + NT]))
            link(v.tensor_tensor_scan(tab[:, 0, :], t.ones[:, 0:NT], tot[:, :], 0.0, ALU.mult, ALU.add))
            link(v.tensor_tensor(tab[:, 0, :], tab[:, 0, :], tot[:, :], ALU.subtract))
            link(v.tensor_tensor(t.base[:, :], ps[0:P, 0:NT], tab[0:P, 0, :], ALU.add))
            link(v.tensor_scalar(tab[:, 1, :], tot[:, :], GRP / 2 - 0.5, 1.0 / GRP, ALU.add, ALU.mult))
            link(v.tensor_scalar(tab[:, 1, :], tab[:, 1, :], MAGIC, None, ALU.add))
            link(v.tensor_scalar(tab[:, 1, :], tab[:, 1, :], MAGIC, None, ALU.subtract))
            link(v.tensor_tensor_scan(tab[:, 2, :], t.ones[:, 0:NT], tab[:, 1, :], 0.0, ALU.mult, ALU.add))
            link(v.tensor_tensor(tab[:, 2, :], tab[:, 2, :], tab[:, 1, :], ALU.subtract))
            link(v.scalar_tensor_tensor(out=tab[:, 3, :], in0=tab[:, 2, :], scalar=-float(GRP), in1=tab[:, 0, :],
                                        op0=ALU.mult, op1=ALU.add))
            link(v.tensor_tensor(tab[:, 4, 1:NT], tab[:, 3, 1:NT], tab[:, 3, 0:NT - 1], ALU.subtract))
            link(v.tensor_scalar(row_f[:, :], t.cols[:, 0:NG], float(GRP), None, ALU.mult))
            link(v.memset(t.group_bucket[:, :], 0.0))
            n1 = link.n
            with dve.Fori(1, NT) as b:
                v.tensor_scalar(jump[:, 0, :], t.cols[:, 0:NG], tab[:, 2, bass.ds(b, 1)], None, ALU.is_ge).then_inc(chain, 1)
                v.tensor_scalar(jump[:, 1, :], t.cols[:, 0:NG], tab[:, 2, bass.ds(b, 1)], tab[:, 4, bass.ds(b, 1)],
                                ALU.is_ge, ALU.mult).then_inc(chain, 1)
                dve.wait_ge(chain, b * 4 + (n1 - 2))
                v.tensor_tensor(t.group_bucket[:, :], t.group_bucket[:, :], jump[:, 0, :], ALU.add).then_inc(chain, 1)
                v.tensor_tensor(row_f[:, :], row_f[:, :], jump[:, 1, :], ALU.add).then_inc(chain, 1)
                dve.wait_ge(chain, b * 4 + n1)
            link.n = n1 + 4 * (NT - 1)
            link(v.tensor_scalar(jump[:, 0, :], row_f[:, :], float(N_EDGES - GRP), None, ALU.min))
            link(v.tensor_tensor(t.group_skip[:, :], row_f[:, :], jump[:, 0, :], ALU.subtract))
            link(v.tensor_copy(t.group_row[:, :], jump[:, 0, :]))
            link(v.tensor_copy(t.group_bucket_i[:, :], t.group_bucket[:, :]))
            link(v.tensor_scalar(t.bucket_node[:, :], t.group_bucket[:, :], float(P), None, ALU.mult))


def edge_sort(nc, t, src, attr, in_order):
    with ExitStack() as ctx:
        sb = lambda n, s, d: ctx.enter_context(nc.sbuf_tensor(n, s, d))
        sem = lambda n: ctx.enter_context(nc.semaphore(n))
        src_i = sb("src_i", [P, EC], I32)
        hot = sb("hot_rank", [P, EC], FP32)
        rank = sb("rank", [P, EC], FP32)
        pos = sb("pos", [P, EC], FP32)
        pos_i = sb("pos_i", [P, EC], I32)
        zeros = sb("zeros", [P, EC], FP32)
        attrs = sb("attrs", [P, 2, SLOT, R], FP32)
        slot_src = sb("slot_src", [P, 2, SLOT], I32)
        slot_dst = sb("slot_dst", [P, 2, SLOT], I32)
        slot_pos = sb("slot_pos", [P, 2, SLOT], I32)
        ids_in, chain, filled, passed = (sem("s_" + n) for n in ("ids_in", "chain", "filled", "passed"))
        attr_in = [sem("attr_in0"), sem("attr_in1")]
        scattered = [sem("scattered0"), sem("scattered1")]
        attr_v = attr.rearrange("(p c s) r -> p c s r", p=P, s=SLOT)
        SENT = 3 * 16 * SLOT
        HALVES = (NCH - 1) // 2
        block = ctx.enter_context(nc.Block())

        @block.sync
        def _(sp):
            def load(c, q, turn):
                if turn is not None:
                    sp.wait_ge(scattered[q], turn * SENT)
                sp.dma_start(attrs[:, q, :, :], attr_v[:, c, :, :]).then_inc(attr_in[q], 16)

            with sp.If(sp.value_load(t.unsorted[0:1, 0:1], min_val=0, max_val=N_EDGES) > 0):
                sp.dma_start(src_i[:, :], src.rearrange("(p c) -> p c", p=P)).then_inc(ids_in, 16)
                load(0, 0, None)
                load(1, 1, None)
                with sp.Fori(1, HALVES) as k:
                    load(2 * k, 0, k)
                    load(2 * k + 1, 1, k)
                load(NCH - 1, 0, HALVES)

        @block.gpsimd
        def _(pool):
            pool.memset(t.gate_cell[:, :], 0.0).then_inc(passed, 1)

            def scatter(q, turn):
                pool.wait_ge(filled, 2 * turn + q + 1)
                pool.wait_ge(passed, 2 * turn + q + 1)
                pool.tensor_tensor(t.gate_cell[:, 1:2], t.gate_cell[:, 0:1], t.gate_cell[:, 0:1], ALU.add).then_inc(passed, 1)
                for s in range(SLOT):
                    at = slot_pos[:, q, s:s + 1].bitcast(U32)
                    for to, what in zip(in_order, (slot_src[:, q, s:s + 1], slot_dst[:, q, s:s + 1], attrs[:, q, s, :])):
                        to = to if len(to.shape) == 2 else to.rearrange("(n o) -> n o", o=1)
                        pool.indirect_dma_start(out=to, out_offset=bass.IndirectOffsetOnAxis(ap=at, axis=0),
                                                in_=what, in_offset=None).then_inc(scattered[q], 16)

            with pool.If(pool.value_load(t.unsorted[0:1, 0:1], min_val=0, max_val=N_EDGES) > 0):
                with pool.Fori(0, HALVES) as k:
                    scatter(0, k)
                    scatter(1, k)
                scatter(0, HALVES)
                pool.wait_ge(scattered[0], (HALVES + 1) * SENT)
                pool.wait_ge(scattered[1], HALVES * SENT)

        @block.vector
        def _(dve):
            v = nc.vector

            def fill(c, q, turn, landed):
                dve.wait_ge(attr_in[q], landed)
                if turn is not None:
                    dve.wait_ge(scattered[q], turn * SENT)
                v.tensor_copy(slot_src[:, q, :], src_i[:, bass.ds(c * SLOT, SLOT)]).then_inc(chain, 1)
                v.tensor_copy(slot_dst[:, q, :], t.dst_i[:, bass.ds(c * SLOT, SLOT)]).then_inc(chain, 1)
                v.tensor_copy(slot_pos[:, q, :], pos_i[:, bass.ds(c * SLOT, SLOT)]).then_inc(filled, 1)

            with dve.If(dve.value_load(t.unsorted[0:1, 0:1], min_val=0, max_val=N_EDGES) > 0):
                link = Link(dve, chain)
                link(v.memset(zeros[:, :], 0.0))
                link(v.memset(pos[:, :], -1.0))
                n2 = link.n
                with dve.Fori(0, NT) as b:
                    v.tensor_scalar(hot[:, :], t.bucket[:, :], t.cols[0:P, bass.ds(b, 1)], None, ALU.is_equal).then_inc(chain, 1)
                    dve.wait_ge(chain, b * 4 + (n2 + 1))
                    v.tensor_tensor_scan(rank[:, :], hot[:, :], zeros[:, :], t.base[:, bass.ds(b, 1)], ALU.add, ALU.add).then_inc(chain, 1)
                    dve.wait_ge(chain, b * 4 + (n2 + 2))
                    v.tensor_tensor(hot[:, :], hot[:, :], rank[:, :], ALU.mult).then_inc(chain, 1)
                    dve.wait_ge(chain, b * 4 + (n2 + 3))
                    v.tensor_tensor(pos[:, :], pos[:, :], hot[:, :], ALU.add).then_inc(chain, 1)
                    dve.wait_ge(chain, b * 4 + (n2 + 4))
                link.n = n2 + 4 * NT
                link(v.tensor_copy(pos_i[:, :], pos[:, :]))
                dve.wait_ge(ids_in, 16)
                fill(0, 0, None, 16)
                fill(1, 1, None, 16)
                with dve.Fori(1, HALVES) as k:
                    fill(2 * k, 0, k, 16 * k + 16)
                    fill(2 * k + 1, 1, k, 16 * k + 16)
                fill(NCH - 1, 0, HALVES, 16 * HALVES + 16)
                dve.wait_ge(chain, link.n + 2 * NCH)


class Turn:

    def __init__(self, k, c):
        self.n, self.half, self.slot = 2 * k + c, k + c // 2, c % 2


def need(eng, sem, value):
    if not isinstance(value, int) or value > 0:
        eng.wait_ge(sem, value)


def pipeline(eng, count, depth, step):
    first = 2 * ((depth + 3) // 2)
    pairs = (count - first) // 2

    def peeled(s):
        step(lambda d: Turn(0, s - d) if 0 <= s - d < count else None)

    for s in range(first):
        peeled(s)
    with eng.Fori(0, pairs) as k:
        for c in (first, first + 1):
            step(lambda d: Turn(k, c - d))
    for s in range(first + 2 * pairs, count + depth):
        peeled(s)


def split_row(nc, link, t, parts, row, work):
    v = nc.vector
    hi, rest = work[:, 0, :], work[:, 1, :]
    acc = work[:, 2, :]
    link(v.tensor_copy(parts[:, :], row[:, :]))
    link(v.tensor_copy(hi, parts[:, :]))
    link(v.tensor_scalar(acc, hi, t.ident[0:3, 0:1], None, ALU.mult))
    link(v.tensor_tensor(rest, row[:, :], hi, ALU.subtract))
    link(v.tensor_copy(parts[:, :], rest))
    link(v.tensor_copy(hi, parts[:, :]))
    link(v.scalar_tensor_tensor(out=acc, in0=hi, scalar=t.ident[0:3, 1:2], in1=acc, op0=ALU.mult, op1=ALU.add))
    link(v.tensor_tensor(rest, rest, hi, ALU.subtract))
    link(v.scalar_tensor_tensor(out=acc, in0=rest, scalar=t.ident[0:3, 2:3], in1=acc, op0=ALU.mult, op1=ALU.add))
    link(v.tensor_copy(parts[:, :], acc))


def edge_messages(nc, t, h_dram, src, dst, attr, in_order, W1, b1, W2, b2):
    with ExitStack() as ctx:
        sb = lambda n, s, d: ctx.enter_context(nc.sbuf_tensor(n, s, d))
        pb = lambda n, s: ctx.enter_context(nc.psum_tensor(n, s, FP32))
        sem = lambda n: ctx.enter_context(nc.semaphore(n))
        w1 = sb("w1", [2 * R, D], FP32)
        w2 = sb("w2", [128, 2, D], FP32)
        b1c = sb("b1c", [128, 2], FP32)
        b2r = sb("b2r", [3, D], FP32)
        b2w = sb("b2w", [3, 3, D], FP32)
        b2p = sb("b2p", [3, D], BF16)
        at = sb("attr_tile", [128, 2, NW, R], FP32)
        ids = sb("ids_tile", [128, 2, 2, NW], I32)
        src_i = sb("src_idx", [128, 2, NW], I32)
        place = sb("place", [128, NW], FP32)
        place_i = sb("place_i", [128, NW], I32)
        skip = sb("skip", [128, 2, NW], FP32)
        hg = sb("hg", [128, 2, NW, D], FP32)
        rT = sb("rT", [2 * R, 2, 2 * WIN], FP32)
        sg = sb("sg", [128, 2, 2, 2 * WIN], FP32)
        hid = sb("hid", [128, 2, 2, 2 * WIN], FP32)
        gate = sb("gate", [128, NW, D], FP32)
        msg = sb("msg", [128, NW, D], FP32)
        hot = sb("hot_dst", [128, NW, P], FP32)
        psT = pb("psT", [128, 512])
        psH = pb("psH", [128, 2, 2, 2 * WIN])
        psG = pb("psG", [128, NW, D])
        psA = pb("psA", [128, 512])
        names = ["w_in", "b_split", "chain", "turned", "copied", "up_done", "sig_ready", "hid_ready", "gate_done",
                 "gate_ready", "msg_ready", "ids_ready", "hot_ready", "sum_done", "sum_added", "passed"]
        (w_in, b_split, chain, turned, copied, up_done, sig_ready, hid_ready, gate_done,
         gate_ready, msg_ready, ids_ready, hot_ready, sum_done, sum_added, passed) = (sem("m_" + n) for n in names)
        rec_in = [sem("rec_in0"), sem("rec_in1")]
        ids_chain, place_made = sem("ids_chain"), sem("place_made")
        hg_in = [sem("hg_in0"), sem("hg_in1")]
        DEPTH = 3
        block = ctx.enter_context(nc.Block())

        @block.sync
        def _(sp):
            sp.dma_start(w1[0:R, :], W1).then_inc(w_in, 16)
            sp.dma_start(w1[R:2 * R, :], W1).then_inc(w_in, 16)
            sp.dma_start(w2[:, :, :], W2.rearrange("(m p) n -> p m n", p=128)).then_inc(w_in, 16)
            sp.dma_start(b1c[:, :], b1.rearrange("(m p) -> p m", p=128), allow_slow_non_contiguous=True).then_inc(w_in, 16)
            for r in range(3):
                sp.dma_start(b2r[r:r + 1, :], b2.rearrange("(o n) -> o n", o=1)).then_inc(w_in, 16)

            def loads(src, dst, attr):
                def step(back):
                    g = back(0)
                    if g is None:
                        return
                    need(sp, turned, g.n - 1)
                    need(sp, ids_ready, g.n - 1)
                    row = sp.value_load(t.group_row[0:1, bass.ds(g.n, 1)], min_val=0, max_val=N_EDGES - GRP)
                    rows = bass.ds(row, GRP)
                    done = rec_in[g.slot]
                    sp.dma_start(ids[:, g.slot, 0, :], src[rows].rearrange("(p j) -> p j", j=NW)).then_inc(done, 16)
                    sp.dma_start(ids[:, g.slot, 1, :], dst[rows].rearrange("(p j) -> p j", j=NW)).then_inc(done, 16)
                    sp.dma_start(at[:, g.slot, :, :], attr[rows, :].rearrange("(p j) c -> p j c", j=NW)).then_inc(done, 16)

                pipeline(sp, NG, DEPTH, step)

            with sp.If(sp.value_load(t.unsorted[0:1, 0:1], min_val=0, max_val=N_EDGES) > 0):
                loads(*in_order)
            with sp.Else():
                loads(src, dst, attr)

        @block.gpsimd
        def _(pool):
            pool.iota(place_i[:, :], pattern=[[1, NW]], base=0, channel_multiplier=NW).then_inc(place_made, 1)
            pool.memset(t.gate_cell[:, :], 0.0).then_inc(passed, 1)

            def step(back):
                g = back(0)
                if g is None:
                    return
                need(pool, msg_ready, g.n - 1)
                pool.wait_ge(ids_ready, g.n + 1)
                pool.wait_ge(passed, g.n + 1)
                pool.tensor_tensor(t.gate_cell[:, 1:2], t.gate_cell[:, 0:1], t.gate_cell[:, 0:1], ALU.add).then_inc(passed, 1)
                for j in range(NW):
                    pool.indirect_dma_start(
                        out=hg[:, g.slot, j, :], out_offset=None, in_=h_dram[:, :],
                        in_offset=bass.IndirectOffsetOnAxis(ap=src_i[:, g.slot, j:j + 1].bitcast(U32), axis=0)
                    ).then_inc(hg_in[g.slot], 16)

            pipeline(pool, NG, DEPTH, step)

        @block.tensor
        def _(pe):
            pe.wait_ge(w_in, 7 * 16)
            pe.wait_ge(b_split, 1)

            def step(back):
                g = back(0)
                if g is not None:
                    pe.wait_ge(rec_in[g.slot], g.half * 48 + 48)
                    need(pe, copied, g.n)
                    for pair in range(2):
                        last = nc.tensor.transpose(psT[:, pair * WIN:(pair + 1) * WIN],
                                                   at[:, g.slot, 2 * pair:2 * pair + 2, :].rearrange("p j r -> p (j r)"), t.ident[:, :])
                    last.then_inc(turned, 1)
                g = back(1)
                if g is not None:
                    pe.wait_ge(copied, g.n + 1)
                    need(pe, hid_ready, g.n)
                    for m in range(2):
                        for odd in range(2):
                            last = nc.tensor.matmul(psH[:, odd, m, :], w1[odd * R:(odd + 1) * R, m * 128:(m + 1) * 128],
                                                    rT[odd * R:(odd + 1) * R, g.slot, :], start=True, stop=True)
                    last.then_inc(up_done, 1)
                g = back(2)
                if g is not None:
                    pe.wait_ge(hid_ready, g.n + 1)
                    need(pe, gate_ready, g.n)
                    for j in range(NW):
                        for m in range(2):
                            nc.tensor.matmul(psG[:, j, :], hid[:, j % 2, m, j // 2 * WIN:(j // 2 + 1) * WIN], w2[:, m, :],
                                             start=(m == 0), stop=False)
                        last = nc.tensor.matmul(psG[:, j, :], t.ones_h[0:3, :], b2p[:, :], start=False, stop=True)
                    last.then_inc(gate_done, 1)
                g = back(3)
                if g is not None:
                    pe.wait_ge(msg_ready, g.n + 1)
                    pe.wait_ge(hot_ready, g.n + 1)
                    need(pe, sum_added, g.n)
                    for j in range(NW):
                        last = nc.tensor.matmul(psA[0:P, 0:D], hot[:, j, :], msg[:, j, :], start=(j == 0), stop=(j == NW - 1))
                    last.then_inc(sum_done, 1)

            pipeline(pe, NG, DEPTH, step)

        @block.scalar
        def _(act):
            act.wait_ge(w_in, 7 * 16)

            def step(back):
                g = back(0)
                if g is not None:
                    act.wait_ge(turned, g.n + 1)
                    need(act, up_done, g.n - 1)
                    nc.scalar.copy(rT[:, g.slot, :], psT[:, 0:2 * WIN]).then_inc(copied, 1)
                g = back(1)
                if g is not None:
                    act.wait_ge(up_done, g.n + 1)
                    need(act, hid_ready, g.n)
                    for m in range(2):
                        last = nc.scalar.activation(sg[:, :, m, :], psH[:, :, m, :], ACT.Sigmoid, bias=b1c[:, m:m + 1])
                    last.then_inc(sig_ready, 1)
                g = back(2)
                if g is not None:
                    act.wait_ge(gate_done, g.n + 1)
                    need(act, msg_ready, g.n)
                    nc.scalar.activation(gate[:, :, :], psG[:, :, :], ACT.Sigmoid).then_inc(gate_ready, 1)

            pipeline(act, NG, DEPTH, step)

        @block.vector
        def _(dve):
            link = Link(dve, chain)
            v = nc.vector
            link(v.memset(t.sums[:, :, :], 0.0))
            dve.wait_ge(w_in, 7 * 16)
            split_row(nc, link, t, b2p, b2r, b2w)
            dve.wait_ge(place_made, 1)
            link(v.tensor_copy(place[:, :], place_i[:, :]))
            dve.sem_inc(b_split, 1)

            def step(back):
                g = back(0)
                if g is not None:
                    dve.wait_ge(rec_in[g.slot], g.half * 48 + 48)
                    need(dve, hg_in[g.slot], g.half * (16 * NW))
                    local = t.local_of[:, bass.ds(g.n * NW, NW)]
                    v.tensor_scalar(skip[:, g.slot, :], place[:, :], t.group_skip[:, bass.ds(g.n, 1)], -float(4 * N_NODES),
                                    ALU.is_lt, ALU.mult).then_inc(ids_chain, 1)
                    v.tensor_scalar(local, ids[:, g.slot, 1, :], t.bucket_node[:, bass.ds(g.n, 1)], None,
                                    ALU.subtract).then_inc(ids_chain, 1)
                    v.tensor_copy(t.src_of[:, bass.ds(g.n * NW, NW)], ids[:, g.slot, 0, :])
                    v.tensor_copy(src_i[:, g.slot, :], ids[:, g.slot, 0, :])
                    dve.wait_ge(ids_chain, g.n * 2 + 2)
                    v.tensor_tensor(local, local, skip[:, g.slot, :], ALU.add).then_inc(ids_ready, 1)
                g = back(1)
                if g is not None:
                    dve.wait_ge(sig_ready, g.n + 1)
                    need(dve, gate_done, g.n)
                    for m in range(2):
                        last = v.scalar_tensor_tensor(out=hid[:, :, m, :], in0=psH[:, :, m, :], scalar=b1c[:, m:m + 1],
                                                      in1=sg[:, :, m, :], op0=ALU.add, op1=ALU.mult)
                    last.then_inc(hid_ready, 1)
                g = back(2)
                if g is not None:
                    dve.wait_ge(gate_ready, g.n + 1)
                    dve.wait_ge(hg_in[g.slot], (g.half + 1) * (16 * NW))
                    need(dve, sum_done, g.n)
                    v.tensor_tensor(msg[:, :, :], gate[:, :, :], hg[:, g.slot, :, :], ALU.mult).then_inc(msg_ready, 1)
                    dve.wait_ge(ids_ready, g.n + 1)
                    for j in range(NW):
                        last = v.tensor_scalar(hot[:, j, :], t.cols[:, 0:P], t.local_of[:, bass.ds(g.n * NW + j, 1)],
                                               None, ALU.is_equal)
                    last.then_inc(hot_ready, 1)
                g = back(3)
                if g is not None:
                    b = dve.value_load(t.group_bucket_i[0:1, bass.ds(g.n, 1)], min_val=0, max_val=NT - 1)
                    dve.wait_ge(sum_done, g.n + 1)
                    need(dve, sum_added, g.n)
                    v.tensor_tensor(t.sums[:, bass.ds(b, 1), :], t.sums[:, bass.ds(b, 1), :],
                                    psA[0:P, 0:D].rearrange("p (o d) -> p o d", o=1), ALU.add).then_inc(sum_added, 1)

            pipeline(dve, NG, DEPTH, step)
            dve.wait_ge(sum_added, NG)


def node_update(nc, t, x, h_dram, x1_dram, U1, c1, U2, c2):
    with ExitStack() as ctx:
        sb = lambda n, s, d: ctx.enter_context(nc.sbuf_tensor(n, s, d))
        pb = lambda n, s: ctx.enter_context(nc.psum_tensor(n, s, FP32))
        sem = lambda n: ctx.enter_context(nc.semaphore(n))
        u1 = sb("u1", [128, 4, D], FP32)
        u2 = sb("u2", [128, 2, D], FP32)
        c1c = sb("c1c", [128, 2], FP32)
        c2r = sb("c2r", [3, D], FP32)
        c2w = sb("c2w", [3, 3, D], FP32)
        c2p = sb("c2p", [3, D], BF16)
        cat = sb("cat", [P, 2, 2, D], FP32)
        h = sb("h_all", [P, NT, D], FP32)
        catT = sb("catT", [128, 2, 4, P], FP32)
        sg = sb("sgu", [128, 2, P], FP32)
        hid = sb("hidu", [128, 2, P], FP32)
        psT = pb("psT1", [128, 4, P])
        psU = pb("psU", [128, 2, P])
        psV = pb("psV", [128, 512])
        names = ["w_in", "b_split", "chain", "sums_set", "turned", "copied", "up_done", "sig_ready", "hid_ready",
                 "down_done", "base_ready", "x1_ready"]
        (w_in, b_split, chain, sums_set, turned, copied, up_done, sig_ready, hid_ready,
         down_done, base_ready, x1_ready) = (sem("u_" + n) for n in names)
        xh_in = sem("xh_in")
        stored = sem("x1_stored")
        DEPTH = 2
        block = ctx.enter_context(nc.Block())

        @block.sync
        def _(sp):
            sp.dma_start(u1[:, :, :], U1.rearrange("(m p) n -> p m n", p=128)).then_inc(w_in, 16)
            sp.dma_start(u2[:, :, :], U2.rearrange("(m p) n -> p m n", p=128)).then_inc(w_in, 16)
            sp.dma_start(c1c[:, :], c1.rearrange("(m p) -> p m", p=128), allow_slow_non_contiguous=True).then_inc(w_in, 16)
            for r in range(3):
                sp.dma_start(c2r[r:r + 1, :], c2.rearrange("(o n) -> o n", o=1)).then_inc(w_in, 16)

            sp.dma_start(h[:, :, :], h_dram.rearrange("(n p) d -> p n d", p=P)).then_inc(xh_in, 16)
            sp.dma_start(t.x1[:, :, :], x.rearrange("(n p) d -> p n d", p=P)).then_inc(xh_in, 16)
            sp.wait_ge(x1_ready, NT)
            sp.dma_start(x1_dram.rearrange("(n p) d -> p n d", p=P), t.x1[:, :, :]).then_inc(stored, 16)
            sp.wait_ge(stored, 16)

        @block.gpsimd
        def _(pool):
            pool.wait_ge(xh_in, 32)

            def step(back):
                g = back(0)
                if g is not None:
                    need(pool, turned, g.n - 1)
                    pool.tensor_copy(cat[:, g.slot, 0, :], h[:, bass.ds(g.n, 1), :].rearrange("p o d -> p (o d)")).then_inc(sums_set, 1)
                    pool.tensor_copy(cat[:, g.slot, 1, :], t.sums[:, bass.ds(g.n, 1), :].rearrange("p o d -> p (o d)")).then_inc(sums_set, 1)

            pipeline(pool, NT, DEPTH, step)

        @block.tensor
        def _(pe):
            pe.wait_ge(w_in, 6 * 16)
            pe.wait_ge(b_split, 1)

            def step(back):
                g = back(0)
                if g is not None:
                    pe.wait_ge(sums_set, g.n * 2 + 2)
                    need(pe, copied, g.n)
                    for m in range(4):
                        last = nc.tensor.transpose(psT[:, m, :], cat[:, g.slot, m // 2, (m % 2) * 128:(m % 2 + 1) * 128],
                                                   t.ident[0:P, 0:P])
                    last.then_inc(turned, 1)
                g = back(1)
                if g is not None:
                    pe.wait_ge(copied, g.n + 1)
                    need(pe, hid_ready, g.n)
                    for o in range(2):
                        for m in range(4):
                            last = nc.tensor.matmul(psU[:, o, :], u1[:, m, o * 128:(o + 1) * 128], catT[:, g.slot, m, :],
                                                    start=(m == 0), stop=(m == 3))
                    last.then_inc(up_done, 1)
                g = back(2)
                if g is not None:
                    pe.wait_ge(hid_ready, g.n + 1)
                    need(pe, x1_ready, g.n)
                    for m in range(2):
                        nc.tensor.matmul(psV[0:P, 0:D], hid[:, m, :], u2[:, m, :], start=(m == 0), stop=False)
                    nc.tensor.matmul(psV[0:P, 0:D], t.ones_h[0:3, 0:P], c2p[:, :], start=False, stop=True).then_inc(down_done, 1)

            pipeline(pe, NT, DEPTH, step)

        @block.scalar
        def _(act):
            act.wait_ge(w_in, 6 * 16)

            def step(back):
                g = back(0)
                if g is not None:
                    act.wait_ge(turned, g.n + 1)
                    need(act, up_done, g.n - 1)
                    nc.scalar.copy(catT[:, g.slot, :, :], psT[:, :, :]).then_inc(copied, 1)
                g = back(1)
                if g is not None:
                    act.wait_ge(up_done, g.n + 1)
                    need(act, hid_ready, g.n)
                    for m in range(2):
                        last = nc.scalar.activation(sg[:, m, :], psU[:, m, :], ACT.Sigmoid, bias=c1c[:, m:m + 1])
                    last.then_inc(sig_ready, 1)

            pipeline(act, NT, DEPTH, step)

        @block.vector
        def _(dve):
            link = Link(dve, chain)
            v = nc.vector
            dve.wait_ge(w_in, 6 * 16)
            split_row(nc, link, t, c2p, c2r, c2w)
            dve.sem_inc(b_split, 1)
            dve.wait_ge(xh_in, 32)
            v.tensor_tensor(t.x1[:, :, :], t.x1[:, :, :], h[:, :, :], ALU.add).then_inc(base_ready, 1)
            dve.wait_ge(base_ready, 1)

            def step(back):
                g = back(1)
                if g is not None:
                    dve.wait_ge(sig_ready, g.n + 1)
                    need(dve, down_done, g.n)
                    for m in range(2):
                        last = v.scalar_tensor_tensor(out=hid[:, m, :], in0=psU[:, m, :], scalar=c1c[:, m:m + 1],
                                                      in1=sg[:, m, :], op0=ALU.add, op1=ALU.mult)
                    last.then_inc(hid_ready, 1)
                g = back(2)
                if g is not None:
                    one = lambda a: a.rearrange("p (o d) -> p o d", o=1)
                    x1 = t.x1[:, bass.ds(g.n, 1), :]
                    dve.wait_ge(down_done, g.n + 1)
                    v.tensor_tensor(x1, x1, one(psV[0:P, 0:D]), ALU.add).then_inc(x1_ready, 1)

            pipeline(dve, NT, DEPTH, step)
            dve.wait_ge(x1_ready, NT)


def node_input(nc, t, y_dram, Win, bin_):
    with ExitStack() as ctx:
        sb = lambda n, s, d: ctx.enter_context(nc.sbuf_tensor(n, s, d))
        pb = lambda n, s: ctx.enter_context(nc.psum_tensor(n, s, FP32))
        sem = lambda n: ctx.enter_context(nc.semaphore(n))
        wi = sb("wi", [128, 2, D], FP32)
        bir = sb("bir", [3, D], FP32)
        biw = sb("biw", [3, 3, D], FP32)
        bip = sb("bip", [3, D], BF16)
        stats = sb("stats2", [P, NT, 6], FP32)
        mv = sb("mv2", [P, NT, 2], FP32)
        rstd = sb("rstd2", [P, NT], FP32)
        nmr = sb("nmr2", [P, NT], FP32)
        h2 = sb("h2", [P, 2, D], FP32)
        hT = sb("hT", [128, 2, 2, P], FP32)
        sg = sb("sgi", [P, D], FP32)
        y = sb("y", [P, NT, D], FP32)
        big = sb("big", [128, 4], FP32)
        psT = pb("psT2", [128, 4, P])
        psY = pb("psY", [128, 512])
        names = ["w_in", "b_split", "chain", "var_ready", "std_ready", "norm_ready", "h_ready", "turned", "copied", "in_done",
                 "sig_ready", "y_ready", "max_ready", "max_all", "scaled", "stored"]
        (w_in, b_split, chain, var_ready, std_ready, norm_ready, h_ready, turned, copied, in_done,
         sig_ready, y_ready, max_ready, max_all, scaled, stored) = (sem("i_" + n) for n in names)
        DEPTH = 1
        block = ctx.enter_context(nc.Block())

        @block.sync
        def _(sp):
            sp.dma_start(wi[:, :, :], Win.rearrange("(m p) n -> p m n", p=128)).then_inc(w_in, 16)
            for r in range(3):
                sp.dma_start(bir[r:r + 1, :], bin_.rearrange("(o n) -> o n", o=1)).then_inc(w_in, 16)
            sp.wait_ge(scaled, 1)
            sp.dma_start(y_dram.rearrange("(n p) d -> p n d", p=P), y[:, :, :]).then_inc(stored, 16)
            sp.wait_ge(stored, 16)

        @block.gpsimd
        def _(pool):
            pool.memset(big[:, :], 0.0).then_inc(max_all, 1)
            pool.wait_ge(max_ready, 1)
            pool.partition_all_reduce(big[:, 1:2], big[:, 0:1], 128, bass.bass_isa.ReduceOp.max).then_inc(max_all, 1)
            pool.wait_ge(max_all, 2)

        @block.tensor
        def _(pe):
            pe.wait_ge(w_in, 4 * 16)
            pe.wait_ge(b_split, 1)

            def step(back):
                g = back(0)
                if g is not None:
                    pe.wait_ge(h_ready, g.n + 1)
                    need(pe, copied, g.n)
                    for m in range(2):
                        last = nc.tensor.transpose(psT[:, m, :], h2[:, g.slot, m * 128:(m + 1) * 128], t.ident[0:P, 0:P])
                    last.then_inc(turned, 1)
                g = back(1)
                if g is not None:
                    pe.wait_ge(copied, g.n + 1)
                    need(pe, y_ready, g.n)
                    for m in range(2):
                        nc.tensor.matmul(psY[0:P, 0:D], hT[:, g.slot, m, :], wi[:, m, :], start=(m == 0), stop=False)
                    nc.tensor.matmul(psY[0:P, 0:D], t.ones_h[0:3, 0:P], bip[:, :], start=False, stop=True).then_inc(in_done, 1)

            pipeline(pe, NT, DEPTH, step)

        @block.scalar
        def _(act):
            act.wait_ge(var_ready, 1)
            nc.scalar.activation(rstd[:, :], nmr[:, :], ACT.Sqrt).then_inc(std_ready, 1)
            act.wait_ge(norm_ready, 1)

            def step(back):
                g = back(0)
                if g is not None:
                    need(act, turned, g.n - 1)
                    nc.scalar.activation(h2[:, g.slot, :], t.x1[:, bass.ds(g.n, 1), :].rearrange("p o d -> p (o d)"), ACT.Relu,
                                         bias=nmr[:, bass.ds(g.n, 1)], scale=rstd[:, bass.ds(g.n, 1)]).then_inc(h_ready, 1)
                g = back(1)
                if g is not None:
                    act.wait_ge(in_done, g.n + 1)
                    need(act, y_ready, g.n)
                    nc.scalar.activation(sg[:, :], psY[0:P, 0:D], ACT.Sigmoid).then_inc(sig_ready, 1)

            pipeline(act, NT, DEPTH, step)

        @block.vector
        def _(dve):
            link = Link(dve, chain)
            v = nc.vector
            for n in range(NT):
                last = v.bn_stats(stats[:, n, :], t.x1[:, n, :])
            link(last)
            for n in range(NT):
                last = v.bn_aggr(mv[:, n, :], stats[:, n, :])
            link(last)
            link(v.tensor_scalar(rstd[:, :], mv[:, :, 1], EPS, None, ALU.add))
            v.reciprocal(nmr[:, :], rstd[:, :]).then_inc(var_ready, 1)
            dve.wait_ge(std_ready, 1)
            v.scalar_tensor_tensor(out=nmr[:, :], in0=mv[:, :, 0], scalar=-1.0, in1=rstd[:, :],
                                   op0=ALU.mult, op1=ALU.mult).then_inc(norm_ready, 1)
            dve.wait_ge(w_in, 4 * 16)
            split_row(nc, link, t, bip, bir, biw)
            dve.sem_inc(b_split, 1)

            def step(back):
                g = back(0)
                if g is not None:
                    dve.wait_ge(turned, g.n + 1)
                    need(dve, in_done, g.n - 1)
                    v.tensor_copy(hT[:, g.slot, :, :], psT[:, 0:2, :]).then_inc(copied, 1)
                g = back(1)
                if g is not None:
                    dve.wait_ge(sig_ready, g.n + 1)
                    one = lambda a: a.rearrange("p (o d) -> p o d", o=1)
                    v.tensor_tensor(y[:, bass.ds(g.n, 1), :], one(psY[0:P, 0:D]), one(sg[:, :]), ALU.mult).then_inc(y_ready, 1)

            pipeline(dve, NT, DEPTH, step)
            dve.wait_ge(y_ready, NT)
            dve.wait_ge(max_all, 1)
            link(v.tensor_reduce(big[0:P, 0:1], y[:, :, :], AX.XY, ALU.max, apply_absolute_value=True))
            v.tensor_scalar(big[0:P, 0:1], big[0:P, 0:1], 2.0 ** -100, 2.0 ** 100, ALU.max, ALU.min).then_inc(max_ready, 1)
            dve.wait_ge(max_all, 2)
            bits = lambda c: big[:, c:c + 1].bitcast(I32)
            link(v.tensor_scalar(bits(2), bits(1), 0x7F800000, None, ALU.bitwise_and))
            link(v.tensor_scalar(t.scale[:, 0:1].bitcast(I32), bits(2), -1.0, float((254 + 13) << 23), ALU.mult, ALU.add))
            link(v.tensor_scalar(t.scale[:, 1:2].bitcast(I32), bits(2), float(13 << 23), None, ALU.subtract))
            v.tensor_scalar(y[:, :, :], y[:, :, :], t.scale[0:P, 0:1], None, ALU.mult).then_inc(scaled, 1)


PIECE = 500
NPIECE = -(-N_NODES // PIECE)


def count_edges(nc, t):
    with ExitStack() as ctx:
        sb = lambda n, s, d: ctx.enter_context(nc.sbuf_tensor(n, s, d))
        sem = lambda n: ctx.enter_context(nc.semaphore(n))
        NE = NG * NW
        key = sb("key", [128, NE], FP32)
        part = sb("part", [128, NE], FP32)
        ok = sb("ok", [128, NE], FP32)
        cols_h = sb("cols_h", [128, PIECE], FP16)
        hot_part = sb("hot_part", [128, 2, NW, 128], FP16)
        hot_key = sb("hot_key", [128, 2, NW, PIECE], FP16)
        ps = [ctx.enter_context(nc.psum_tensor(f"ps_count{i}", [128, 512], FP32)) for i in range(2)]
        chain, cleared, part_ready, key_ready, block_done, block_added = (
            sem("c_" + n) for n in ("chain", "cleared", "part_ready", "key_ready", "block_done", "block_added"))
        block = ctx.enter_context(nc.Block())

        @block.gpsimd
        def _(pool):
            cut = 16 * N_NODES
            pool.memset(t.counts[:, 0:cut], 0.0).then_inc(cleared, 1)
            pool.memset(t.counts[:, cut:NT * N_NODES + 8], 0.0).then_inc(cleared, 1)

        @block.tensor
        def _(pe):
            def step(back):
                g = back(0)
                if g is None:
                    return
                pe.wait_ge(part_ready, g.n + 1)
                for i in range(NPIECE):
                    w = min(PIECE, N_NODES - i * PIECE)
                    n = g.n * NPIECE + i
                    pe.wait_ge(key_ready, n + 1)
                    q = (g.slot * NPIECE + i) % 2
                    need(pe, block_added, n - 1)
                    for j in range(NW):
                        last = nc.tensor.matmul(ps[q][:, 0:w], hot_part[:, g.slot, j, :], hot_key[:, q, j, 0:w],
                                                start=(j == 0), stop=(j == NW - 1))
                    last.then_inc(block_done, 1)

            pipeline(pe, NG, 0, step)

        @block.vector
        def _(dve):
            link = Link(dve, chain)
            v = nc.vector
            link(v.tensor_copy(cols_h[:, :], t.cols[:, 0:PIECE]))
            link(v.tensor_scalar(key[:, :], t.src_of[:, :], -float(P // 2), 1.0 / P, ALU.add, ALU.mult))
            link(v.tensor_scalar(key[:, :], key[:, :], MAGIC, None, ALU.add))
            link(v.tensor_scalar(key[:, :], key[:, :], MAGIC, None, ALU.subtract))
            link(v.tensor_scalar(key[:, :], key[:, :], float(P), None, ALU.mult))
            link(v.tensor_tensor(part[:, :], t.src_of[:, :], key[:, :], ALU.subtract))
            link(v.tensor_scalar(ok[:, :], t.local_of[:, :], 0.0, None, ALU.is_ge))
            link(v.scalar_tensor_tensor(out=ok[:, :], in0=t.local_of[:, :], scalar=float(P), in1=ok[:, :],
                                        op0=ALU.is_lt, op1=ALU.mult))
            link(v.scalar_tensor_tensor(out=key[:, :], in0=key[:, :], scalar=1.0, in1=t.local_of[:, :],
                                        op0=ALU.add, op1=ALU.add))
            link(v.tensor_tensor(key[:, :], key[:, :], ok[:, :], ALU.mult))
            link(v.tensor_scalar(key[:, :], key[:, :], 1.0, None, ALU.subtract))
            dve.wait_ge(cleared, 2)

            def hots(g):
                need(dve, block_done, (g.n - 1) * NPIECE)
                for j in range(NW):
                    last = v.tensor_scalar(hot_part[:, g.slot, j, :], cols_h[:, 0:128], part[:, bass.ds(g.n * NW + j, 1)],
                                           None, ALU.is_equal)
                last.then_inc(part_ready, 1)

            def piece(g, i):
                n = g.n * NPIECE + i
                q = (g.slot * NPIECE + i) % 2
                w = min(PIECE, N_NODES - i * PIECE)
                need(dve, block_done, n - 1)
                for j in range(NW):
                    last = v.tensor_scalar(hot_key[:, q, j, 0:w], cols_h[:, 0:w], float(i * PIECE),
                                           key[:, bass.ds(g.n * NW + j, 1)], ALU.add, ALU.is_equal)
                last.then_inc(key_ready, 1)

            def add(g, i, b):
                n = g.n * NPIECE + i
                q = (g.slot * NPIECE + i) % 2
                w = min(PIECE, N_NODES - i * PIECE)
                at = t.counts[0:P, bass.ds(b * N_NODES + i * PIECE, w)]
                dve.wait_ge(block_done, n + 1)
                need(dve, block_added, n)
                v.tensor_tensor(at, at, ps[q][0:P, 0:w], ALU.add).then_inc(block_added, 1)

            def step(back):
                g, before = back(0), back(1)
                if g is not None:
                    hots(g)
                    piece(g, 0)
                if before is not None:
                    b = dve.value_load(t.group_bucket_i[0:1, bass.ds(before.n, 1)], min_val=0, max_val=NT - 1)
                    add(before, NPIECE - 1, b)
                if g is not None:
                    b = dve.value_load(t.group_bucket_i[0:1, bass.ds(g.n, 1)], min_val=0, max_val=NT - 1)
                    for i in range(1, NPIECE):
                        piece(g, i)
                        add(g, i - 1, b)

            pipeline(dve, NG, 1, step)
            dve.wait_ge(block_added, NG * NPIECE)


def degrees(nc, t):
    with ExitStack() as ctx:
        sb = lambda n, s, d: ctx.enter_context(nc.sbuf_tensor(n, s, d))
        sem = lambda n: ctx.enter_context(nc.semaphore(n))
        ones16 = sb("ones16", [128, 2], FP16)
        inv = sb("inv", [P, NT], FP32)
        psd = ctx.enter_context(nc.psum_tensor("ps_deg", [128, 512], FP32))
        chain, made, deg_done = (sem("d_" + n) for n in ("chain", "made", "deg_done"))
        block = ctx.enter_context(nc.Block())

        @block.tensor
        def _(pe):
            pe.wait_ge(made, 1)
            for b in range(NT):
                for k in range(NT):
                    last = nc.tensor.matmul(psd[0:P, b:b + 1], t.counts[0:P, b * N_NODES + k * P:b * N_NODES + (k + 1) * P],
                                            ones16[0:P, 0:1], start=(k == 0), stop=(k == NT - 1))
            last.then_inc(deg_done, 1)

        @block.vector
        def _(dve):
            link = Link(dve, chain)
            v = nc.vector
            v.memset(ones16[:, :], 1.0).then_inc(made, 1)
            dve.wait_ge(deg_done, 1)
            link(v.tensor_scalar(inv[:, :], psd[0:P, 0:NT], 1.0, None, ALU.max))
            for i in range(NSTEPS):
                link(v.tensor_scalar(t.inv_deg[:, 1, i, :], inv[:, :], float(i + 1), None, ALU.mult))
                link(v.reciprocal(t.inv_deg[:, 0, i, :], t.inv_deg[:, 1, i, :]))
                link(v.tensor_scalar(t.inv_deg[:, 1, i, :], t.inv_deg[:, 0, i, :], 1.0 / LOW, None, ALU.mult))


def diffusion(nc, t, y_dram, d_dram):
    with ExitStack() as ctx:
        sb = lambda n, s, d: ctx.enter_context(nc.sbuf_tensor(n, s, d))
        sem = lambda n: ctx.enter_context(nc.semaphore(n))
        term = [sb(f"term{i}", [P, NT, 2 * HALF], FP16) for i in range(2)]
        acc = sb("acc", [P, NT, HALF], FP32)
        low = sb("low_sum", [P, 2, HALF], FP32)
        val = sb("val", [P, 2, HALF], FP32)
        rest = sb("rest", [P, 2, HALF], FP32)
        ps = [ctx.enter_context(nc.psum_tensor(f"ps_term{i}", [128, 512], FP32)) for i in range(2)]
        names = ["chain", "y_in", "product", "low_ready", "val_ready", "high_ready", "rest_ready", "term_ready", "acc_ready", "stored"]
        chain, y_in, product, low_ready, val_ready, high_ready, rest_ready, term_ready, acc_ready, stored = (
            sem("f_" + n) for n in names)
        y_v = y_dram.rearrange("(n p) (c d) -> c p n d", p=P, c=2)
        d_v = d_dram.rearrange("(n p) (c d) -> c p n d", p=P, c=2)
        PER = NT * NSTEPS
        block = ctx.enter_context(nc.Block())

        def steps(eng, do):
            for c in range(2):
                for i in range(NSTEPS):
                    at = (c * NSTEPS + i) * NT
                    for n in range(3):
                        do(c, i, Turn(0, n), at, n == 0)
                    with eng.Fori(0, (NT - 3) // 2) as k:
                        for m in (3, 4):
                            do(c, i, Turn(k, m), at, False)

        @block.sync
        def _(sp):
            for c in range(2):
                if c:
                    sp.wait_ge(stored, 16)
                sp.dma_start(acc[:, :, :], y_v[c]).then_inc(y_in, 16)
                sp.wait_ge(acc_ready, (c + 1) * (PER + 1))
                sp.dma_start(d_v[c], acc[:, :, :]).then_inc(stored, 16)
            sp.wait_ge(stored, 32)

        @block.tensor
        def _(pe):
            def do(c, i, g, at, first):
                if first:
                    if i == 0:
                        pe.wait_ge(acc_ready, c * (PER + 1) + 1)
                    else:
                        pe.wait_ge(term_ready, at)
                n = g.n + at
                q = (g.slot + at) % 2
                need(pe, val_ready, n - 1)
                for k in range(NT):
                    last = nc.tensor.matmul(ps[q][:, 0:2 * HALF], t.counts[0:P, bass.ds(g.n * N_NODES + k * P, 128)],
                                            term[i % 2][:, k, :], start=(k == 0), stop=(k == NT - 1))
                last.then_inc(product, 1)

            steps(pe, do)

        @block.scalar
        def _(act):
            def do(c, i, g, at, first):
                n = g.n + at
                q = (g.slot + at) % 2
                act.wait_ge(product, n + 1)
                need(act, val_ready, n - 1)
                nc.scalar.activation(low[:, q, :], ps[q][0:P, HALF:2 * HALF], ACT.Copy,
                                     scale=t.inv_deg[:, 1, i, bass.ds(g.n, 1)]).then_inc(low_ready, 1)
                act.wait_ge(val_ready, n + 1)
                one = lambda a: a.rearrange("p (o d) -> p o d", o=1)
                nc.scalar.copy(term[(i + 1) % 2][:, bass.ds(g.n, 1), 0:HALF], one(val[:, q, :])).then_inc(high_ready, 1)
                act.wait_ge(rest_ready, n + 1)
                nc.scalar.mul(term[(i + 1) % 2][:, bass.ds(g.n, 1), HALF:2 * HALF], one(rest[:, q, :]), LOW).then_inc(term_ready, 1)

            steps(act, do)

        @block.vector
        def _(dve):
            link = Link(dve, chain)
            v = nc.vector

            def do(c, i, g, at, first):
                if first and i == 0:
                    dve.wait_ge(y_in, 16 * (c + 1))
                    if c:
                        dve.wait_ge(product, at)
                        dve.wait_ge(term_ready, at)
                    link(v.tensor_copy(term[0][:, :, 0:HALF], acc[:, :, :]))
                    link(v.tensor_tensor(term[1][:, :, :].bitcast(FP32), acc[:, :, :], term[0][:, :, 0:HALF], ALU.subtract))
                    v.tensor_scalar(term[0][:, :, HALF:2 * HALF], term[1][:, :, :].bitcast(FP32), LOW, None,
                                    ALU.mult).then_inc(acc_ready, 1)
                    dve.wait_ge(acc_ready, c * (PER + 1) + 1)
                n = g.n + at
                q = (g.slot + at) % 2
                one = lambda a: a.rearrange("p (o d) -> p o d", o=1)
                dve.wait_ge(low_ready, n + 1)
                need(dve, term_ready, n - 1)
                v.scalar_tensor_tensor(out=val[:, q, :], in0=ps[q][0:P, 0:HALF], scalar=t.inv_deg[:, 0, i, bass.ds(g.n, 1)],
                                       in1=low[:, q, :], op0=ALU.mult, op1=ALU.add).then_inc(val_ready, 1)
                dve.wait_ge(high_ready, n + 1)
                v.tensor_tensor(rest[:, q, :], val[:, q, :], term[(i + 1) % 2][:, bass.ds(g.n, 1), 0:HALF].rearrange("p o d -> p (o d)"),
                                ALU.subtract).then_inc(rest_ready, 1)
                if i:
                    dve.wait_ge(acc_ready, n - NT + c + 2)
                a = acc[:, bass.ds(g.n, 1), :]
                v.tensor_tensor(a, a, one(val[:, q, :]), ALU.add).then_inc(acc_ready, 1)

            steps(dve, do)
            dve.wait_ge(acc_ready, 2 * (PER + 1))


def node_output(nc, t, x1_dram, d_dram, Wout, bout, out):
    with ExitStack() as ctx:
        sb = lambda n, s, d: ctx.enter_context(nc.sbuf_tensor(n, s, d))
        pb = lambda n, s: ctx.enter_context(nc.psum_tensor(n, s, FP32))
        sem = lambda n: ctx.enter_context(nc.semaphore(n))
        wo = sb("wo", [128, 2, D], FP32)
        bor = sb("bor", [3, D], FP32)
        bow = sb("bow", [3, 3, D], FP32)
        bop = sb("bop", [3, D], BF16)
        dt_ = sb("d_tile", [P, 2, D], FP32)
        x1 = sb("x1_tile", [P, 2, D], FP32)
        dT = sb("dT", [128, 2, 2, P], FP32)
        res = sb("res", [P, 2, D], FP32)
        psT = pb("psT3", [128, 4, P])
        psO = pb("psO", [128, 512])
        names = ["w_in", "b_split", "chain", "turned", "copied", "out_done", "res_ready", "base_ready"]
        w_in, b_split, chain, turned, copied, out_done, res_ready, base_ready = (sem("o_" + n) for n in names)
        d_in = [sem("d_in0"), sem("d_in1")]
        stored = [sem("out_stored0"), sem("out_stored1")]
        DEPTH = 1
        block = ctx.enter_context(nc.Block())

        @block.sync
        def _(sp):
            sp.dma_start(wo[:, :, :], Wout.rearrange("(m p) n -> p m n", p=128)).then_inc(w_in, 16)
            for r in range(3):
                sp.dma_start(bor[r:r + 1, :], bout.rearrange("(o n) -> o n", o=1)).then_inc(w_in, 16)

            def step(back):
                g = back(0)
                if g is not None:
                    need(sp, res_ready, g.n - 1)
                    need(sp, turned, g.n - 1)
                    sp.dma_start(dt_[:, g.slot, :], d_dram[bass.ds(g.n * P, P), :]).then_inc(d_in[g.slot], 16)
                    sp.dma_start(x1[:, g.slot, :], x1_dram[bass.ds(g.n * P, P), :]).then_inc(d_in[g.slot], 16)
                g = back(1)
                if g is not None:
                    sp.wait_ge(res_ready, g.n + 1)
                    sp.dma_start(out[bass.ds(g.n * P, P), :], res[:, g.slot, :]).then_inc(stored[g.slot], 16)

            pipeline(sp, NT, DEPTH, step)
            sp.wait_ge(stored[0], 16 * ((NT + 1) // 2))
            sp.wait_ge(stored[1], 16 * (NT // 2))

        @block.tensor
        def _(pe):
            pe.wait_ge(w_in, 4 * 16)
            pe.wait_ge(b_split, 1)

            def step(back):
                g = back(0)
                if g is not None:
                    pe.wait_ge(d_in[g.slot], g.half * 32 + 32)
                    need(pe, copied, g.n)
                    for m in range(2):
                        last = nc.tensor.transpose(psT[:, m, :], dt_[:, g.slot, m * 128:(m + 1) * 128], t.ident[0:P, 0:P])
                    last.then_inc(turned, 1)
                g = back(1)
                if g is not None:
                    pe.wait_ge(copied, g.n + 1)
                    need(pe, res_ready, g.n)
                    for m in range(2):
                        nc.tensor.matmul(psO[0:P, 0:D], dT[:, g.slot, m, :], wo[:, m, :], start=(m == 0), stop=False)
                    nc.tensor.matmul(psO[0:P, 0:D], t.ones_h[0:3, 0:P], bop[:, :], start=False, stop=True).then_inc(out_done, 1)

            pipeline(pe, NT, DEPTH, step)

        @block.scalar
        def _(act):
            def step(back):
                g = back(0)
                if g is not None:
                    act.wait_ge(turned, g.n + 1)
                    need(act, out_done, g.n - 1)
                    nc.scalar.activation(dT[:, g.slot, :, :], psT[:, 0:2, :], ACT.Copy, scale=t.scale[:, 1:2]).then_inc(copied, 1)

            pipeline(act, NT, DEPTH, step)

        @block.vector
        def _(dve):
            link = Link(dve, chain)
            dve.wait_ge(w_in, 4 * 16)
            split_row(nc, link, t, bop, bor, bow)
            dve.sem_inc(b_split, 1)

            def step(back):
                g = back(1)
                if g is not None:
                    dve.wait_ge(out_done, g.n + 1)
                    dve.wait_ge(d_in[g.slot], g.half * 32 + 32)
                    need(dve, stored[g.slot], g.half * 16)
                    nc.vector.tensor_tensor(res[:, g.slot, :], x1[:, g.slot, :], psO[0:P, 0:D], ALU.add).then_inc(res_ready, 1)

            pipeline(dve, NT, DEPTH, step)


class Tables:
    pass


def gnn_kernel(nc, x, src, dst, attr, W1, b1, W2, b2, U1, c1, U2, c2, Win, bin_, Wout, bout, out):
    dram = lambda n, s: nc.dram_tensor(n, s, FP32).ap()
    h_dram = dram("h_nodes", [N_NODES, D])
    in_order = (nc.dram_tensor("src_in_order", [N_EDGES], I32).ap(), nc.dram_tensor("dst_in_order", [N_EDGES], I32).ap(),
                dram("attr_in_order", [N_EDGES, R]))
    x1_dram = dram("x1_nodes", [N_NODES, D])
    y_dram = dram("y_nodes", [N_NODES, D])
    d_dram = dram("diffused", [N_NODES, D])
    t = Tables()
    with ExitStack() as ctx:
        sb = lambda n, s, d: ctx.enter_context(nc.sbuf_tensor(n, s, d))
        t.ident = sb("ident", [128, 128], FP32)
        t.before = sb("before", [128, 128], FP32)
        t.ones = sb("ones", [128, 128], FP32)
        t.ones_h = sb("ones_h", [128, 128], BF16)
        t.gate_cell = sb("gate_cell", [1, 2], FP32)
        t.cols_i = sb("cols_i", [128, 500], I32)
        t.cols = sb("cols", [128, 500], FP32)
        t.group_row = sb("group_row", [128, NG], I32)
        t.group_bucket = sb("group_bucket", [128, NG], FP32)
        t.group_bucket_i = sb("group_bucket_i", [128, NG], I32)
        t.bucket_node = sb("bucket_node", [128, NG], FP32)
        t.group_skip = sb("group_skip", [128, NG], FP32)
        t.unsorted = sb("unsorted", [128, 1], I32)
        t.scale = sb("scale", [128, 2], FP32)
        t.inv_deg = sb("inv_deg", [P, 2, NSTEPS, NT], FP32)
        constants_and_node_norm(nc, t, x, h_dram)
        with ExitStack() as edges:
            t.dst_i = edges.enter_context(nc.sbuf_tensor("dst_i", [P, EC], I32))
            t.dst_f = edges.enter_context(nc.sbuf_tensor("dst_f", [P, EC], FP32))
            t.bucket = edges.enter_context(nc.sbuf_tensor("bucket", [P, EC], FP32))
            t.base = edges.enter_context(nc.sbuf_tensor("base", [P, NT], FP32))
            edge_tables(nc, t, src, dst)
            edge_sort(nc, t, src, attr, in_order)
        t.src_of = sb("src_of", [128, NG * NW], FP32)
        t.local_of = sb("local_of", [128, NG * NW], FP32)
        with ExitStack() as nodes:
            t.sums = nodes.enter_context(nc.sbuf_tensor("sums", [P, NT, D], FP32))
            edge_messages(nc, t, h_dram, src, dst, attr, in_order, W1, b1, W2, b2)
            t.x1 = nodes.enter_context(nc.sbuf_tensor("x1", [P, NT, D], FP32))
            node_update(nc, t, x, h_dram, x1_dram, U1, c1, U2, c2)
            node_input(nc, t, y_dram, Win, bin_)
        with ExitStack() as graph:
            t.counts = graph.enter_context(nc.sbuf_tensor("counts", [128, NT * N_NODES + 8], FP16))
            count_edges(nc, t)
            degrees(nc, t)
            diffusion(nc, t, y_dram, d_dram)
        node_output(nc, t, x1_dram, d_dram, Wout, bout, out)


_INS = ["x", "src", "dst", "edge_attr_64", "L0_gnn_W1", "L0_gnn_b1", "L0_gnn_W2", "L0_gnn_b2", "L0_gnn_U1", "L0_gnn_c1",
        "L0_gnn_U2", "L0_gnn_c2", "L1_gnn_W_in", "L1_gnn_b_in", "L1_gnn_W_out", "L1_gnn_b_out"]


def kernel(**inputs):
    import numpy as _np
    import concourse.bacc as _bacc
    from concourse import mybir as _mybir
    from concourse.bass_utils import run_bass_kernel_spmd as _run

    nc = _bacc.Bacc("TRN2", target_bir_lowering=False, num_devices=1)
    arrays, args = {}, []
    for name in _INS:
        a = _np.asarray(inputs[name])
        if name in ("L1_gnn_W_in", "L1_gnn_W_out"):
            a = a.T
        a = _np.ascontiguousarray(a)
        arrays[f"in_{name}"] = a
        args.append(nc.dram_tensor(f"in_{name}", a.shape, _mybir.dt.from_np(a.dtype), kind="ExternalInput").ap())
    args.append(nc.dram_tensor("out_0", (N_NODES, D), FP32, kind="ExternalOutput").ap())
    gnn_kernel(nc, *args)
    r = _run(nc, [arrays], core_ids=[0])
    return r.results[0]["out_0"]
```

```python
import concourse.bass as bass
from concourse import mybir
from contextlib import ExitStack

FP32 = mybir.dt.float32
FP16 = mybir.dt.float16
BF16 = mybir.dt.bfloat16
I32 = mybir.dt.int32
U32 = mybir.dt.uint32
ALU = mybir.AluOpType
ACT = mybir.ActivationFunctionType
AX = mybir.AxisListType

N_NODES = 3125
N_EDGES = 53125
D = 256
R = 64
P = 125
NT = N_NODES // P
EC = N_EDGES // P
NSTEPS = 6
EPS = 1e-5

WIN = 128
GW = 2
GRP = WIN * GW
NG = (N_EDGES + NT * (GRP - 1)) // GRP
NG += NG % 2
TG = 2
TURNS = NG // TG
NW = TG * GW
CHK = 114
SLOT = 25
NCH = EC // SLOT
MAGIC = 1.5 * 2.0 ** 23
HALF = D // 2
MSG_SCALE = 1024.0
COLS = 256
LOW = 2048.0


class Link:

    def __init__(self, eng, sem):
        self.eng, self.sem, self.n = eng, sem, 0

    def __call__(self, ins):
        self.n += 1
        ins.then_inc(self.sem, 1)
        self.eng.wait_ge(self.sem, self.n)


def prepare(nc, t, x, src, dst, h_dram):
    with ExitStack() as ctx:
        sb = lambda n, s, d: ctx.enter_context(nc.sbuf_tensor(n, s, d))
        sem = lambda n: ctx.enter_context(nc.semaphore(n))
        xs = sb("xs", [P, NT, D], FP32)
        hs = sb("hs", [P, NT, D], FP32)
        stats = sb("stats", [P, NT, 6], FP32)
        mv = sb("mv", [P, NT, 2], FP32)
        rstd = sb("rstd", [P, NT], FP32)
        nmr = sb("nmr", [P, NT], FP32)
        here = sb("here", [CHK, (N_EDGES - 1) // CHK], I32)
        after = sb("after", [CHK, (N_EDGES - 1) // CHK], I32)
        falls = sb("falls", [CHK, 1], FP32)
        hot = sb("hot", [P, 2, EC], FP32)
        cnt = sb("cnt", [P, NT], FP32)
        tot = sb("tot", [128, NT], FP32)
        tab = sb("tab", [128, 5, NT], FP32)
        jump = sb("jump", [128, 2, NG], FP32)
        row_f = sb("row_f", [128, NG], FP32)
        ps = ctx.enter_context(nc.psum_tensor("ps_sort", [128, 512], FP32))
        made, chain, var_ready, std_ready, norm_ready, h_ready, h_out = (
            sem(n) for n in ("made", "prep_chain", "var_ready", "std_ready", "norm_ready", "h_ready", "h_out"))
        ids_in, next_in, counted, totals = (sem(n) for n in ("ids_in", "next_in", "counted", "totals"))
        XC = 5
        x_in = [sem(f"x_in{c}") for c in range(NT // XC)]
        block = ctx.enter_context(nc.Block())

        @block.sync
        def _(sp):
            sp.dma_start(t.dst_i[:, :], dst.rearrange("(p c) -> p c", p=P)).then_inc(ids_in, 16)
            x_v = x.rearrange("(n p) d -> p n d", p=P)
            for c in range(NT // XC):
                sp.dma_start(xs[:, c * XC:(c + 1) * XC, :], x_v[:, c * XC:(c + 1) * XC, :]).then_inc(x_in[c], 16)
            sp.dma_start(here[:, :], dst[0:N_EDGES - 1].rearrange("(p c) -> p c", p=CHK)).then_inc(next_in, 16)
            sp.dma_start(after[:, :], dst[1:N_EDGES].rearrange("(p c) -> p c", p=CHK)).then_inc(next_in, 16)
            h_v = h_dram.rearrange("(n p) d -> p n d", p=P)
            for c in range(NT // XC):
                sp.wait_ge(h_ready, c + 1)
                sp.dma_start(h_v[:, c * XC:(c + 1) * XC, :], hs[:, c * XC:(c + 1) * XC, :]).then_inc(h_out, 16)
            sp.wait_ge(h_out, 16 * (NT // XC))

        @block.gpsimd
        def _(pool):
            pool.iota(t.cols_i[:, :], pattern=[[1, COLS]], base=0, channel_multiplier=0).then_inc(made, 1)
            pool.wait_ge(made, 1)
            pool.tensor_copy(t.cols[:, :], t.cols_i[:, :]).then_inc(made, 1)
            pool.memset(t.ident[:, :], 0.0).then_inc(made, 1)
            pool.memset(t.before[:, :], 1.0).then_inc(made, 1)
            pool.memset(t.ones[:, :], 1.0).then_inc(made, 1)
            pool.memset(t.ones_h[:, :], 1.0).then_inc(made, 1)
            pool.wait_ge(made, 6)
            pool.affine_select(out=t.ident[:, :], in_=t.ident[:, :], compare_op=ALU.not_equal, fill=1.0,
                               base=0, pattern=[[-1, 128]], channel_multiplier=1).then_inc(made, 1)
            pool.affine_select(out=t.before[:, :], in_=t.before[:, :], compare_op=ALU.is_gt, fill=0.0,
                               base=0, pattern=[[1, 128]], channel_multiplier=-1).then_inc(made, 1)
            pool.iota(t.place_i[:, :, :], pattern=[[0, TG], [1, GW]], base=0, channel_multiplier=GW).then_inc(made, 1)
            pool.wait_ge(made, 9)
            pool.tensor_copy(t.place[:, :, :], t.place_i[:, :, :]).then_inc(made, 1)
            pool.wait_ge(made, 10)

        @block.tensor
        def _(pe):
            pe.wait_ge(made, 10)
            pe.wait_ge(counted, 1)
            nc.tensor.matmul(ps[0:128, 0:NT], t.before[0:P, :], cnt[:, :], start=True, stop=True)
            nc.tensor.matmul(ps[0:128, 64:64 + NT], t.ones[0:P, :], cnt[:, :], start=True, stop=True)
            nc.tensor.matmul(ps[0:128, 128:129], t.ones[0:CHK, :], falls[:, :], start=True, stop=True).then_inc(totals, 1)

        @block.scalar
        def _(act):
            act.wait_ge(var_ready, 1)
            nc.scalar.activation(rstd[:, :], nmr[:, :], ACT.Sqrt).then_inc(std_ready, 1)
            act.wait_ge(norm_ready, 1)
            for n in range(NT):
                last = nc.scalar.activation(hs[:, n, :], xs[:, n, :], ACT.Relu, bias=nmr[:, n:n + 1],
                                            scale=rstd[:, n:n + 1])
                if n % XC == XC - 1:
                    last.then_inc(h_ready, 1)

        @block.vector
        def _(dve):
            link = Link(dve, chain)
            v = nc.vector
            for n in range(NT):
                if n % XC == 0:
                    dve.wait_ge(x_in[n // XC], 16)
                last = v.bn_stats(stats[:, n, :], xs[:, n, :])
            link(last)
            for n in range(NT):
                last = v.bn_aggr(mv[:, n, :], stats[:, n, :])
            link(last)
            link(v.tensor_scalar(rstd[:, :], mv[:, :, 1], EPS, None, ALU.add))
            v.reciprocal(nmr[:, :], rstd[:, :]).then_inc(var_ready, 1)
            dve.wait_ge(std_ready, 1)
            v.scalar_tensor_tensor(out=nmr[:, :], in0=mv[:, :, 0], scalar=-1.0, in1=rstd[:, :],
                                   op0=ALU.mult, op1=ALU.mult).then_inc(norm_ready, 1)
            dve.wait_ge(ids_in, 16)
            dve.wait_ge(made, 10)
            link(v.tensor_copy(t.dst_f[:, :], t.dst_i[:, :]))
            link(v.tensor_scalar(t.bucket[:, :], t.dst_f[:, :], -float(P // 2), 1.0 / P, ALU.add, ALU.mult))
            link(v.tensor_scalar(t.bucket[:, :], t.bucket[:, :], MAGIC, None, ALU.add))
            link(v.tensor_scalar(t.bucket[:, :], t.bucket[:, :], MAGIC, None, ALU.subtract))
            n0 = link.n
            with dve.Fori(0, NT) as b:
                v.tensor_scalar(hot[:, 0, :], t.bucket[:, :], t.cols[0:P, bass.ds(b, 1)], None, ALU.is_equal).then_inc(chain, 1)
                dve.wait_ge(chain, b * 2 + (n0 + 1))
                v.tensor_reduce(cnt[:, bass.ds(b, 1)], hot[:, 0, :], AX.X, ALU.add).then_inc(chain, 1)
                dve.wait_ge(chain, b * 2 + (n0 + 2))
            link.n = n0 + 2 * NT
            dve.wait_ge(next_in, 32)
            wide = hot[0:CHK, :, :].rearrange("p a b -> p (a b)")[:, 0:(N_EDGES - 1) // CHK]
            link(v.tensor_tensor(wide, after[:, :], here[:, :], ALU.is_lt))
            v.tensor_reduce(falls[:, :], wide, AX.X, ALU.add).then_inc(counted, 1)
            dve.wait_ge(totals, 1)
            link(v.tensor_copy(t.unsorted[:, :], ps[:, 128:129]))
            link(v.tensor_copy(tot[:, :], ps[:, 64:64 + NT]))
            link(v.tensor_tensor_scan(tab[:, 0, :], t.ones[:, 0:NT], tot[:, :], 0.0, ALU.mult, ALU.add))
            link(v.tensor_tensor(tab[:, 0, :], tab[:, 0, :], tot[:, :], ALU.subtract))
            link(v.tensor_tensor(t.base[:, :], ps[0:P, 0:NT], tab[0:P, 0, :], ALU.add))
            link(v.tensor_scalar(tab[:, 1, :], tot[:, :], GRP / 2 - 0.5, 1.0 / GRP, ALU.add, ALU.mult))
            link(v.tensor_scalar(tab[:, 1, :], tab[:, 1, :], MAGIC, None, ALU.add))
            link(v.tensor_scalar(tab[:, 1, :], tab[:, 1, :], MAGIC, None, ALU.subtract))
            link(v.tensor_tensor_scan(tab[:, 2, :], t.ones[:, 0:NT], tab[:, 1, :], 0.0, ALU.mult, ALU.add))
            link(v.tensor_tensor(tab[:, 2, :], tab[:, 2, :], tab[:, 1, :], ALU.subtract))
            link(v.scalar_tensor_tensor(out=tab[:, 3, :], in0=tab[:, 2, :], scalar=-float(GRP), in1=tab[:, 0, :],
                                        op0=ALU.mult, op1=ALU.add))
            link(v.tensor_tensor(tab[:, 4, 1:NT], tab[:, 3, 1:NT], tab[:, 3, 0:NT - 1], ALU.subtract))
            link(v.tensor_scalar(row_f[:, :], t.cols[:, 0:NG], float(GRP), None, ALU.mult))
            link(v.memset(t.group_bucket[:, :], 0.0))
            n1 = link.n
            with dve.Fori(1, NT) as b:
                v.tensor_scalar(jump[:, 0, :], t.cols[:, 0:NG], tab[:, 2, bass.ds(b, 1)], None, ALU.is_ge).then_inc(chain, 1)
                v.tensor_scalar(jump[:, 1, :], t.cols[:, 0:NG], tab[:, 2, bass.ds(b, 1)], tab[:, 4, bass.ds(b, 1)],
                                ALU.is_ge, ALU.mult).then_inc(chain, 1)
                dve.wait_ge(chain, b * 4 + (n1 - 2))
                v.tensor_tensor(t.group_bucket[:, :], t.group_bucket[:, :], jump[:, 0, :], ALU.add).then_inc(chain, 1)
                v.tensor_tensor(row_f[:, :], row_f[:, :], jump[:, 1, :], ALU.add).then_inc(chain, 1)
                dve.wait_ge(chain, b * 4 + n1)
            link.n = n1 + 4 * (NT - 1)
            link(v.tensor_scalar(jump[:, 0, :], row_f[:, :], float(N_EDGES - GRP), None, ALU.min))
            link(v.tensor_tensor(t.group_skip[:, :], row_f[:, :], jump[:, 0, :], ALU.subtract))
            link(v.tensor_copy(t.group_row[:, :], jump[:, 0, :]))
            link(v.tensor_copy(t.group_bucket_i[:, :], t.group_bucket[:, :]))
            link(v.tensor_scalar(t.bucket_node[:, :], t.group_bucket[:, :], float(P), None, ALU.mult))
            link(v.memset(t.opens[:, :], 1))
            link(v.memset(t.closes[:, :], 1))
            link(v.tensor_tensor(t.opens[:, 1:NG], t.group_bucket[:, 1:NG], t.group_bucket[:, 0:NG - 1], ALU.not_equal))
            link(v.tensor_copy(t.closes[:, 0:NG - 1], t.opens[:, 1:NG]))


def edge_sort(nc, t, src, attr, in_order):
    with ExitStack() as ctx:
        sb = lambda n, s, d: ctx.enter_context(nc.sbuf_tensor(n, s, d))
        sem = lambda n: ctx.enter_context(nc.semaphore(n))
        src_i = sb("src_i", [P, EC], I32)
        hot = sb("hot_rank", [P, EC], FP32)
        rank = sb("rank", [P, EC], FP32)
        pos = sb("pos", [P, EC], FP32)
        pos_i = sb("pos_i", [P, EC], I32)
        zeros = sb("zeros", [P, EC], FP32)
        attrs = sb("attrs", [P, 2, SLOT, R], FP32)
        slot_src = sb("slot_src", [P, 2, SLOT], I32)
        slot_dst = sb("slot_dst", [P, 2, SLOT], I32)
        slot_pos = sb("slot_pos", [P, 2, SLOT], I32)
        ids_in, chain, filled, passed = (sem("s_" + n) for n in ("ids_in", "chain", "filled", "passed"))
        attr_in = [sem("attr_in0"), sem("attr_in1")]
        scattered = [sem("scattered0"), sem("scattered1")]
        attr_v = attr.rearrange("(p c s) r -> p c s r", p=P, s=SLOT)
        SENT = 3 * 16 * SLOT
        HALVES = (NCH - 1) // 2
        block = ctx.enter_context(nc.Block())

        @block.sync
        def _(sp):
            def load(c, q, turn):
                if turn is not None:
                    sp.wait_ge(scattered[q], turn * SENT)
                sp.dma_start(attrs[:, q, :, :], attr_v[:, c, :, :]).then_inc(attr_in[q], 16)

            with sp.If(sp.value_load(t.unsorted[0:1, 0:1], min_val=0, max_val=N_EDGES) > 0):
                sp.dma_start(src_i[:, :], src.rearrange("(p c) -> p c", p=P)).then_inc(ids_in, 16)
                load(0, 0, None)
                load(1, 1, None)
                with sp.Fori(1, HALVES) as k:
                    load(2 * k, 0, k)
                    load(2 * k + 1, 1, k)
                load(NCH - 1, 0, HALVES)

        @block.gpsimd
        def _(pool):
            pool.memset(t.gate_cell[:, :], 0.0).then_inc(passed, 1)

            def scatter(q, turn):
                pool.wait_ge(filled, 2 * turn + q + 1)
                pool.wait_ge(passed, 2 * turn + q + 1)
                pool.tensor_tensor(t.gate_cell[:, 1:2], t.gate_cell[:, 0:1], t.gate_cell[:, 0:1], ALU.add).then_inc(passed, 1)
                for s in range(SLOT):
                    at = slot_pos[:, q, s:s + 1].bitcast(U32)
                    for to, what in zip(in_order, (slot_src[:, q, s:s + 1], slot_dst[:, q, s:s + 1], attrs[:, q, s, :])):
                        to = to if len(to.shape) == 2 else to.rearrange("(n o) -> n o", o=1)
                        pool.indirect_dma_start(out=to, out_offset=bass.IndirectOffsetOnAxis(ap=at, axis=0),
                                                in_=what, in_offset=None).then_inc(scattered[q], 16)

            with pool.If(pool.value_load(t.unsorted[0:1, 0:1], min_val=0, max_val=N_EDGES) > 0):
                with pool.Fori(0, HALVES) as k:
                    scatter(0, k)
                    scatter(1, k)
                scatter(0, HALVES)
                pool.wait_ge(scattered[0], (HALVES + 1) * SENT)
                pool.wait_ge(scattered[1], HALVES * SENT)

        @block.vector
        def _(dve):
            v = nc.vector

            def fill(c, q, turn, landed):
                dve.wait_ge(attr_in[q], landed)
                if turn is not None:
                    dve.wait_ge(scattered[q], turn * SENT)
                v.tensor_copy(slot_src[:, q, :], src_i[:, bass.ds(c * SLOT, SLOT)]).then_inc(chain, 1)
                v.tensor_copy(slot_dst[:, q, :], t.dst_i[:, bass.ds(c * SLOT, SLOT)]).then_inc(chain, 1)
                v.tensor_copy(slot_pos[:, q, :], pos_i[:, bass.ds(c * SLOT, SLOT)]).then_inc(filled, 1)

            with dve.If(dve.value_load(t.unsorted[0:1, 0:1], min_val=0, max_val=N_EDGES) > 0):
                link = Link(dve, chain)
                link(v.memset(zeros[:, :], 0.0))
                link(v.memset(pos[:, :], -1.0))
                n2 = link.n
                with dve.Fori(0, NT) as b:
                    v.tensor_scalar(hot[:, :], t.bucket[:, :], t.cols[0:P, bass.ds(b, 1)], None, ALU.is_equal).then_inc(chain, 1)
                    dve.wait_ge(chain, b * 4 + (n2 + 1))
                    v.tensor_tensor_scan(rank[:, :], hot[:, :], zeros[:, :], t.base[:, bass.ds(b, 1)], ALU.add, ALU.add).then_inc(chain, 1)
                    dve.wait_ge(chain, b * 4 + (n2 + 2))
                    v.tensor_tensor(hot[:, :], hot[:, :], rank[:, :], ALU.mult).then_inc(chain, 1)
                    dve.wait_ge(chain, b * 4 + (n2 + 3))
                    v.tensor_tensor(pos[:, :], pos[:, :], hot[:, :], ALU.add).then_inc(chain, 1)
                    dve.wait_ge(chain, b * 4 + (n2 + 4))
                link.n = n2 + 4 * NT
                link(v.tensor_copy(pos_i[:, :], pos[:, :]))
                dve.wait_ge(ids_in, 16)
                fill(0, 0, None, 16)
                fill(1, 1, None, 16)
                with dve.Fori(1, HALVES) as k:
                    fill(2 * k, 0, k, 16 * k + 16)
                    fill(2 * k + 1, 1, k, 16 * k + 16)
                fill(NCH - 1, 0, HALVES, 16 * HALVES + 16)
                dve.wait_ge(chain, link.n + 2 * NCH)


class Turn:

    def __init__(self, k, c, slots=2):
        self.n, self.half, self.slot = slots * k + c, k + c // slots, c % slots


def need(eng, sem, value):
    if not isinstance(value, int) or value > 0:
        eng.wait_ge(sem, value)


def pipeline(eng, count, depth, step):
    first = 2 * ((depth + 3) // 2)
    pairs = max(0, (count - first) // 2)

    def peeled(s):
        step(lambda d: Turn(0, s - d) if 0 <= s - d < count else None)

    for s in range(first):
        peeled(s)
    if pairs > 0:
        with eng.Fori(0, pairs) as k:
            for c in (first, first + 1):
                step(lambda d: Turn(k, c - d))
    for s in range(first + 2 * pairs, count + depth):
        peeled(s)


def split_row(nc, link, t, parts, row, work):
    v = nc.vector
    hi, rest = work[:, 0, :], work[:, 1, :]
    acc = work[:, 2, :]
    link(v.tensor_copy(parts[:, :], row[:, :]))
    link(v.tensor_copy(hi, parts[:, :]))
    link(v.tensor_scalar(acc, hi, t.ident[0:3, 0:1], None, ALU.mult))
    link(v.tensor_tensor(rest, row[:, :], hi, ALU.subtract))
    link(v.tensor_copy(parts[:, :], rest))
    link(v.tensor_copy(hi, parts[:, :]))
    link(v.scalar_tensor_tensor(out=acc, in0=hi, scalar=t.ident[0:3, 1:2], in1=acc, op0=ALU.mult, op1=ALU.add))
    link(v.tensor_tensor(rest, rest, hi, ALU.subtract))
    link(v.scalar_tensor_tensor(out=acc, in0=rest, scalar=t.ident[0:3, 2:3], in1=acc, op0=ALU.mult, op1=ALU.add))
    link(v.tensor_copy(parts[:, :], acc))


def edge_messages(nc, t, h_dram, src, dst, attr, in_order, W1, b1, W2, b2):
    with ExitStack() as ctx:
        sb = lambda n, s, d: ctx.enter_context(nc.sbuf_tensor(n, s, d))
        pb = lambda n, s: ctx.enter_context(nc.psum_tensor(n, s, FP32))
        sem = lambda n: ctx.enter_context(nc.semaphore(n))
        w1 = sb("w1", [2 * R, 2, D], FP32)
        w2 = sb("w2", [128, 2, D], FP32)
        b1c = sb("b1c", [128, 2], FP32)
        b2r = sb("b2r", [3, D], FP32)
        b2w = sb("b2w", [3, 3, D], FP32)
        b2p = sb("b2p", [3, D], BF16)
        at = sb("attr_tile", [128, 2, NW, R], FP32)
        ids = sb("ids_tile", [128, 2, 2, TG, GW], I32)
        src_i = sb("src_idx", [128, 2, NW], I32)
        skip = sb("skip", [128, 2, TG, GW], FP32)
        hg = sb("hg", [128, 2, NW, D], FP32)
        rT = sb("rT", [2 * R, 2, 2 * WIN], FP32)
        sg = sb("sg", [128, 2, 2, 2 * WIN], FP32)
        hid = sb("hid", [128, 2, 2, 2 * WIN], FP32)
        gate = sb("gate", [128, NW, D], FP32)
        msg = sb("msg", [128, NW, D], FP32)
        msg_hi = sb("msg_hi", [128, 2, NW, D + 1], FP16)
        msg_lo = sb("msg_lo", [128, 2, NW, D], FP16)
        hot = sb("hot_dst", [128, 2, NW, P], FP16)
        psT = pb("psT", [128, 512])
        psH = pb("psH", [128, 2, 2, 2 * WIN])
        psG = pb("psG", [128, NW, D])
        psA = pb("psA", [128, TG, 512])
        names = ["w_in", "b_split", "chain", "turned", "copied", "up_done", "sig_ready", "hid_ready", "gate_done",
                 "gate_ready", "msg_ready", "high_ready", "low_ready", "ids_ready", "hot_ready", "sum_done", "sum_added", "passed"]
        (w_in, b_split, chain, turned, copied, up_done, sig_ready, hid_ready, gate_done,
         gate_ready, msg_ready, high_ready, low_ready, ids_ready, hot_ready, sum_done, sum_added, passed) = (sem("m_" + n) for n in names)
        rec_in = [sem("rec_in0"), sem("rec_in1")]
        ids_chain, w1_clear = sem("ids_chain"), sem("w1_clear")
        hg_in = [sem("hg_in0"), sem("hg_in1")]
        DEPTH = 4
        LOADS = 3 * TG * 16
        block = ctx.enter_context(nc.Block())

        @block.sync
        def _(sp):
            sp.wait_ge(w1_clear, 1)
            sp.dma_start(w1[0:R, 0, :], W1).then_inc(w_in, 16)
            sp.dma_start(w1[R:2 * R, 1, :], W1).then_inc(w_in, 16)
            sp.dma_start(w2[:, :, :], W2.rearrange("(m p) n -> p m n", p=128)).then_inc(w_in, 16)
            sp.dma_start(b1c[:, :], b1.rearrange("(m p) -> p m", p=128), allow_slow_non_contiguous=True).then_inc(w_in, 16)
            for r in range(3):
                sp.dma_start(b2r[r:r + 1, :], b2.rearrange("(o n) -> o n", o=1)).then_inc(w_in, 16)

            def loads(src, dst, attr):
                def step(back):
                    g = back(0)
                    if g is None:
                        return
                    need(sp, turned, g.n - 1)
                    need(sp, ids_ready, g.n - 1)
                    for u in range(TG):
                        row = sp.value_load(t.group_row[0:1, bass.ds(g.n * TG + u, 1)], min_val=0, max_val=N_EDGES - GRP)
                        rows = bass.ds(row, GRP)
                        pairs = lambda a: a[rows].rearrange("(p j) -> p j", j=GW)
                        sp.dma_start(ids[:, g.slot, 0, u, :], pairs(src)).then_inc(rec_in[g.slot], 16)
                        sp.dma_start(ids[:, g.slot, 1, u, :], pairs(dst)).then_inc(rec_in[g.slot], 16)
                        sp.dma_start(at[:, g.slot, u * GW:(u + 1) * GW, :],
                                     attr[rows, :].rearrange("(p j) c -> p j c", j=GW)).then_inc(rec_in[g.slot], 16)

                pipeline(sp, TURNS, DEPTH, step)

            with sp.If(sp.value_load(t.unsorted[0:1, 0:1], min_val=0, max_val=N_EDGES) > 0):
                loads(*in_order)
            with sp.Else():
                loads(src, dst, attr)

        @block.gpsimd
        def _(pool):
            pool.memset(t.gate_cell[:, :], 0.0).then_inc(passed, 1)

            def step(back):
                g = back(0)
                if g is None:
                    return
                need(pool, msg_ready, g.n - 1)
                pool.wait_ge(ids_ready, g.n + 1)
                pool.wait_ge(passed, g.n + 1)
                pool.tensor_tensor(t.gate_cell[:, 1:2], t.gate_cell[:, 0:1], t.gate_cell[:, 0:1], ALU.add).then_inc(passed, 1)
                for j in range(NW):
                    pool.indirect_dma_start(
                        out=hg[:, g.slot, j, :], out_offset=None, in_=h_dram[:, :],
                        in_offset=bass.IndirectOffsetOnAxis(ap=src_i[:, g.slot, j:j + 1].bitcast(U32), axis=0)
                    ).then_inc(hg_in[g.slot], 16)

            pipeline(pool, TURNS, DEPTH, step)

        @block.tensor
        def _(pe):
            pe.wait_ge(w_in, 7 * 16)
            pe.wait_ge(b_split, 1)

            def step(back):
                g = back(0)
                if g is not None:
                    pe.wait_ge(rec_in[g.slot], g.half * LOADS + LOADS)
                    need(pe, copied, g.n)
                    for pair in range(2):
                        last = nc.tensor.transpose(psT[:, pair * WIN:(pair + 1) * WIN],
                                                   at[:, g.slot, 2 * pair:2 * pair + 2, :].rearrange("p j r -> p (j r)"), t.ident[:, :])
                    last.then_inc(turned, 1)
                g = back(1)
                if g is not None:
                    pe.wait_ge(copied, g.n + 1)
                    need(pe, hid_ready, g.n)
                    for m in range(2):
                        for odd in range(2):
                            last = nc.tensor.matmul(psH[:, odd, m, :], w1[:, odd, m * 128:(m + 1) * 128],
                                                    rT[:, g.slot, :], start=True, stop=True)
                    last.then_inc(up_done, 1)
                g = back(2)
                if g is not None:
                    pe.wait_ge(hid_ready, g.n + 1)
                    need(pe, gate_ready, g.n)
                    for j in range(NW):
                        for m in range(2):
                            nc.tensor.matmul(psG[:, j, :], hid[:, j % 2, m, j // 2 * WIN:(j // 2 + 1) * WIN], w2[:, m, :],
                                             start=(m == 0), stop=False)
                        last = nc.tensor.matmul(psG[:, j, :], t.ones_h[0:3, :], b2p[:, :], start=False, stop=True)
                    last.then_inc(gate_done, 1)
                g = back(4)
                if g is not None:
                    pe.wait_ge(high_ready, g.n + 1)
                    pe.wait_ge(low_ready, g.n + 1)
                    need(pe, sum_added, g.n * TG)
                    for u in range(TG):
                        for j in range(u * GW, (u + 1) * GW):
                            nc.tensor.matmul(psA[0:P, u, 0:D + 1], hot[:, g.slot, j, :], msg_hi[:, g.slot, j, :],
                                             start=(j == u * GW), stop=False)
                            last = nc.tensor.matmul(psA[0:P, u, 0:D], hot[:, g.slot, j, :], msg_lo[:, g.slot, j, :],
                                                    start=False, stop=(j == (u + 1) * GW - 1))
                        last.then_inc(sum_done, 1)

            pipeline(pe, TURNS, DEPTH, step)

        @block.scalar
        def _(act):
            act.wait_ge(w_in, 7 * 16)

            def step(back):
                g = back(3)
                if g is not None:
                    act.wait_ge(msg_ready, g.n + 1)
                    need(act, sum_done, (g.n - 1) * TG)
                    nc.scalar.mul(msg_hi[:, g.slot, :, 0:D], msg[:, :, :], MSG_SCALE).then_inc(high_ready, 1)
                g = back(0)
                if g is not None:
                    act.wait_ge(turned, g.n + 1)
                    need(act, up_done, g.n - 1)
                    nc.scalar.copy(rT[:, g.slot, :], psT[:, 0:2 * WIN]).then_inc(copied, 1)
                g = back(1)
                if g is not None:
                    act.wait_ge(up_done, g.n + 1)
                    need(act, hid_ready, g.n)
                    for m in range(2):
                        last = nc.scalar.activation(sg[:, :, m, :], psH[:, :, m, :], ACT.Sigmoid, bias=b1c[:, m:m + 1])
                    last.then_inc(sig_ready, 1)
                g = back(2)
                if g is not None:
                    act.wait_ge(gate_done, g.n + 1)
                    need(act, msg_ready, g.n)
                    nc.scalar.activation(gate[:, :, :], psG[:, :, :], ACT.Sigmoid).then_inc(gate_ready, 1)

            pipeline(act, TURNS, DEPTH, step)

        @block.vector
        def _(dve):
            link = Link(dve, chain)
            v = nc.vector
            v.memset(w1[:, :, :], 0.0).then_inc(w1_clear, 1)
            link(v.memset(t.sums[:, :, :], 0.0))
            link(v.memset(msg_hi[:, :, :, D:D + 1], MSG_SCALE))
            dve.wait_ge(w_in, 7 * 16)
            split_row(nc, link, t, b2p, b2r, b2w)
            dve.sem_inc(b_split, 1)

            def step(back):
                g = back(0)
                if g is not None:
                    dve.wait_ge(rec_in[g.slot], g.half * LOADS + LOADS)
                    need(dve, hg_in[g.slot], g.half * (16 * NW))
                    local = t.local_of[:, bass.ds(g.n * NW, NW)].rearrange("p (u j) -> p u j", u=TG)
                    of_group = lambda a: a[:, bass.ds(g.n * TG, TG)].rearrange("p (u o) -> p u o", o=1).to_broadcast([128, TG, GW])
                    v.tensor_tensor(skip[:, g.slot, :, :], t.place[:, :, :], of_group(t.group_skip), ALU.is_lt).then_inc(ids_chain, 1)
                    v.tensor_tensor(local, ids[:, g.slot, 1, :, :], of_group(t.bucket_node), ALU.subtract).then_inc(ids_chain, 1)
                    now = ids[:, g.slot, 0, :, :].rearrange("p u j -> p (u j)")
                    v.tensor_copy(t.src_of[:, bass.ds(g.n * NW, NW)], now)
                    v.tensor_copy(src_i[:, g.slot, :], now)
                    dve.wait_ge(ids_chain, g.n * 2 + 2)
                    v.scalar_tensor_tensor(out=local, in0=skip[:, g.slot, :, :], scalar=-float(4 * N_NODES), in1=local,
                                           op0=ALU.mult, op1=ALU.add).then_inc(ids_ready, 1)
                g = back(1)
                if g is not None:
                    dve.wait_ge(sig_ready, g.n + 1)
                    need(dve, gate_done, g.n)
                    for m in range(2):
                        last = v.scalar_tensor_tensor(out=hid[:, :, m, :], in0=psH[:, :, m, :], scalar=b1c[:, m:m + 1],
                                                      in1=sg[:, :, m, :], op0=ALU.add, op1=ALU.mult)
                    last.then_inc(hid_ready, 1)
                g = back(3)
                if g is not None:
                    dve.wait_ge(high_ready, g.n + 1)
                    v.scalar_tensor_tensor(out=msg_lo[:, g.slot, :, :], in0=msg[:, :, :], scalar=MSG_SCALE,
                                           in1=msg_hi[:, g.slot, :, 0:D], op0=ALU.mult, op1=ALU.subtract).then_inc(low_ready, 1)
                g = back(2)
                if g is not None:
                    dve.wait_ge(gate_ready, g.n + 1)
                    dve.wait_ge(hg_in[g.slot], (g.half + 1) * (16 * NW))
                    need(dve, high_ready, g.n)
                    need(dve, low_ready, g.n)
                    v.tensor_tensor(msg[:, :, :], gate[:, :, :], hg[:, g.slot, :, :], ALU.mult).then_inc(msg_ready, 1)
                    need(dve, sum_done, (g.n - 1) * TG)
                    v.tensor_tensor(hot[:, g.slot, :, :], t.cols[:, 0:P].rearrange("p (o c) -> p o c", o=1).to_broadcast([128, NW, P]),
                                    t.local_of[:, bass.ds(g.n * NW, NW)].rearrange("p (j o) -> p j o", o=1).to_broadcast([128, NW, P]),
                                    ALU.is_equal).then_inc(hot_ready, 1)
                g = back(4)
                if g is not None:
                    for u in range(TG):
                        n = g.n * TG + u
                        b = dve.value_load(t.group_bucket_i[0:1, bass.ds(n, 1)], min_val=0, max_val=NT - 1)
                        dve.wait_ge(sum_done, n + 1)
                        need(dve, sum_added, n)
                        at_b = t.sums[:, bass.ds(b, 1), :]
                        v.tensor_tensor(at_b, at_b, psA[0:P, u:u + 1, 0:D + 1], ALU.add).then_inc(sum_added, 1)

            pipeline(dve, TURNS, DEPTH, step)
            dve.wait_ge(sum_added, TG * TURNS)


def node_update(nc, t, x, h_dram, x1_dram, U1, c1, U2, c2):
    with ExitStack() as ctx:
        sb = lambda n, s, d: ctx.enter_context(nc.sbuf_tensor(n, s, d))
        pb = lambda n, s: ctx.enter_context(nc.psum_tensor(n, s, FP32))
        sem = lambda n: ctx.enter_context(nc.semaphore(n))
        u1 = sb("u1", [128, 4, D], FP32)
        u2 = sb("u2", [128, 2, D], FP32)
        c1c = sb("c1c", [128, 2], FP32)
        c2r = sb("c2r", [3, D], FP32)
        c2w = sb("c2w", [3, 3, D], FP32)
        c2p = sb("c2p", [3, D], BF16)
        cat = sb("cat", [P, 2, 2, D], FP32)
        h = sb("h_all", [P, NT, D], FP32)
        catT = sb("catT", [128, 2, 4, P], FP32)
        sg = sb("sgu", [128, 2, P], FP32)
        hid = sb("hidu", [128, 2, P], FP32)
        psT = pb("psT1", [128, 4, P])
        psU = pb("psU", [128, 2, P])
        psV = pb("psV", [128, 512])
        names = ["w_in", "b_split", "chain", "sums_set", "turned", "copied", "up_done", "sig_ready", "hid_ready",
                 "down_done", "base_ready", "x1_ready", "stats_ready"]
        (w_in, b_split, chain, sums_set, turned, copied, up_done, sig_ready, hid_ready,
         down_done, base_ready, x1_ready, stats_ready) = (sem("u_" + n) for n in names)
        xh_in = sem("xh_in")
        stored = sem("x1_stored")
        DEPTH = 2
        block = ctx.enter_context(nc.Block())

        @block.sync
        def _(sp):
            sp.dma_start(u1[:, :, :], U1.rearrange("(m p) n -> p m n", p=128)).then_inc(w_in, 16)
            sp.dma_start(u2[:, :, :], U2.rearrange("(m p) n -> p m n", p=128)).then_inc(w_in, 16)
            sp.dma_start(c1c[:, :], c1.rearrange("(m p) -> p m", p=128), allow_slow_non_contiguous=True).then_inc(w_in, 16)
            for r in range(3):
                sp.dma_start(c2r[r:r + 1, :], c2.rearrange("(o n) -> o n", o=1)).then_inc(w_in, 16)

            sp.dma_start(h[:, :, :], h_dram.rearrange("(n p) d -> p n d", p=P)).then_inc(xh_in, 16)
            sp.dma_start(t.x1[:, :, :], x.rearrange("(n p) d -> p n d", p=P)).then_inc(xh_in, 16)
            sp.wait_ge(x1_ready, NT)
            sp.dma_start(x1_dram.rearrange("(n p) d -> p n d", p=P), t.x1[:, :, :]).then_inc(stored, 16)
            sp.wait_ge(stored, 16)

        @block.gpsimd
        def _(pool):
            pool.wait_ge(xh_in, 32)

            def step(back):
                g = back(0)
                if g is not None:
                    need(pool, turned, g.n - 1)
                    pool.tensor_copy(cat[:, g.slot, 0, :], h[:, bass.ds(g.n, 1), :].rearrange("p o d -> p (o d)")).then_inc(sums_set, 1)
                    pool.tensor_copy(cat[:, g.slot, 1, :], t.sums[:, bass.ds(g.n, 1), 0:D].rearrange("p o d -> p (o d)")).then_inc(sums_set, 1)

            pipeline(pool, NT, DEPTH, step)

        @block.tensor
        def _(pe):
            pe.wait_ge(w_in, 6 * 16)
            pe.wait_ge(b_split, 1)

            def step(back):
                g = back(0)
                if g is not None:
                    pe.wait_ge(sums_set, g.n * 2 + 2)
                    need(pe, copied, g.n)
                    for m in range(4):
                        last = nc.tensor.transpose(psT[:, m, :], cat[:, g.slot, m // 2, (m % 2) * 128:(m % 2 + 1) * 128],
                                                   t.ident[0:P, 0:P])
                    last.then_inc(turned, 1)
                g = back(1)
                if g is not None:
                    pe.wait_ge(copied, g.n + 1)
                    need(pe, hid_ready, g.n)
                    for o in range(2):
                        for m in range(4):
                            last = nc.tensor.matmul(psU[:, o, :], u1[:, m, o * 128:(o + 1) * 128], catT[:, g.slot, m, :],
                                                    start=(m == 0), stop=(m == 3))
                    last.then_inc(up_done, 1)
                g = back(2)
                if g is not None:
                    pe.wait_ge(hid_ready, g.n + 1)
                    need(pe, x1_ready, g.n)
                    for m in range(2):
                        nc.tensor.matmul(psV[0:P, 0:D], hid[:, m, :], u2[:, m, :], start=(m == 0), stop=False)
                    nc.tensor.matmul(psV[0:P, 0:D], t.ones_h[0:3, 0:P], c2p[:, :], start=False, stop=True).then_inc(down_done, 1)

            pipeline(pe, NT, DEPTH, step)

        @block.scalar
        def _(act):
            act.wait_ge(w_in, 6 * 16)

            def step(back):
                g = back(0)
                if g is not None:
                    act.wait_ge(turned, g.n + 1)
                    need(act, up_done, g.n - 1)
                    nc.scalar.copy(catT[:, g.slot, 0:2, :], psT[:, 0:2, :])
                    nc.scalar.mul(catT[:, g.slot, 2:4, :], psT[:, 2:4, :], 1.0 / MSG_SCALE).then_inc(copied, 1)
                g = back(1)
                if g is not None:
                    act.wait_ge(up_done, g.n + 1)
                    need(act, hid_ready, g.n)
                    for m in range(2):
                        last = nc.scalar.activation(sg[:, m, :], psU[:, m, :], ACT.Sigmoid, bias=c1c[:, m:m + 1])
                    last.then_inc(sig_ready, 1)

            pipeline(act, NT, DEPTH, step)

        @block.vector
        def _(dve):
            link = Link(dve, chain)
            v = nc.vector
            dve.wait_ge(w_in, 6 * 16)
            split_row(nc, link, t, c2p, c2r, c2w)
            dve.sem_inc(b_split, 1)
            dve.wait_ge(xh_in, 32)
            v.tensor_tensor(t.x1[:, :, :], t.x1[:, :, :], h[:, :, :], ALU.add).then_inc(base_ready, 1)
            dve.wait_ge(base_ready, 1)

            def step(back):
                g = back(1)
                if g is not None:
                    dve.wait_ge(sig_ready, g.n + 1)
                    need(dve, down_done, g.n)
                    for m in range(2):
                        last = v.scalar_tensor_tensor(out=hid[:, m, :], in0=psU[:, m, :], scalar=c1c[:, m:m + 1],
                                                      in1=sg[:, m, :], op0=ALU.add, op1=ALU.mult)
                    last.then_inc(hid_ready, 1)
                g = back(2)
                if g is not None:
                    one = lambda a: a.rearrange("p (o d) -> p o d", o=1)
                    x1 = t.x1[:, bass.ds(g.n, 1), :]
                    dve.wait_ge(down_done, g.n + 1)
                    need(dve, x1_ready, g.n)
                    v.tensor_tensor(x1, x1, one(psV[0:P, 0:D]), ALU.add).then_inc(x1_ready, 1)
                g = back(3)
                if g is not None:
                    if isinstance(g.n, int) and g.n == NT - 1:
                        dve.wait_ge(x1_ready, NT)
                    v.bn_stats(t.moments[:, bass.ds(g.n, 1), :].rearrange("p o d -> p (o d)"),
                               t.x1[:, bass.ds(g.n, 1), :].rearrange("p o d -> p (o d)")).then_inc(stats_ready, 1)

            pipeline(dve, NT, DEPTH + 1, step)
            dve.wait_ge(stats_ready, NT)


def node_input(nc, t, y_dram, Win, bin_):
    with ExitStack() as ctx:
        sb = lambda n, s, d: ctx.enter_context(nc.sbuf_tensor(n, s, d))
        pb = lambda n, s: ctx.enter_context(nc.psum_tensor(n, s, FP32))
        sem = lambda n: ctx.enter_context(nc.semaphore(n))
        wi = sb("wi", [128, 2, D], FP32)
        bir = sb("bir", [3, D], FP32)
        biw = sb("biw", [3, 3, D], FP32)
        bip = sb("bip", [3, D], BF16)
        mv = sb("mv2", [P, NT, 2], FP32)
        rstd = sb("rstd2", [P, NT], FP32)
        nmr = sb("nmr2", [P, NT], FP32)
        h2 = sb("h2", [P, 2, CH, D], FP32)
        hT = sb("hT", [128, 2, 2 * CH * P], FP32)
        sg = sb("sgi", [P, CH, D], FP32)
        y = sb("y", [P, NT, D], FP32)
        big = sb("big", [128, 4], FP32)
        psT = pb("psT2", [128, 3, 512])
        psY = pb("psY", [128, 3, 512])
        names = ["w_in", "b_split", "chain", "var_ready", "std_ready", "norm_ready", "h_ready", "turned", "copied", "in_done",
                 "sig_ready", "y_ready", "max_ready", "max_all", "scaled", "stored"]
        (w_in, b_split, chain, var_ready, std_ready, norm_ready, h_ready, turned_, copied, in_done,
         sig_ready, y_ready, max_ready, max_all, scaled, stored) = (sem("i_" + n) for n in names)
        DEPTH = 1
        block = ctx.enter_context(nc.Block())

        @block.sync
        def _(sp):
            sp.dma_start(wi[:, :, :], Win.rearrange("(m p) n -> p m n", p=128)).then_inc(w_in, 16)
            for r in range(3):
                sp.dma_start(bir[r:r + 1, :], bin_.rearrange("(o n) -> o n", o=1)).then_inc(w_in, 16)
            sp.wait_ge(scaled, 1)
            sp.dma_start(y_dram.rearrange("(n p) d -> p n d", p=P), y[:, :, :]).then_inc(stored, 16)
            sp.wait_ge(stored, 16)

        @block.gpsimd
        def _(pool):
            pool.memset(big[:, :], 0.0).then_inc(max_all, 1)
            pool.wait_ge(max_ready, 1)
            pool.partition_all_reduce(big[:, 1:2], big[:, 0:1], 128, bass.bass_isa.ReduceOp.max).then_inc(max_all, 1)
            pool.wait_ge(max_all, 2)

        @block.tensor
        def _(pe):
            def step(back):
                g = back(0)
                if g is not None:
                    pe.wait_ge(h_ready, g.n + 1)
                    need(pe, copied, g.n)
                    turn_chunk(nc, psT, h2[:, g.slot, :, :], t.ident).then_inc(turned_, 1)
                g = back(1)
                if g is not None:
                    if isinstance(g.n, int) and g.n == 0:
                        pe.wait_ge(w_in, 4 * 16)
                        pe.wait_ge(b_split, 1)
                    pe.wait_ge(copied, g.n + 1)
                    need(pe, y_ready, g.n)
                    multiply_chunk(nc, psY, hT[:, g.slot, :], wi, t.ones_h, bip).then_inc(in_done, 1)

            pipeline(pe, NCHUNK, DEPTH, step)

        @block.scalar
        def _(act):
            act.wait_ge(var_ready, 1)
            nc.scalar.activation(rstd[:, :], nmr[:, :], ACT.Sqrt).then_inc(std_ready, 1)
            act.wait_ge(norm_ready, 1)

            def step(back):
                g = back(0)
                if g is not None:
                    need(act, turned_, g.n - 1)
                    for n in range(CH):
                        at = bass.ds(g.n * CH + n, 1)
                        last = nc.scalar.activation(h2[:, g.slot, n, :], t.x1[:, at, :].rearrange("p o d -> p (o d)"), ACT.Relu,
                                                    bias=nmr[:, at], scale=rstd[:, at])
                    last.then_inc(h_ready, 1)
                g = back(1)
                if g is not None:
                    act.wait_ge(in_done, g.n + 1)
                    need(act, y_ready, g.n)
                    for of, to in products(psY, sg[:, :, :]):
                        last = nc.scalar.activation(to, of, ACT.Sigmoid)
                    last.then_inc(sig_ready, 1)

            pipeline(act, NCHUNK, DEPTH, step)

        @block.vector
        def _(dve):
            link = Link(dve, chain)
            v = nc.vector
            for n in range(NT):
                last = v.bn_aggr(mv[:, n, :], t.moments[:, n, :])
            link(last)
            link(v.tensor_scalar(rstd[:, :], mv[:, :, 1], EPS, None, ALU.add))
            v.reciprocal(nmr[:, :], rstd[:, :]).then_inc(var_ready, 1)
            dve.wait_ge(std_ready, 1)
            v.scalar_tensor_tensor(out=nmr[:, :], in0=mv[:, :, 0], scalar=-1.0, in1=rstd[:, :],
                                   op0=ALU.mult, op1=ALU.mult).then_inc(norm_ready, 1)
            dve.wait_ge(w_in, 4 * 16)
            split_row(nc, link, t, bip, bir, biw)
            dve.sem_inc(b_split, 1)

            def step(back):
                g = back(0)
                if g is not None:
                    dve.wait_ge(turned_, g.n + 1)
                    need(dve, in_done, g.n - 1)
                    for of, to in turned(psT, hT[:, g.slot, :]):
                        last = v.tensor_copy(to, of)
                    last.then_inc(copied, 1)
                g = back(1)
                if g is not None:
                    dve.wait_ge(sig_ready, g.n + 1)
                    of_chunk = y[:, bass.ds(g.n * CH, CH), :]
                    for (of, gate), (_, to) in zip(products(psY, sg[:, :, :]), products(psY, of_chunk)):
                        last = v.tensor_tensor(to, of, gate, ALU.mult)
                    last.then_inc(y_ready, 1)

            pipeline(dve, NCHUNK, DEPTH, step)
            dve.wait_ge(y_ready, NCHUNK)
            dve.wait_ge(max_all, 1)
            link(v.tensor_reduce(big[0:P, 0:1], y[:, :, :], AX.XY, ALU.max, apply_absolute_value=True))
            v.tensor_scalar(big[0:P, 0:1], big[0:P, 0:1], 2.0 ** -100, 2.0 ** 100, ALU.max, ALU.min).then_inc(max_ready, 1)
            dve.wait_ge(max_all, 2)
            bits = lambda c: big[:, c:c + 1].bitcast(I32)
            link(v.tensor_scalar(bits(2), bits(1), 0x7F800000, None, ALU.bitwise_and))
            link(v.tensor_scalar(t.scale[:, 0:1].bitcast(I32), bits(2), -1.0, float((254 + 13) << 23), ALU.mult, ALU.add))
            link(v.tensor_scalar(t.scale[:, 1:2].bitcast(I32), bits(2), float(13 << 23), None, ALU.subtract))
            v.tensor_scalar(y[:, :, :], y[:, :, :], t.scale[0:P, 0:1], None, ALU.mult).then_inc(scaled, 1)


PIECE = 500
NPIECE = -(-N_NODES // PIECE)


def count_edges(nc, t):
    with ExitStack() as ctx:
        sb = lambda n, s, d: ctx.enter_context(nc.sbuf_tensor(n, s, d))
        sem = lambda n: ctx.enter_context(nc.semaphore(n))
        NE = NG * GW
        key = sb("key", [128, NE], FP32)
        part = sb("part", [128, NE], FP32)
        ok = sb("ok", [128, NE], FP32)
        mid = N_NODES // 2
        cols_h = sb("cols_h", [128, N_NODES], FP16)
        hot_part = sb("hot_part", [128, 2, GW, 128], FP16)
        hot_key = sb("hot_key", [128, 2, GW, N_NODES], FP16)
        ps = [ctx.enter_context(nc.psum_tensor(f"ps_count{i}", [128, 512], FP32)) for i in range(NPIECE)]
        chain, part_ready, key_ready, window_done, block_done, taken = (
            sem("c_" + n) for n in ("chain", "part_ready", "key_ready", "window_done", "block_done", "taken"))
        BY_ACT = 4
        taken_v, cols_made = sem("c_taken_v"), sem("c_cols_made")
        block = ctx.enter_context(nc.Block())
        width = lambda i: min(PIECE, N_NODES - i * PIECE)

        @block.gpsimd
        def _(pool):
            pool.memset(t.counts[:, NT * N_NODES:NT * N_NODES + 8], 0.0)
            pool.iota(cols_h[:, :], pattern=[[1, N_NODES]], base=-mid, channel_multiplier=0,
                      allow_small_or_imprecise_dtypes=True).then_inc(cols_made, 1)

        @block.tensor
        def _(pe):
            def multiply(g, j, opens):
                for i in range(NPIECE):
                    if opens and j == 0:
                        if i < BY_ACT:
                            need(pe, taken, g.n * BY_ACT - BY_ACT + 1 + i)
                        else:
                            need(pe, taken_v, g.n * (NPIECE - BY_ACT) - (NPIECE - BY_ACT) + 1 + i - BY_ACT)
                    last = nc.tensor.matmul(ps[i][:, 0:width(i)], hot_part[:, g.slot, j, :],
                                            hot_key[:, g.slot, j, i * PIECE:i * PIECE + width(i)],
                                            start=opens and j == 0, stop=False, skip_group_check=True)
                    if j == GW - 1:
                        last.then_inc(block_done, 1)
                last.then_inc(window_done, 1) if j < GW - 1 else None

            def step(back):
                g = back(0)
                if g is None:
                    return
                for j in range(GW):
                    pe.wait_ge(key_ready, g.n * GW + j + 1)
                    if j == 0:
                        pe.wait_ge(part_ready, g.n + 1)
                        opens = pe.value_load(t.opens[0:1, bass.ds(g.n, 1)], min_val=0, max_val=1)
                        with pe.If(opens > 0):
                            multiply(g, j, True)
                        with pe.Else():
                            multiply(g, j, False)
                    else:
                        multiply(g, j, False)

            pipeline(pe, NG, 0, step)

        def take(eng, g, pieces, done, move):
            b = eng.value_load(t.group_bucket_i[0:1, bass.ds(g.n, 1)], min_val=0, max_val=NT - 1)
            closes = eng.value_load(t.closes[0:1, bass.ds(g.n, 1)], min_val=0, max_val=1)
            with eng.If(closes > 0):
                for i in pieces:
                    eng.wait_ge(block_done, g.n * NPIECE + i + 1)
                    move(t.counts[0:P, bass.ds(b * N_NODES + i * PIECE, width(i))], ps[i][0:P, 0:width(i)]).then_inc(done, 1)
            with eng.Else():
                eng.wait_ge(block_done, (g.n + 1) * NPIECE)
                eng.sem_inc(done, len(pieces))

        @block.scalar
        def _(act):
            def step(back):
                g = back(0)
                if g is not None:
                    take(act, g, range(BY_ACT), taken, nc.scalar.copy)

            pipeline(act, NG, 1, step)
            act.wait_ge(taken, NG * BY_ACT)

        @block.vector
        def _(dve):
            link = Link(dve, chain)
            v = nc.vector
            link(v.tensor_scalar(key[:, :], t.src_of[:, :], -float(P // 2), 1.0 / P, ALU.add, ALU.mult))
            link(v.tensor_scalar(key[:, :], key[:, :], MAGIC, None, ALU.add))
            link(v.tensor_scalar(key[:, :], key[:, :], MAGIC, None, ALU.subtract))
            link(v.tensor_scalar(key[:, :], key[:, :], float(P), None, ALU.mult))
            link(v.tensor_tensor(part[:, :], t.src_of[:, :], key[:, :], ALU.subtract))
            link(v.tensor_scalar(ok[:, :], t.local_of[:, :], 0.0, None, ALU.is_ge))
            link(v.scalar_tensor_tensor(out=ok[:, :], in0=t.local_of[:, :], scalar=float(P), in1=ok[:, :],
                                        op0=ALU.is_lt, op1=ALU.mult))
            link(v.scalar_tensor_tensor(out=key[:, :], in0=key[:, :], scalar=1.0, in1=t.local_of[:, :],
                                        op0=ALU.add, op1=ALU.add))
            link(v.tensor_tensor(key[:, :], key[:, :], ok[:, :], ALU.mult))
            link(v.tensor_scalar(key[:, :], key[:, :], 1.0 + mid, None, ALU.subtract))
            dve.wait_ge(cols_made, 1)

            def step(back):
                g, before = back(0), back(1)
                if g is not None:
                    need(dve, block_done, (g.n - 1) * NPIECE)
                    for j in range(GW):
                        last = v.tensor_scalar(hot_part[:, g.slot, j, :], t.cols[:, 0:128], part[:, bass.ds(g.n * GW + j, 1)],
                                               None, ALU.is_equal)
                    last.then_inc(part_ready, 1)
                    for j in range(GW):
                        v.tensor_scalar(hot_key[:, g.slot, j, :], cols_h[:, :], key[:, bass.ds(g.n * GW + j, 1)],
                                        None, ALU.is_equal).then_inc(key_ready, 1)
                if before is not None:
                    take(dve, before, range(BY_ACT, NPIECE), taken_v, v.tensor_copy)

            pipeline(dve, NG, 1, step)
            dve.wait_ge(taken_v, NG * (NPIECE - BY_ACT))


def degrees(nc, t):
    with ExitStack() as ctx:
        inv = ctx.enter_context(nc.sbuf_tensor("inv", [P, NT], FP32))
        chain = ctx.enter_context(nc.semaphore("d_chain"))
        block = ctx.enter_context(nc.Block())

        @block.vector
        def _(dve):
            link = Link(dve, chain)
            v = nc.vector
            link(v.tensor_scalar(inv[:, :], t.sums[:, :, D], 1.0 / MSG_SCALE, 1.0, ALU.mult, ALU.max))
            for i in range(NSTEPS):
                link(v.tensor_scalar(t.inv_deg[:, 1, i, :], inv[:, :], float(i + 1), None, ALU.mult))
                link(v.reciprocal(t.inv_deg[:, 0, i, :], t.inv_deg[:, 1, i, :]))
                link(v.tensor_scalar(t.inv_deg[:, 1, i, :], t.inv_deg[:, 0, i, :], 1.0 / LOW, None, ALU.mult))


def diffusion(nc, t, y_dram, d_dram):
    with ExitStack() as ctx:
        sb = lambda n, s, d: ctx.enter_context(nc.sbuf_tensor(n, s, d))
        sem = lambda n: ctx.enter_context(nc.semaphore(n))
        term = [sb(f"term{i}", [P, NT, 2 * HALF], FP16) for i in range(2)]
        acc = sb("acc", [P, NT, HALF], FP32)
        SL = 5
        low = sb("low_sum", [P, SL, HALF], FP32)
        rest = low
        val = sb("val", [P, SL, HALF], FP32)
        ps = [ctx.enter_context(nc.psum_tensor(f"ps_term{i}", [128, 512], FP32)) for i in range(SL)]
        names = ["chain", "y_in", "product", "low_ready", "val_ready", "high_ready", "rest_ready", "term_ready", "acc_ready", "stored"]
        chain, y_in, product, low_ready, val_ready, high_ready, rest_ready, term_ready, acc_ready, stored = (
            sem("f_" + n) for n in names)
        y_v = y_dram.rearrange("(n p) (c d) -> c p n d", p=P, c=2)
        d_v = d_dram.rearrange("(n p) (c d) -> c p n d", p=P, c=2)
        PER = NT * NSTEPS
        PAIRS = NSTEPS // 2
        one = lambda a: a.rearrange("p (o d) -> p o d", o=1)
        block = ctx.enter_context(nc.Block())

        def steps(eng, do):
            for c in range(2):
                for i in range(NSTEPS):
                    at = (c * NSTEPS + i) * NT
                    for n in range(SL):
                        do(c, i, Turn(0, n, SL), at)
                    with eng.Fori(1, NT // SL) as k:
                        for n in range(SL):
                            do(c, i, Turn(k, n, SL), at)

        @block.sync
        def _(sp):
            for c in range(2):
                if c:
                    sp.wait_ge(stored, 16)
                sp.dma_start(acc[:, :, :], y_v[c]).then_inc(y_in, 16)
                sp.wait_ge(acc_ready, (c + 1) * PER)
                sp.dma_start(d_v[c], acc[:, :, :]).then_inc(stored, 16)
            sp.wait_ge(stored, 32)

        @block.tensor
        def _(pe):
            with pe.Fori(0, 2 * PAIRS) as r:
                for odd in range(2):
                    for n in range(NT):
                        m = odd * NT + n
                        if m >= SL:
                            pe.wait_ge(val_ready, r * (2 * NT) + (m - SL + 1))
                        for k in range(NT):
                            if n == 0 and (k == 0 or k > NT - SL):
                                pe.wait_ge(term_ready, r * (2 * NT) + (m + max(k, NT - SL) + 1))
                            last = nc.tensor.matmul(ps[m % SL][:, 0:2 * HALF],
                                                    t.counts[0:P, n * N_NODES + k * P:n * N_NODES + k * P + 128],
                                                    term[odd][:, k, :], start=(k == 0), stop=(k == NT - 1))
                        last.then_inc(product, 1)

        @block.scalar
        def _(act):
            def do(c, i, g, at):
                n = g.n + at
                q = g.slot
                act.wait_ge(product, n + 1)
                need(act, val_ready, n - SL + 1)
                nc.scalar.activation(low[:, q, :], ps[q][0:P, HALF:2 * HALF], ACT.Copy,
                                     scale=t.inv_deg[:, 1, i, bass.ds(g.n, 1)]).then_inc(low_ready, 1)
                if i < NSTEPS - 1:
                    made = term[(i + 1) % 2]
                    act.wait_ge(val_ready, n + 1)
                    nc.scalar.copy(made[:, bass.ds(g.n, 1), 0:HALF], one(val[:, q, :])).then_inc(high_ready, 1)
                    act.wait_ge(rest_ready, n - c * NT + 1)
                    nc.scalar.mul(made[:, bass.ds(g.n, 1), HALF:2 * HALF], one(rest[:, q, :]), LOW).then_inc(term_ready, 1)

            steps(act, do)

        @block.vector
        def _(dve):
            link = Link(dve, chain)
            v = nc.vector

            def split_y(c):
                dve.wait_ge(y_in, 16 * (c + 1))
                if c:
                    dve.wait_ge(product, PER)
                    dve.wait_ge(term_ready, PER)
                link(v.tensor_copy(term[0][:, :, 0:HALF], acc[:, :, :]))
                link(v.tensor_tensor(term[1][:, :, :].bitcast(FP32), acc[:, :, :], term[0][:, :, 0:HALF], ALU.subtract))
                v.tensor_scalar(term[0][:, :, HALF:2 * HALF], term[1][:, :, :].bitcast(FP32), LOW, None,
                                ALU.mult).then_inc(term_ready, NT)
                dve.wait_ge(term_ready, c * PER + NT)

            def do(c, i, g, at):
                if i == 0 and isinstance(g.n, int) and g.n == 0:
                    split_y(c)
                n = g.n + at
                q = g.slot
                dve.wait_ge(low_ready, n + 1)
                if not isinstance(n, int) or n >= SL:
                    dve.wait_ge(acc_ready, n - SL + 1)
                v.scalar_tensor_tensor(out=val[:, q, :], in0=ps[q][0:P, 0:HALF], scalar=t.inv_deg[:, 0, i, bass.ds(g.n, 1)],
                                       in1=low[:, q, :], op0=ALU.mult, op1=ALU.add).then_inc(val_ready, 1)
                if i < NSTEPS - 1:
                    dve.wait_ge(high_ready, n - c * NT + 1)
                    v.tensor_tensor(rest[:, q, :], val[:, q, :], term[(i + 1) % 2][:, bass.ds(g.n, 1), 0:HALF].rearrange("p o d -> p (o d)"),
                                    ALU.subtract).then_inc(rest_ready, 1)
                else:
                    dve.wait_ge(val_ready, n + 1)
                a = acc[:, bass.ds(g.n, 1), :]
                v.tensor_tensor(a, a, one(val[:, q, :]), ALU.add).then_inc(acc_ready, 1)

            steps(dve, do)
            dve.wait_ge(acc_ready, 2 * PER)


CH = 5
NCHUNK = NT // CH


def turn_chunk(nc, psT, src, ident):
    for u in range(2 * CH):
        last = nc.tensor.transpose(psT[:, u // 4, (u % 4) * P:(u % 4 + 1) * P],
                                   src[:, u // 2, (u % 2) * 128:(u % 2 + 1) * 128], ident[0:P, 0:P])
    return last


def turned(psT, out):
    full = 2 * CH // 4
    return [(psT[:, 0:full, 0:4 * P], out[:, 0:full * 4 * P].rearrange("p (b c) -> p b c", b=full)),
            (psT[:, full, 0:(2 * CH - 4 * full) * P], out[:, full * 4 * P:2 * CH * P])]


def multiply_chunk(nc, psO, xT, w, ones, bias_parts):
    for n in range(CH):
        to = psO[0:P, n // 2, (n % 2) * D:(n % 2 + 1) * D]
        for m in range(2):
            u = 2 * n + m
            nc.tensor.matmul(to, xT[:, u * P:(u + 1) * P], w[:, m, :], start=(m == 0), stop=False)
        last = nc.tensor.matmul(to, ones[0:3, 0:P], bias_parts[:, :], start=False, stop=True)
    return last


def products(psO, tiles):
    even = CH // 2
    return [(psO[0:P, 0:even, :].rearrange("p b (h d) -> p (b h) d", h=2), tiles[:, 0:2 * even, :]),
            (psO[0:P, even:even + 1, 0:D], tiles[:, 2 * even:CH, :])]


def node_output(nc, t, x1_dram, d_dram, Wout, bout, out):
    with ExitStack() as ctx:
        sb = lambda n, s, d: ctx.enter_context(nc.sbuf_tensor(n, s, d))
        pb = lambda n, s: ctx.enter_context(nc.psum_tensor(n, s, FP32))
        sem = lambda n: ctx.enter_context(nc.semaphore(n))
        wo = sb("wo", [128, 2, D], FP32)
        bor = sb("bor", [3, D], FP32)
        bow = sb("bow", [3, 3, D], FP32)
        bop = sb("bop", [3, D], BF16)
        d_tile = sb("d_tile", [P, 2, CH, D], FP32)
        x1 = sb("x1_tile", [P, 2, CH, D], FP32)
        dT = sb("dT", [128, 2, 2 * CH * P], FP32)
        res = sb("res", [P, 2, CH, D], FP32)
        psT = pb("psT3", [128, 3, 512])
        psO = pb("psO", [128, 3, 512])
        names = ["w_in", "b_split", "chain", "turned", "copied", "out_done", "res_ready"]
        w_in, b_split, chain, turned_, copied, out_done, res_ready = (sem("o_" + n) for n in names)
        d_in = [sem("d_in0"), sem("d_in1")]
        stored = [sem("out_stored0"), sem("out_stored1")]
        DEPTH = 1
        block = ctx.enter_context(nc.Block())
        rows = lambda a, g: a.rearrange("(c n p) d -> c p n d", n=CH, p=P)[bass.ds(g.n, 1)].rearrange("o p n d -> (o p) n d")

        @block.sync
        def _(sp):
            sp.dma_start(wo[:, :, :], Wout.rearrange("(m p) n -> p m n", p=128)).then_inc(w_in, 16)
            for r in range(3):
                sp.dma_start(bor[r:r + 1, :], bout.rearrange("(o n) -> o n", o=1)).then_inc(w_in, 16)

            def step(back):
                g = back(0)
                if g is not None:
                    need(sp, res_ready, g.n - 1)
                    need(sp, turned_, g.n - 1)
                    sp.dma_start(d_tile[:, g.slot, :, :], rows(d_dram, g)).then_inc(d_in[g.slot], 16)
                    sp.dma_start(x1[:, g.slot, :, :], rows(x1_dram, g)).then_inc(d_in[g.slot], 16)
                g = back(1)
                if g is not None:
                    sp.wait_ge(res_ready, g.n + 1)
                    sp.dma_start(rows(out, g), res[:, g.slot, :, :]).then_inc(stored[g.slot], 16)

            pipeline(sp, NCHUNK, DEPTH, step)
            sp.wait_ge(stored[0], 16 * ((NCHUNK + 1) // 2))
            sp.wait_ge(stored[1], 16 * (NCHUNK // 2))

        @block.tensor
        def _(pe):
            def step(back):
                g = back(0)
                if g is not None:
                    pe.wait_ge(d_in[g.slot], g.half * 32 + 32)
                    need(pe, copied, g.n)
                    turn_chunk(nc, psT, d_tile[:, g.slot, :, :], t.ident).then_inc(turned_, 1)
                g = back(1)
                if g is not None:
                    if isinstance(g.n, int) and g.n == 0:
                        pe.wait_ge(w_in, 4 * 16)
                        pe.wait_ge(b_split, 1)
                    pe.wait_ge(copied, g.n + 1)
                    need(pe, res_ready, g.n)
                    multiply_chunk(nc, psO, dT[:, g.slot, :], wo, t.ones_h, bop).then_inc(out_done, 1)

            pipeline(pe, NCHUNK, DEPTH, step)

        @block.scalar
        def _(act):
            def step(back):
                g = back(0)
                if g is not None:
                    act.wait_ge(turned_, g.n + 1)
                    need(act, out_done, g.n - 1)
                    for of, to in turned(psT, dT[:, g.slot, :]):
                        last = nc.scalar.activation(to, of, ACT.Copy, scale=t.scale[:, 1:2])
                    last.then_inc(copied, 1)

            pipeline(act, NCHUNK, DEPTH, step)

        @block.vector
        def _(dve):
            link = Link(dve, chain)
            dve.wait_ge(w_in, 4 * 16)
            split_row(nc, link, t, bop, bor, bow)
            dve.sem_inc(b_split, 1)

            def step(back):
                g = back(1)
                if g is not None:
                    dve.wait_ge(out_done, g.n + 1)
                    dve.wait_ge(d_in[g.slot], g.half * 32 + 32)
                    need(dve, stored[g.slot], g.half * 16)
                    for (of, old), (_, to) in zip(products(psO, x1[:, g.slot, :, :]), products(psO, res[:, g.slot, :, :])):
                        last = nc.vector.tensor_tensor(to, old, of, ALU.add)
                    last.then_inc(res_ready, 1)

            pipeline(dve, NCHUNK, DEPTH, step)


class Tables:
    pass


def gnn_kernel(nc, x, src, dst, attr, W1, b1, W2, b2, U1, c1, U2, c2, Win, bin_, Wout, bout, out):
    dram = lambda n, s: nc.dram_tensor(n, s, FP32).ap()
    h_dram = dram("h_nodes", [N_NODES, D])
    in_order = (nc.dram_tensor("src_in_order", [N_EDGES], I32).ap(), nc.dram_tensor("dst_in_order", [N_EDGES], I32).ap(),
                dram("attr_in_order", [N_EDGES, R]))
    x1_dram = dram("x1_nodes", [N_NODES, D])
    y_dram = dram("y_nodes", [N_NODES, D])
    d_dram = dram("diffused", [N_NODES, D])
    t = Tables()
    with ExitStack() as ctx:
        keep = lambda scope: (lambda n, s, d: scope.enter_context(nc.sbuf_tensor(n, s, d)))
        sb = keep(ctx)
        t.ident = sb("ident", [128, 128], FP32)
        t.ones_h = sb("ones_h", [128, 128], BF16)
        t.gate_cell = sb("gate_cell", [1, 2], FP32)
        t.cols = sb("cols", [128, COLS], FP32)
        t.group_bucket_i = sb("group_bucket_i", [128, NG], I32)
        t.opens = sb("opens", [128, NG], I32)
        t.closes = sb("closes", [128, NG], I32)
        t.unsorted = sb("unsorted", [128, 1], I32)
        t.scale = sb("scale", [128, 2], FP32)
        t.inv_deg = sb("inv_deg", [P, 2, NSTEPS, NT], FP32)
        t.src_of = sb("src_of", [128, NG * GW], FP32)
        t.local_of = sb("local_of", [128, NG * GW], FP32)
        with ExitStack() as nodes:
            sb = keep(nodes)
            t.before = sb("before", [128, 128], FP32)
            t.ones = sb("ones", [128, 128], FP32)
            t.place_i = sb("place_i", [128, TG, GW], I32)
            t.place = sb("place", [128, TG, GW], FP32)
            t.group_row = sb("group_row", [128, NG], I32)
            t.group_bucket = sb("group_bucket", [128, NG], FP32)
            t.group_skip = sb("group_skip", [128, NG], FP32)
            t.bucket_node = sb("bucket_node", [128, NG], FP32)
            with ExitStack() as edges:
                sb = keep(edges)
                t.dst_i = sb("dst_i", [P, EC], I32)
                t.dst_f = sb("dst_f", [P, EC], FP32)
                t.bucket = sb("bucket", [P, EC], FP32)
                t.base = sb("base", [P, NT], FP32)
                t.cols_i = sb("cols_i", [128, COLS], I32)
                prepare(nc, t, x, src, dst, h_dram)
                edge_sort(nc, t, src, attr, in_order)
            t.sums = nodes.enter_context(nc.sbuf_tensor("sums", [P, NT, D + 1], FP32))
            edge_messages(nc, t, h_dram, src, dst, attr, in_order, W1, b1, W2, b2)
            t.moments = nodes.enter_context(nc.sbuf_tensor("moments", [P, NT, 6], FP32))
            t.x1 = nodes.enter_context(nc.sbuf_tensor("x1", [P, NT, D], FP32))
            degrees(nc, t)
            node_update(nc, t, x, h_dram, x1_dram, U1, c1, U2, c2)
            node_input(nc, t, y_dram, Win, bin_)
        with ExitStack() as graph:
            t.counts = graph.enter_context(nc.sbuf_tensor("counts", [128, NT * N_NODES + 8], FP16))
            count_edges(nc, t)
            diffusion(nc, t, y_dram, d_dram)
        node_output(nc, t, x1_dram, d_dram, Wout, bout, out)


_INS = ["x", "src", "dst", "edge_attr_64", "L0_gnn_W1", "L0_gnn_b1", "L0_gnn_W2", "L0_gnn_b2", "L0_gnn_U1", "L0_gnn_c1",
        "L0_gnn_U2", "L0_gnn_c2", "L1_gnn_W_in", "L1_gnn_b_in", "L1_gnn_W_out", "L1_gnn_b_out"]


def kernel(**inputs):
    import numpy as _np
    import concourse.bacc as _bacc
    from concourse import mybir as _mybir
    from concourse.bass_utils import run_bass_kernel_spmd as _run

    nc = _bacc.Bacc("TRN2", target_bir_lowering=False, num_devices=1)
    arrays, args = {}, []
    for name in _INS:
        a = _np.asarray(inputs[name])
        if name in ("L1_gnn_W_in", "L1_gnn_W_out"):
            a = a.T
        a = _np.ascontiguousarray(a)
        arrays[f"in_{name}"] = a
        args.append(nc.dram_tensor(f"in_{name}", a.shape, _mybir.dt.from_np(a.dtype), kind="ExternalInput").ap())
    args.append(nc.dram_tensor("out_0", (N_NODES, D), FP32, kind="ExternalOutput").ap())
    gnn_kernel(nc, *args)
    r = _run(nc, [arrays], core_ids=[0])
    return r.results[0]["out_0"]
```

```python
import concourse.bass as bass
from concourse import mybir
from contextlib import ExitStack

FP32 = mybir.dt.float32
FP16 = mybir.dt.float16
BF16 = mybir.dt.bfloat16
I32 = mybir.dt.int32
U32 = mybir.dt.uint32
ALU = mybir.AluOpType
ACT = mybir.ActivationFunctionType
AX = mybir.AxisListType

N_NODES = 3125
N_EDGES = 53125
D = 256
R = 64
P = 125
NT = N_NODES // P
EC = N_EDGES // P
NSTEPS = 6
EPS = 1e-5

WIN = 128
GW = 2
GRP = WIN * GW
NG = (N_EDGES + NT * (GRP - 1)) // GRP
NG += NG % 2
TG = 2
TURNS = NG // TG
NW = TG * GW
CHK = 114
SLOT = 25
NCH = EC // SLOT
Q = 25
NPATCH = N_NODES // Q
PPB = P // Q
PW = 4
KEYS = NT * Q
MAGIC = 1.5 * 2.0 ** 23
HALF = D // 2
MSG_SCALE = 1024.0
COLS = 256
CH = 5
NCHUNK = NT // CH
LOW = 2048.0


class Link:

    def __init__(self, eng, sem):
        self.eng, self.sem, self.n = eng, sem, 0

    def __call__(self, ins):
        self.n += 1
        ins.then_inc(self.sem, 1)
        self.eng.wait_ge(self.sem, self.n)


def prepare(nc, t, x, src, dst, h_dram):
    with ExitStack() as ctx:
        sb = lambda n, s, d: ctx.enter_context(nc.sbuf_tensor(n, s, d))
        sem = lambda n: ctx.enter_context(nc.semaphore(n))
        xs = sb("xs", [P, NT, D], FP32)
        hs = sb("hs", [P, NT, D], FP32)
        stats = sb("stats", [P, NT, 6], FP32)
        mv = sb("mv", [P, NT, 2], FP32)
        rstd = sb("rstd", [P, NT], FP32)
        nmr = sb("nmr", [P, NT], FP32)
        here = sb("here", [CHK, (N_EDGES - 1) // CHK], I32)
        after = sb("after", [CHK, (N_EDGES - 1) // CHK], I32)
        falls = sb("falls", [CHK, 1], FP32)
        fell = sb("fell", [CHK, (N_EDGES - 1) // CHK], FP32)
        bucket = sb("bucket", [P, EC], FP32)
        bucket_h = sb("bucket_h", [P, EC], FP16)
        hot = sb("hot", [P, NT, EC], FP16)
        pick = sb("pick", [P, 2 * NT - 1], FP16)
        tab = sb("tab", [NT, 4], FP32)
        tot, groups, end, room = (tab[:, i:i + 1] for i in range(4))
        passed = sb("passed_ends", [NT, 2, NG], FP32)
        row_f = sb("row_f", [128, 2, NG], FP32)
        ps_hot, ps, ps_row = (ctx.enter_context(nc.psum_tensor(n, [128, 512], FP32)) for n in ("ps_hot", "ps_sort", "ps_row"))
        made, chain, var_ready, std_ready, norm_ready, h_ready, h_out = (
            sem(n) for n in ("made", "prep_chain", "var_ready", "std_ready", "norm_ready", "h_ready", "h_out"))
        ids_in, next_in, hot_made, histogram, falls_ready, groups_ready, ends_set, passed_ready, rows_set = (
            sem(n) for n in ("ids_in", "next_in", "hot_made", "histogram", "falls_ready", "groups_ready", "ends_set",
                             "passed_ready", "rows_set"))
        XC = 5
        x_in = [sem(f"x_in{c}") for c in range(NT // XC)]
        block = ctx.enter_context(nc.Block())

        @block.sync
        def _(sp):
            sp.dma_start(t.dst_i[:, :], dst.rearrange("(p c) -> p c", p=P)).then_inc(ids_in, 16)
            sp.dma_start(here[:, :], dst[0:N_EDGES - 1].rearrange("(p c) -> p c", p=CHK)).then_inc(next_in, 16)
            sp.dma_start(after[:, :], dst[1:N_EDGES].rearrange("(p c) -> p c", p=CHK)).then_inc(next_in, 16)
            x_v = x.rearrange("(n p) d -> p n d", p=P)
            for c in range(NT // XC):
                sp.dma_start(xs[:, c * XC:(c + 1) * XC, :], x_v[:, c * XC:(c + 1) * XC, :]).then_inc(x_in[c], 16)
            h_v = h_dram.rearrange("(n p) d -> p n d", p=P)
            for c in range(NT // XC):
                sp.wait_ge(h_ready, c + 1)
                sp.dma_start(h_v[:, c * XC:(c + 1) * XC, :], hs[:, c * XC:(c + 1) * XC, :]).then_inc(h_out, 16)
            sp.wait_ge(h_out, 16 * (NT // XC))

        @block.gpsimd
        def _(pool):
            pool.iota(t.cols_i[:, :], pattern=[[1, COLS]], base=0, channel_multiplier=0).then_inc(made, 1)
            pool.wait_ge(made, 1)
            pool.tensor_copy(t.cols[:, :], t.cols_i[:, :]).then_inc(made, 1)
            pool.memset(t.ident[:, :], 0.0).then_inc(made, 1)
            pool.memset(t.before[:, :], 1.0).then_inc(made, 1)
            pool.memset(t.ones[:, :], 1.0).then_inc(made, 1)
            pool.memset(t.ones_h[:, :], 1.0).then_inc(made, 1)
            pool.wait_ge(made, 6)
            pool.affine_select(out=t.ident[:, :], in_=t.ident[:, :], compare_op=ALU.not_equal, fill=1.0,
                               base=0, pattern=[[-1, 128]], channel_multiplier=1).then_inc(made, 1)
            pool.affine_select(out=t.before[:, :], in_=t.before[:, :], compare_op=ALU.is_gt, fill=0.0,
                               base=0, pattern=[[1, 128]], channel_multiplier=-1).then_inc(made, 1)
            pool.iota(t.place_i[:, :, :], pattern=[[0, TG], [1, GW]], base=0, channel_multiplier=GW).then_inc(made, 1)
            pool.wait_ge(made, 9)
            pool.tensor_copy(t.place[:, :, :], t.place_i[:, :, :]).then_inc(made, 1)
            pool.wait_ge(made, 10)

        @block.tensor
        def _(pe):
            pe.wait_ge(made, 10)
            for b in range(NT):
                pe.wait_ge(hot_made, b + 2)
                last = nc.tensor.matmul(ps_hot[0:NT, 0:EC], pick[:, NT - 1 - b:2 * NT - 1 - b], hot[:, b, :],
                                        start=(b == 0), stop=(b == NT - 1))
            last.then_inc(histogram, 1)
            pe.wait_ge(falls_ready, 1)
            nc.tensor.matmul(ps[:, 8:9], t.ones[0:CHK, :], falls[:, :], start=True, stop=True)
            pe.wait_ge(groups_ready, 1)
            nc.tensor.matmul(ps[:, 0:1], t.before[0:NT, :], groups, start=True, stop=True).then_inc(ends_set, 1)
            pe.wait_ge(passed_ready, 1)
            nc.tensor.matmul(ps_row[:, 0:2 * NG], t.ones[0:NT - 1, :], passed[0:NT - 1, :, :].rearrange("p a g -> p (a g)"),
                             start=True, stop=True).then_inc(rows_set, 1)

        @block.scalar
        def _(act):
            act.wait_ge(var_ready, 1)
            nc.scalar.activation(rstd[:, :], nmr[:, :], ACT.Sqrt).then_inc(std_ready, 1)
            act.wait_ge(norm_ready, 1)
            for n in range(NT):
                last = nc.scalar.activation(hs[:, n, :], xs[:, n, :], ACT.Relu, bias=nmr[:, n:n + 1],
                                            scale=rstd[:, n:n + 1])
                if n % XC == XC - 1:
                    last.then_inc(h_ready, 1)

        @block.vector
        def _(dve):
            link = Link(dve, chain)
            v = nc.vector
            v.memset(pick[:, :], 0.0).then_inc(hot_made, 1)
            dve.wait_ge(hot_made, 1)
            link(v.memset(pick[:, NT - 1:NT], 1.0))
            dve.wait_ge(ids_in, 16)
            dve.wait_ge(made, 10)
            link(v.tensor_copy(t.dst_f[:, :], t.dst_i[:, :]))
            link(v.tensor_scalar(bucket[:, :], t.dst_f[:, :], -float(P // 2), 1.0 / P, ALU.add, ALU.mult))
            link(v.tensor_scalar(bucket[:, :], bucket[:, :], MAGIC, None, ALU.add))
            link(v.tensor_scalar(bucket_h[:, :], bucket[:, :], MAGIC, None, ALU.subtract))
            for b in range(NT):
                v.tensor_scalar(hot[:, b, :], bucket_h[:, :], float(b), None, ALU.is_equal).then_inc(hot_made, 1)
            dve.wait_ge(next_in, 32)
            link(v.tensor_tensor(fell[:, :], after[:, :], here[:, :], ALU.is_lt))
            v.tensor_reduce(falls[:, :], fell[:, :], AX.X, ALU.add).then_inc(falls_ready, 1)
            for n in range(NT):
                if n % XC == 0:
                    dve.wait_ge(x_in[n // XC], 16)
                last = v.bn_stats(stats[:, n, :], xs[:, n, :])
            link(last)
            for n in range(NT):
                last = v.bn_aggr(mv[:, n, :], stats[:, n, :])
            link(last)
            link(v.tensor_scalar(rstd[:, :], mv[:, :, 1], EPS, None, ALU.add))
            v.reciprocal(nmr[:, :], rstd[:, :]).then_inc(var_ready, 1)
            dve.wait_ge(std_ready, 1)
            v.scalar_tensor_tensor(out=nmr[:, :], in0=mv[:, :, 0], scalar=-1.0, in1=rstd[:, :],
                                   op0=ALU.mult, op1=ALU.mult).then_inc(norm_ready, 1)
            dve.wait_ge(histogram, 1)
            link(v.tensor_reduce(tot, ps_hot[0:NT, 0:EC], AX.X, ALU.add))
            link(v.tensor_scalar(groups, tot, GRP / 2 - 0.5, 1.0 / GRP, ALU.add, ALU.mult))
            link(v.tensor_scalar(groups, groups, MAGIC, None, ALU.add))
            v.tensor_scalar(groups, groups, MAGIC, None, ALU.subtract).then_inc(groups_ready, 1)
            dve.wait_ge(ends_set, 1)
            link(v.tensor_tensor(end, ps[0:NT, 0:1], groups, ALU.add))
            link(v.scalar_tensor_tensor(out=room, in0=groups, scalar=-float(GRP), in1=tot, op0=ALU.mult, op1=ALU.add))
            link(v.tensor_scalar(passed[:, 0, :], t.cols[0:NT, 0:NG], end, None, ALU.is_ge))
            v.tensor_scalar(passed[:, 1, :], t.cols[0:NT, 0:NG], end, room, ALU.is_ge, ALU.mult).then_inc(passed_ready, 1)
            link(v.tensor_copy(t.unsorted[:, :], ps[:, 8:9]))
            dve.wait_ge(rows_set, 1)
            link(v.tensor_copy(t.group_bucket[:, :], ps_row[:, 0:NG]))
            link(v.scalar_tensor_tensor(out=row_f[:, 0, :], in0=t.cols[:, 0:NG], scalar=float(GRP), in1=ps_row[:, NG:2 * NG],
                                        op0=ALU.mult, op1=ALU.add))
            link(v.tensor_scalar(row_f[:, 1, :], row_f[:, 0, :], float(N_EDGES - GRP), None, ALU.min))
            link(v.tensor_tensor(t.group_skip[:, :], row_f[:, 0, :], row_f[:, 1, :], ALU.subtract))
            link(v.tensor_copy(t.group_row[:, :], row_f[:, 1, :]))
            link(v.tensor_copy(t.group_bucket_i[:, :], t.group_bucket[:, :]))
            link(v.tensor_scalar(t.bucket_node[:, :], t.group_bucket[:, :], float(P), None, ALU.mult))


def edge_sort(nc, t, src, attr, in_order):
    with ExitStack() as ctx:
        sb = lambda n, s, d: ctx.enter_context(nc.sbuf_tensor(n, s, d))
        sem = lambda n: ctx.enter_context(nc.semaphore(n))
        src_i = sb("src_i", [P, EC], I32)
        patch = sb("patch", [P, EC], FP32)
        cnt = sb("patch_cnt", [P, NPATCH], FP32)
        base = sb("base", [P, NPATCH], FP32)
        first = sb("first", [128, 2, NPATCH], FP32)
        ps = ctx.enter_context(nc.psum_tensor("ps_rank", [128, 512], FP32))
        hot = sb("hot_rank", [P, EC], FP32)
        rank = sb("rank", [P, EC], FP32)
        pos = sb("pos", [P, EC], FP32)
        pos_i = sb("pos_i", [P, EC], I32)
        zeros = sb("zeros", [P, EC], FP32)
        attrs = sb("attrs", [P, 2, SLOT, R], FP32)
        slot_src = sb("slot_src", [P, 2, SLOT], I32)
        slot_dst = sb("slot_dst", [P, 2, SLOT], I32)
        slot_pos = sb("slot_pos", [P, 2, SLOT], I32)
        ids_in, chain, filled, passed, counted, totals = (
            sem("s_" + n) for n in ("ids_in", "chain", "filled", "passed", "counted", "totals"))
        attr_in = [sem("attr_in0"), sem("attr_in1")]
        scattered = [sem("scattered0"), sem("scattered1")]
        attr_v = attr.rearrange("(p c s) r -> p c s r", p=P, s=SLOT)
        SENT = 3 * 16 * SLOT
        HALVES = (NCH - 1) // 2
        block = ctx.enter_context(nc.Block())

        @block.sync
        def _(sp):
            def load(c, q, turn):
                if turn is not None:
                    sp.wait_ge(scattered[q], turn * SENT)
                sp.dma_start(attrs[:, q, :, :], attr_v[:, c, :, :]).then_inc(attr_in[q], 16)

            with sp.If(sp.value_load(t.unsorted[0:1, 0:1], min_val=0, max_val=N_EDGES) > 0):
                sp.dma_start(src_i[:, :], src.rearrange("(p c) -> p c", p=P)).then_inc(ids_in, 16)
                load(0, 0, None)
                load(1, 1, None)
                with sp.Fori(1, HALVES) as k:
                    load(2 * k, 0, k)
                    load(2 * k + 1, 1, k)
                load(NCH - 1, 0, HALVES)

        @block.gpsimd
        def _(pool):
            pool.memset(t.gate_cell[:, :], 0.0).then_inc(passed, 1)

            def scatter(q, turn):
                pool.wait_ge(filled, 2 * turn + q + 1)
                pool.wait_ge(passed, 2 * turn + q + 1)
                pool.tensor_tensor(t.gate_cell[:, 1:2], t.gate_cell[:, 0:1], t.gate_cell[:, 0:1], ALU.add).then_inc(passed, 1)
                for s in range(SLOT):
                    at = slot_pos[:, q, s:s + 1].bitcast(U32)
                    for to, what in zip(in_order, (slot_src[:, q, s:s + 1], slot_dst[:, q, s:s + 1], attrs[:, q, s, :])):
                        to = to if len(to.shape) == 2 else to.rearrange("(n o) -> n o", o=1)
                        pool.indirect_dma_start(out=to, out_offset=bass.IndirectOffsetOnAxis(ap=at, axis=0),
                                                in_=what, in_offset=None).then_inc(scattered[q], 16)

            with pool.If(pool.value_load(t.unsorted[0:1, 0:1], min_val=0, max_val=N_EDGES) > 0):
                with pool.Fori(0, HALVES) as k:
                    scatter(0, k)
                    scatter(1, k)
                scatter(0, HALVES)
                pool.wait_ge(scattered[0], (HALVES + 1) * SENT)
                pool.wait_ge(scattered[1], HALVES * SENT)

        @block.tensor
        def _(pe):
            with pe.If(pe.value_load(t.unsorted[0:1, 0:1], min_val=0, max_val=N_EDGES) > 0):
                pe.wait_ge(counted, 1)
                nc.tensor.matmul(ps[:, 0:NPATCH], t.before[0:P, :], cnt[:, :], start=True, stop=True)
                nc.tensor.matmul(ps[:, 128:128 + NPATCH], t.ones[0:P, :], cnt[:, :], start=True, stop=True).then_inc(totals, 1)

        @block.vector
        def _(dve):
            v = nc.vector

            def fill(c, q, turn, landed):
                dve.wait_ge(attr_in[q], landed)
                if turn is not None:
                    dve.wait_ge(scattered[q], turn * SENT)
                v.tensor_copy(slot_src[:, q, :], src_i[:, bass.ds(c * SLOT, SLOT)]).then_inc(chain, 1)
                v.tensor_copy(slot_dst[:, q, :], t.dst_i[:, bass.ds(c * SLOT, SLOT)]).then_inc(chain, 1)
                v.tensor_copy(slot_pos[:, q, :], pos_i[:, bass.ds(c * SLOT, SLOT)]).then_inc(filled, 1)

            with dve.If(dve.value_load(t.unsorted[0:1, 0:1], min_val=0, max_val=N_EDGES) > 0):
                link = Link(dve, chain)
                link(v.memset(zeros[:, :], 0.0))
                link(v.memset(pos[:, :], -1.0))
                link(v.tensor_scalar(patch[:, :], t.dst_f[:, :], -float(Q // 2), 1.0 / Q, ALU.add, ALU.mult))
                link(v.tensor_scalar(patch[:, :], patch[:, :], MAGIC, None, ALU.add))
                link(v.tensor_scalar(patch[:, :], patch[:, :], MAGIC, None, ALU.subtract))
                n1 = link.n
                with dve.Fori(0, NPATCH) as b:
                    v.tensor_scalar(hot[:, :], patch[:, :], t.cols[0:P, bass.ds(b, 1)], None, ALU.is_equal).then_inc(chain, 1)
                    dve.wait_ge(chain, b * 2 + (n1 + 1))
                    v.tensor_reduce(cnt[:, bass.ds(b, 1)], hot[:, :], AX.X, ALU.add).then_inc(chain, 1)
                    dve.wait_ge(chain, b * 2 + (n1 + 2))
                link.n = n1 + 2 * NPATCH
                dve.sem_inc(counted, 1)
                dve.wait_ge(totals, 1)
                link(v.tensor_copy(first[:, 1, :], ps[:, 128:128 + NPATCH]))
                link(v.tensor_tensor_scan(first[:, 0, :], t.ones[:, 0:NPATCH], first[:, 1, :], 0.0, ALU.mult, ALU.add))
                link(v.tensor_tensor(first[:, 0, :], first[:, 0, :], first[:, 1, :], ALU.subtract))
                link(v.tensor_tensor(base[:, :], ps[0:P, 0:NPATCH], first[0:P, 0, :], ALU.add))
                n2 = link.n
                with dve.Fori(0, NPATCH) as b:
                    v.tensor_scalar(hot[:, :], patch[:, :], t.cols[0:P, bass.ds(b, 1)], None, ALU.is_equal).then_inc(chain, 1)
                    dve.wait_ge(chain, b * 4 + (n2 + 1))
                    v.tensor_tensor_scan(rank[:, :], hot[:, :], zeros[:, :], base[:, bass.ds(b, 1)], ALU.add, ALU.add).then_inc(chain, 1)
                    dve.wait_ge(chain, b * 4 + (n2 + 2))
                    v.tensor_tensor(hot[:, :], hot[:, :], rank[:, :], ALU.mult).then_inc(chain, 1)
                    dve.wait_ge(chain, b * 4 + (n2 + 3))
                    v.tensor_tensor(pos[:, :], pos[:, :], hot[:, :], ALU.add).then_inc(chain, 1)
                    dve.wait_ge(chain, b * 4 + (n2 + 4))
                link.n = n2 + 4 * NPATCH
                link(v.tensor_copy(pos_i[:, :], pos[:, :]))
                dve.wait_ge(ids_in, 16)
                fill(0, 0, None, 16)
                fill(1, 1, None, 16)
                with dve.Fori(1, HALVES) as k:
                    fill(2 * k, 0, k, 16 * k + 16)
                    fill(2 * k + 1, 1, k, 16 * k + 16)
                fill(NCH - 1, 0, HALVES, 16 * HALVES + 16)
                dve.wait_ge(chain, link.n + 2 * NCH)


class Turn:

    def __init__(self, k, c, slots=2):
        self.n, self.half, self.slot = slots * k + c, k + c // slots, c % slots


def need(eng, sem, value):
    if not isinstance(value, int) or value > 0:
        eng.wait_ge(sem, value)


def pipeline(eng, count, depth, step):
    first = 2 * ((depth + 3) // 2)
    pairs = max(0, (count - first) // 2)

    def peeled(s):
        step(lambda d: Turn(0, s - d) if 0 <= s - d < count else None)

    for s in range(first):
        peeled(s)
    if pairs > 0:
        with eng.Fori(0, pairs) as k:
            for c in (first, first + 1):
                step(lambda d: Turn(k, c - d))
    for s in range(first + 2 * pairs, count + depth):
        peeled(s)


def split_row(nc, link, t, parts, row, work):
    v = nc.vector
    hi, rest = work[:, 0, :], work[:, 1, :]
    acc = work[:, 2, :]
    link(v.tensor_copy(parts[:, :], row[:, :]))
    link(v.tensor_copy(hi, parts[:, :]))
    link(v.tensor_scalar(acc, hi, t.ident[0:3, 0:1], None, ALU.mult))
    link(v.tensor_tensor(rest, row[:, :], hi, ALU.subtract))
    link(v.tensor_copy(parts[:, :], rest))
    link(v.tensor_copy(hi, parts[:, :]))
    link(v.scalar_tensor_tensor(out=acc, in0=hi, scalar=t.ident[0:3, 1:2], in1=acc, op0=ALU.mult, op1=ALU.add))
    link(v.tensor_tensor(rest, rest, hi, ALU.subtract))
    link(v.scalar_tensor_tensor(out=acc, in0=rest, scalar=t.ident[0:3, 2:3], in1=acc, op0=ALU.mult, op1=ALU.add))
    link(v.tensor_copy(parts[:, :], acc))


def edge_messages(nc, t, x, h_dram, src, dst, attr, in_order, W1, b1, W2, b2):
    with ExitStack() as ctx:
        sb = lambda n, s, d: ctx.enter_context(nc.sbuf_tensor(n, s, d))
        pb = lambda n, s: ctx.enter_context(nc.psum_tensor(n, s, FP32))
        sem = lambda n: ctx.enter_context(nc.semaphore(n))
        w1 = sb("w1", [2 * R, 2, D], FP32)
        w2 = sb("w2", [128, 2, D], FP32)
        b1c = sb("b1c", [128, 2], FP32)
        b2r = sb("b2r", [3, D], FP32)
        b2w = sb("b2w", [3, 3, D], FP32)
        b2p = sb("b2p", [3, D], BF16)
        at = sb("attr_tile", [128, 2, NW, R], FP32)
        ids = sb("ids_tile", [128, 2, 2, TG, GW], I32)
        src_i = sb("src_idx", [128, 2, NW], I32)
        skip = sb("skip", [128, 2, TG, GW], FP32)
        hg = sb("hg", [128, 2, NW, D], FP32)
        rT = sb("rT", [2 * R, 2, 2 * WIN], FP32)
        sg = sb("sg", [128, 2, 2, 2 * WIN], FP32)
        hid = sb("hid", [128, 2, 2, 2, 2 * WIN], FP32)
        gate = sb("gate", [128, NW, D], FP32)
        msg = sb("msg", [128, NW, D], FP32)
        msg_hi = sb("msg_hi", [128, 2, NW, D + 1], FP16)
        msg_lo = sb("msg_lo", [128, 2, NW, D], FP16)
        hot = sb("hot_dst", [128, 2, NW, P], FP16)
        psT = pb("psT", [128, 512])
        psH = pb("psH", [128, 2, 2, 2 * WIN])
        psG = pb("psG", [128, NW, D])
        psA = pb("psA", [128, TG, 512])
        names = ["w_in", "b_split", "chain", "turned", "copied", "up_done", "sig_ready", "hid_ready", "gate_done",
                 "gate_ready", "msg_ready", "high_ready", "low_ready", "ids_ready", "hot_ready", "sum_done", "sum_added", "passed"]
        (w_in, b_split, chain, turned, copied, up_done, sig_ready, hid_ready, gate_done,
         gate_ready, msg_ready, high_ready, low_ready, ids_ready, hot_ready, sum_done, sum_added, passed) = (sem("m_" + n) for n in names)
        rec_in = [sem("rec_in0"), sem("rec_in1")]
        ids_chain, w1_clear, xh_in = sem("ids_chain"), sem("w1_clear"), sem("xh_in")
        hg_in = [sem("hg_in0"), sem("hg_in1")]
        DEPTH = 4
        LOADS = 3 * TG * 16
        block = ctx.enter_context(nc.Block())

        @block.sync
        def _(sp):
            sp.wait_ge(w1_clear, 1)
            sp.dma_start(w1[0:R, 0, :], W1).then_inc(w_in, 16)
            sp.dma_start(w1[R:2 * R, 1, :], W1).then_inc(w_in, 16)
            sp.dma_start(w2[:, :, :], W2.rearrange("(m p) n -> p m n", p=128)).then_inc(w_in, 16)
            sp.dma_start(b1c[:, :], b1.rearrange("(m p) -> p m", p=128), allow_slow_non_contiguous=True).then_inc(w_in, 16)
            for r in range(3):
                sp.dma_start(b2r[r:r + 1, :], b2.rearrange("(o n) -> o n", o=1)).then_inc(w_in, 16)

            def loads(src, dst, attr):
                def step(back):
                    g = back(0)
                    if g is None:
                        return
                    need(sp, turned, g.n - 1)
                    need(sp, ids_ready, g.n - 1)
                    for u in range(TG):
                        row = sp.value_load(t.group_row[0:1, bass.ds(g.n * TG + u, 1)], min_val=0, max_val=N_EDGES - GRP)
                        rows = bass.ds(row, GRP)
                        pairs = lambda a: a[rows].rearrange("(p j) -> p j", j=GW)
                        sp.dma_start(ids[:, g.slot, 0, u, :], pairs(src)).then_inc(rec_in[g.slot], 16)
                        sp.dma_start(ids[:, g.slot, 1, u, :], pairs(dst)).then_inc(rec_in[g.slot], 16)
                        sp.dma_start(at[:, g.slot, u * GW:(u + 1) * GW, :],
                                     attr[rows, :].rearrange("(p j) c -> p j c", j=GW)).then_inc(rec_in[g.slot], 16)

                pipeline(sp, TURNS, DEPTH, step)

            with sp.If(sp.value_load(t.unsorted[0:1, 0:1], min_val=0, max_val=N_EDGES) > 0):
                loads(*in_order)
            with sp.Else():
                loads(src, dst, attr)

        @block.gpsimd
        def _(pool):
            pool.memset(t.gate_cell[:, :], 0.0).then_inc(passed, 1)

            def step(back):
                g = back(0)
                if g is None:
                    return
                need(pool, msg_ready, g.n - 1)
                pool.wait_ge(ids_ready, g.n + 1)
                pool.wait_ge(passed, g.n + 1)
                pool.tensor_tensor(t.gate_cell[:, 1:2], t.gate_cell[:, 0:1], t.gate_cell[:, 0:1], ALU.add).then_inc(passed, 1)
                for j in range(NW):
                    pool.indirect_dma_start(
                        out=hg[:, g.slot, j, :], out_offset=None, in_=h_dram[:, :],
                        in_offset=bass.IndirectOffsetOnAxis(ap=src_i[:, g.slot, j:j + 1].bitcast(U32), axis=0)
                    ).then_inc(hg_in[g.slot], 16)

            pipeline(pool, TURNS, DEPTH, step)

        @block.tensor
        def _(pe):
            pe.wait_ge(w_in, 7 * 16)
            pe.wait_ge(b_split, 1)

            def step(back):
                g = back(0)
                if g is not None:
                    pe.wait_ge(rec_in[g.slot], g.half * LOADS + LOADS)
                    need(pe, copied, g.n)
                    for pair in range(2):
                        last = nc.tensor.transpose(psT[:, pair * WIN:(pair + 1) * WIN],
                                                   at[:, g.slot, 2 * pair:2 * pair + 2, :].rearrange("p j r -> p (j r)"), t.ident[:, :])
                    last.then_inc(turned, 1)
                g = back(1)
                if g is not None:
                    pe.wait_ge(copied, g.n + 1)
                    need(pe, hid_ready, g.n)
                    for m in range(2):
                        for odd in range(2):
                            last = nc.tensor.matmul(psH[:, odd, m, :], w1[:, odd, m * 128:(m + 1) * 128],
                                                    rT[:, g.slot, :], start=True, stop=True)
                    last.then_inc(up_done, 1)
                g = back(2)
                if g is not None:
                    pe.wait_ge(hid_ready, g.n + 1)
                    need(pe, gate_ready, g.n)
                    for j in range(NW):
                        for m in range(2):
                            nc.tensor.matmul(psG[:, j, :], hid[:, g.slot, j % 2, m, j // 2 * WIN:(j // 2 + 1) * WIN], w2[:, m, :],
                                             start=(m == 0), stop=False)
                        last = nc.tensor.matmul(psG[:, j, :], t.ones_h[0:3, :], b2p[:, :], start=False, stop=True)
                    last.then_inc(gate_done, 1)
                g = back(4)
                if g is not None:
                    pe.wait_ge(high_ready, g.n + 1)
                    pe.wait_ge(low_ready, g.n + 1)
                    need(pe, sum_added, g.n * TG)
                    for u in range(TG):
                        for j in range(u * GW, (u + 1) * GW):
                            nc.tensor.matmul(psA[0:P, u, 0:D + 1], hot[:, g.slot, j, :], msg_hi[:, g.slot, j, :],
                                             start=(j == u * GW), stop=False)
                            last = nc.tensor.matmul(psA[0:P, u, 0:D], hot[:, g.slot, j, :], msg_lo[:, g.slot, j, :],
                                                    start=False, stop=(j == (u + 1) * GW - 1))
                        last.then_inc(sum_done, 1)

            pipeline(pe, TURNS, DEPTH, step)

        @block.scalar
        def _(act):
            act.wait_ge(w_in, 7 * 16)

            def step(back):
                g = back(3)
                if g is not None:
                    act.wait_ge(msg_ready, g.n + 1)
                    need(act, sum_done, (g.n - 1) * TG)
                    nc.scalar.mul(msg_hi[:, g.slot, :, 0:D], msg[:, :, :], MSG_SCALE).then_inc(high_ready, 1)
                g = back(0)
                if g is not None:
                    act.wait_ge(turned, g.n + 1)
                    need(act, up_done, g.n - 1)
                    nc.scalar.copy(rT[:, g.slot, :], psT[:, 0:2 * WIN]).then_inc(copied, 1)
                g = back(1)
                if g is not None:
                    act.wait_ge(up_done, g.n + 1)
                    need(act, hid_ready, g.n)
                    for m in range(2):
                        last = nc.scalar.activation(sg[:, :, m, :], psH[:, :, m, :], ACT.Sigmoid, bias=b1c[:, m:m + 1])
                    last.then_inc(sig_ready, 1)
                g = back(2)
                if g is not None:
                    act.wait_ge(gate_done, g.n + 1)
                    need(act, msg_ready, g.n)
                    nc.scalar.activation(gate[:, :, :], psG[:, :, :], ACT.Sigmoid).then_inc(gate_ready, 1)
                    if isinstance(g.n, int) and g.n in (2, 3):
                        to, of = ((t.x1, x), (t.h, h_dram))[g.n - 2]
                        act.dma_start(to[:, :, :], of.rearrange("(n p) d -> p n d", p=P)).then_inc(xh_in, 16)

            pipeline(act, TURNS, DEPTH, step)
            act.wait_ge(xh_in, 32)

        @block.vector
        def _(dve):
            link = Link(dve, chain)
            v = nc.vector
            v.memset(w1[:, :, :], 0.0).then_inc(w1_clear, 1)
            link(v.memset(t.sums[:, :, :], 0.0))
            link(v.memset(msg_hi[:, :, :, D:D + 1], MSG_SCALE))
            dve.wait_ge(w_in, 7 * 16)
            split_row(nc, link, t, b2p, b2r, b2w)
            dve.sem_inc(b_split, 1)

            def step(back):
                g = back(0)
                if g is not None:
                    dve.wait_ge(rec_in[g.slot], g.half * LOADS + LOADS)
                    need(dve, hg_in[g.slot], g.half * (16 * NW))
                    local = t.local_of[:, bass.ds(g.n * NW, NW)].rearrange("p (u j) -> p u j", u=TG)
                    of_group = lambda a: a[:, bass.ds(g.n * TG, TG)].rearrange("p (u o) -> p u o", o=1).to_broadcast([128, TG, GW])
                    v.tensor_tensor(skip[:, g.slot, :, :], t.place[:, :, :], of_group(t.group_skip), ALU.is_lt).then_inc(ids_chain, 1)
                    v.tensor_tensor(local, ids[:, g.slot, 1, :, :], of_group(t.bucket_node), ALU.subtract).then_inc(ids_chain, 1)
                    now = ids[:, g.slot, 0, :, :].rearrange("p u j -> p (u j)")
                    v.tensor_copy(t.src_of[:, bass.ds(g.n * NW, NW)], now)
                    v.tensor_copy(src_i[:, g.slot, :], now)
                    dve.wait_ge(ids_chain, g.n * 2 + 2)
                    v.scalar_tensor_tensor(out=local, in0=skip[:, g.slot, :, :], scalar=-float(4 * N_NODES), in1=local,
                                           op0=ALU.mult, op1=ALU.add).then_inc(ids_ready, 1)
                g = back(1)
                if g is not None:
                    dve.wait_ge(sig_ready, g.n + 1)
                    need(dve, gate_done, g.n - 1)
                    for m in range(2):
                        last = v.scalar_tensor_tensor(out=hid[:, g.slot, :, m, :], in0=psH[:, :, m, :], scalar=b1c[:, m:m + 1],
                                                      in1=sg[:, :, m, :], op0=ALU.add, op1=ALU.mult)
                    last.then_inc(hid_ready, 1)
                g = back(3)
                if g is not None:
                    dve.wait_ge(high_ready, g.n + 1)
                    v.scalar_tensor_tensor(out=msg_lo[:, g.slot, :, :], in0=msg[:, :, :], scalar=MSG_SCALE,
                                           in1=msg_hi[:, g.slot, :, 0:D], op0=ALU.mult, op1=ALU.subtract).then_inc(low_ready, 1)
                g = back(2)
                if g is not None:
                    dve.wait_ge(gate_ready, g.n + 1)
                    dve.wait_ge(hg_in[g.slot], (g.half + 1) * (16 * NW))
                    need(dve, high_ready, g.n)
                    need(dve, low_ready, g.n)
                    v.tensor_tensor(msg[:, :, :], gate[:, :, :], hg[:, g.slot, :, :], ALU.mult).then_inc(msg_ready, 1)
                    need(dve, sum_done, (g.n - 1) * TG)
                    v.tensor_tensor(hot[:, g.slot, :, :], t.cols[:, 0:P].rearrange("p (o c) -> p o c", o=1).to_broadcast([128, NW, P]),
                                    t.local_of[:, bass.ds(g.n * NW, NW)].rearrange("p (j o) -> p j o", o=1).to_broadcast([128, NW, P]),
                                    ALU.is_equal).then_inc(hot_ready, 1)
                g = back(4)
                if g is not None:
                    for u in range(TG):
                        n = g.n * TG + u
                        b = dve.value_load(t.group_bucket_i[0:1, bass.ds(n, 1)], min_val=0, max_val=NT - 1)
                        dve.wait_ge(sum_done, n + 1)
                        need(dve, sum_added, n)
                        at_b = t.sums[:, bass.ds(b, 1), :]
                        v.tensor_tensor(at_b, at_b, psA[0:P, u:u + 1, 0:D + 1], ALU.add).then_inc(sum_added, 1)

            pipeline(dve, TURNS, DEPTH, step)
            dve.wait_ge(sum_added, TG * TURNS)


def node_update(nc, t, src, dst, in_order, U1, c1, U2, c2):
    with ExitStack() as ctx:
        sb = lambda n, s, d: ctx.enter_context(nc.sbuf_tensor(n, s, d))
        pb = lambda n, s: ctx.enter_context(nc.psum_tensor(n, s, FP32))
        sem = lambda n: ctx.enter_context(nc.semaphore(n))
        u1 = sb("u1", [128, 4, D], FP32)
        u2 = sb("u2", [128, 2, D], FP32)
        c1c = sb("c1c", [128, 2], FP32)
        c2r = sb("c2r", [3, D], FP32)
        c2w = sb("c2w", [3, 3, D], FP32)
        c2p = sb("c2p", [3, D], BF16)
        cat = sb("cat", [P, 2, 2, D], FP32)
        catT = sb("catT", [128, 2, 4, P], FP32)
        sg = sb("sgu", [128, 2, P], FP32)
        hid = sb("hidu", [128, 2, P], FP32)
        psT = pb("psT1", [128, 4, P])
        psU = pb("psU", [128, 2, P])
        psV = pb("psV", [128, 512])
        names = ["w_in", "b_split", "chain", "sums_set", "turned", "copied", "up_done", "sig_ready", "hid_ready",
                 "down_done", "base_ready", "x1_ready", "stats_ready"]
        (w_in, b_split, chain, sums_set, turned, copied, up_done, sig_ready, hid_ready,
         down_done, base_ready, x1_ready, stats_ready) = (sem("u_" + n) for n in names)
        DEPTH = 2
        block = ctx.enter_context(nc.Block())

        @block.sync
        def _(sp):
            sp.dma_start(u1[:, :, :], U1.rearrange("(m p) n -> p m n", p=128)).then_inc(w_in, 16)
            sp.dma_start(u2[:, :, :], U2.rearrange("(m p) n -> p m n", p=128)).then_inc(w_in, 16)
            sp.dma_start(c1c[:, :], c1.rearrange("(m p) -> p m", p=128), allow_slow_non_contiguous=True).then_inc(w_in, 16)
            for r in range(3):
                sp.dma_start(c2r[r:r + 1, :], c2.rearrange("(o n) -> o n", o=1)).then_inc(w_in, 16)

            load_patches(sp, t, (0, SHARE[0]), src, dst, in_order, t.patches_in)

        @block.gpsimd
        def _(pool):
            def step(back):
                g = back(0)
                if g is not None:
                    need(pool, turned, g.n - 1)
                    pool.tensor_copy(cat[:, g.slot, 0, :], t.h[:, bass.ds(g.n, 1), :].rearrange("p o d -> p (o d)")).then_inc(sums_set, 1)
                    pool.tensor_copy(cat[:, g.slot, 1, :], t.sums[:, bass.ds(g.n, 1), 0:D].rearrange("p o d -> p (o d)")).then_inc(sums_set, 1)

            pipeline(pool, NT, DEPTH, step)

        @block.tensor
        def _(pe):
            pe.wait_ge(w_in, 6 * 16)
            pe.wait_ge(b_split, 1)

            def step(back):
                g = back(0)
                if g is not None:
                    pe.wait_ge(sums_set, g.n * 2 + 2)
                    need(pe, copied, g.n)
                    for m in range(4):
                        last = nc.tensor.transpose(psT[:, m, :], cat[:, g.slot, m // 2, (m % 2) * 128:(m % 2 + 1) * 128],
                                                   t.ident[0:P, 0:P])
                    last.then_inc(turned, 1)
                g = back(1)
                if g is not None:
                    pe.wait_ge(copied, g.n + 1)
                    need(pe, hid_ready, g.n)
                    for o in range(2):
                        for m in range(4):
                            last = nc.tensor.matmul(psU[:, o, :], u1[:, m, o * 128:(o + 1) * 128], catT[:, g.slot, m, :],
                                                    start=(m == 0), stop=(m == 3))
                    last.then_inc(up_done, 1)
                g = back(2)
                if g is not None:
                    pe.wait_ge(hid_ready, g.n + 1)
                    need(pe, x1_ready, g.n)
                    for m in range(2):
                        nc.tensor.matmul(psV[0:P, 0:D], hid[:, m, :], u2[:, m, :], start=(m == 0), stop=False)
                    nc.tensor.matmul(psV[0:P, 0:D], t.ones_h[0:3, 0:P], c2p[:, :], start=False, stop=True).then_inc(down_done, 1)

            pipeline(pe, NT, DEPTH, step)

        @block.scalar
        def _(act):
            act.wait_ge(w_in, 6 * 16)

            def step(back):
                g = back(0)
                if g is not None:
                    act.wait_ge(turned, g.n + 1)
                    need(act, up_done, g.n - 1)
                    nc.scalar.copy(catT[:, g.slot, 0:2, :], psT[:, 0:2, :])
                    nc.scalar.mul(catT[:, g.slot, 2:4, :], psT[:, 2:4, :], 1.0 / MSG_SCALE).then_inc(copied, 1)
                g = back(1)
                if g is not None:
                    act.wait_ge(up_done, g.n + 1)
                    need(act, hid_ready, g.n)
                    for m in range(2):
                        last = nc.scalar.activation(sg[:, m, :], psU[:, m, :], ACT.Sigmoid, bias=c1c[:, m:m + 1])
                    last.then_inc(sig_ready, 1)

            pipeline(act, NT, DEPTH, step)

        @block.vector
        def _(dve):
            link = Link(dve, chain)
            v = nc.vector
            dve.wait_ge(w_in, 6 * 16)
            split_row(nc, link, t, c2p, c2r, c2w)
            dve.sem_inc(b_split, 1)
            v.tensor_tensor(t.x1[:, :, :], t.x1[:, :, :], t.h[:, :, :], ALU.add).then_inc(base_ready, 1)
            dve.wait_ge(base_ready, 1)

            def step(back):
                g = back(1)
                if g is not None:
                    dve.wait_ge(sig_ready, g.n + 1)
                    need(dve, down_done, g.n)
                    for m in range(2):
                        last = v.scalar_tensor_tensor(out=hid[:, m, :], in0=psU[:, m, :], scalar=c1c[:, m:m + 1],
                                                      in1=sg[:, m, :], op0=ALU.add, op1=ALU.mult)
                    last.then_inc(hid_ready, 1)
                g = back(2)
                if g is not None:
                    one = lambda a: a.rearrange("p (o d) -> p o d", o=1)
                    x1 = t.x1[:, bass.ds(g.n, 1), :]
                    dve.wait_ge(down_done, g.n + 1)
                    need(dve, x1_ready, g.n)
                    v.tensor_tensor(x1, x1, one(psV[0:P, 0:D]), ALU.add).then_inc(x1_ready, 1)
                g = back(3)
                if g is not None:
                    if isinstance(g.n, int) and g.n == NT - 1:
                        dve.wait_ge(x1_ready, NT)
                    v.bn_stats(t.moments[:, bass.ds(g.n, 1), :].rearrange("p o d -> p (o d)"),
                               t.x1[:, bass.ds(g.n, 1), :].rearrange("p o d -> p (o d)")).then_inc(stats_ready, 1)

            pipeline(dve, NT, DEPTH + 1, step)
            dve.wait_ge(stats_ready, NT)


def node_input(nc, t, x1_dram, y_dram, src, dst, in_order, Win, bin_):
    with ExitStack() as ctx:
        sb = lambda n, s, d: ctx.enter_context(nc.sbuf_tensor(n, s, d))
        pb = lambda n, s: ctx.enter_context(nc.psum_tensor(n, s, FP32))
        sem = lambda n: ctx.enter_context(nc.semaphore(n))
        wi = sb("wi", [128, 2, D], FP32)
        bir = sb("bir", [3, D], FP32)
        biw = sb("biw", [3, 3, D], FP32)
        bip = sb("bip", [3, D], BF16)
        mv = sb("mv2", [P, NT, 2], FP32)
        rstd = sb("rstd2", [P, NT], FP32)
        nmr = sb("nmr2", [P, NT], FP32)
        h2 = sb("h2", [P, 2, CH, D], FP32)
        hT = sb("hT", [128, 2, 2 * CH * P], FP32)
        sg = sb("sgi", [P, CH, D], FP32)
        y = sb("y", [P, NT, D], FP32)
        chunk_max = sb("chunk_max", [P, NCHUNK], FP32)
        psT = pb("psT2", [128, 3, 512])
        psY = pb("psY", [128, 3, 512])
        names = ["w_in", "b_split", "chain", "var_ready", "std_ready", "norm_ready", "h_ready", "turned", "copied", "in_done",
                 "sig_ready", "y_ready", "chunk_done", "cleared", "max_ready", "x1_stored", "stored"]
        (w_in, b_split, chain, var_ready, std_ready, norm_ready, h_ready, turned_, copied, in_done,
         sig_ready, y_ready, chunk_done, cleared, max_ready, x1_stored, stored) = (sem("i_" + n) for n in names)
        DEPTH = 1
        block = ctx.enter_context(nc.Block())

        @block.sync
        def _(sp):
            sp.dma_start(wi[:, :, :], Win.rearrange("(m p) n -> p m n", p=128)).then_inc(w_in, 16)
            for r in range(3):
                sp.dma_start(bir[r:r + 1, :], bin_.rearrange("(o n) -> o n", o=1)).then_inc(w_in, 16)
            sp.dma_start(x1_dram.rearrange("(n p) d -> p n d", p=P), t.x1[:, :, :]).then_inc(x1_stored, 16)
            load_patches(sp, t, (SHARE[0], SHARE[1]), src, dst, in_order, t.patches_in)
            sp.wait_ge(x1_stored, 16)

        @block.gpsimd
        def _(pool):
            pool.memset(t.big[:, :], 0.0).then_inc(cleared, 1)
            load_patches(pool, t, (SHARE[1], SHARE[2]), src, dst, in_order, t.patches_in_too)

        @block.tensor
        def _(pe):
            def step(back):
                g = back(0)
                if g is not None:
                    pe.wait_ge(h_ready, g.n + 1)
                    need(pe, copied, g.n)
                    turn_chunk(nc, psT, h2[:, g.slot, :, :], t.ident).then_inc(turned_, 1)
                g = back(1)
                if g is not None:
                    if isinstance(g.n, int) and g.n == 0:
                        pe.wait_ge(w_in, 4 * 16)
                        pe.wait_ge(b_split, 1)
                    pe.wait_ge(copied, g.n + 1)
                    need(pe, y_ready, g.n)
                    multiply_chunk(nc, psY, hT[:, g.slot, :], wi, t.ones_h, bip).then_inc(in_done, 1)

            pipeline(pe, NCHUNK, DEPTH, step)

        @block.scalar
        def _(act):
            act.wait_ge(var_ready, 1)
            nc.scalar.activation(rstd[:, :], nmr[:, :], ACT.Sqrt).then_inc(std_ready, 1)
            act.wait_ge(norm_ready, 1)

            def step(back):
                g = back(0)
                if g is not None:
                    need(act, turned_, g.n - 1)
                    for n in range(CH):
                        at = bass.ds(g.n * CH + n, 1)
                        last = nc.scalar.activation(h2[:, g.slot, n, :], t.x1[:, at, :].rearrange("p o d -> p (o d)"), ACT.Relu,
                                                    bias=nmr[:, at], scale=rstd[:, at])
                    last.then_inc(h_ready, 1)
                g = back(1)
                if g is not None:
                    act.wait_ge(in_done, g.n + 1)
                    need(act, y_ready, g.n)
                    for of, to in products(psY, sg[:, :, :]):
                        last = nc.scalar.activation(to, of, ACT.Sigmoid)
                    last.then_inc(sig_ready, 1)
                g = back(2)
                if g is not None:
                    act.wait_ge(y_ready, g.n + 1)
                    act.dma_start(y_v[:, bass.ds(g.n * CH, CH), :], y[:, bass.ds(g.n * CH, CH), :]).then_inc(stored, 16)

            y_v = y_dram.rearrange("(n p) d -> p n d", p=P)
            pipeline(act, NCHUNK, DEPTH + 1, step)
            act.wait_ge(stored, 16 * NCHUNK)

        @block.vector
        def _(dve):
            link = Link(dve, chain)
            v = nc.vector
            for n in range(NT):
                last = v.bn_aggr(mv[:, n, :], t.moments[:, n, :])
            link(last)
            link(v.tensor_scalar(rstd[:, :], mv[:, :, 1], EPS, None, ALU.add))
            v.reciprocal(nmr[:, :], rstd[:, :]).then_inc(var_ready, 1)
            dve.wait_ge(std_ready, 1)
            v.scalar_tensor_tensor(out=nmr[:, :], in0=mv[:, :, 0], scalar=-1.0, in1=rstd[:, :],
                                   op0=ALU.mult, op1=ALU.mult).then_inc(norm_ready, 1)
            dve.wait_ge(w_in, 4 * 16)
            split_row(nc, link, t, bip, bir, biw)
            dve.sem_inc(b_split, 1)

            def step(back):
                g = back(0)
                if g is not None:
                    dve.wait_ge(turned_, g.n + 1)
                    need(dve, in_done, g.n - 1)
                    for of, to in turned(psT, hT[:, g.slot, :]):
                        last = v.tensor_copy(to, of)
                    last.then_inc(copied, 1)
                g = back(1)
                if g is not None:
                    dve.wait_ge(sig_ready, g.n + 1)
                    of_chunk = y[:, bass.ds(g.n * CH, CH), :]
                    for (of, gate), (_, to) in zip(products(psY, sg[:, :, :]), products(psY, of_chunk)):
                        last = v.tensor_tensor(to, of, gate, ALU.mult)
                    last.then_inc(y_ready, 1)
                    dve.wait_ge(y_ready, g.n + 1)
                    v.tensor_reduce(chunk_max[:, bass.ds(g.n, 1)], of_chunk, AX.XY, ALU.max, apply_absolute_value=True).then_inc(chunk_done, 1)

            pipeline(dve, NCHUNK, DEPTH, step)
            dve.wait_ge(chunk_done, NCHUNK)
            dve.wait_ge(cleared, 1)
            link(v.tensor_reduce(t.big[0:P, 0:1], chunk_max[:, :], AX.X, ALU.max))
            v.tensor_scalar(t.big[0:P, 0:1], t.big[0:P, 0:1], 2.0 ** -100, 2.0 ** 100, ALU.max, ALU.min).then_inc(max_ready, 1)
            dve.wait_ge(max_ready, 1)


def load_patches(eng, t, patches, src, dst, in_order, loaded):
    def load(src, dst):
        with eng.Fori(*patches) as n:
            row = eng.value_load(t.patch_row[0:1, bass.ds(n, 1)], min_val=0, max_val=N_EDGES - PW * WIN)
            for k, a in enumerate((src, dst)):
                eng.dma_start(t.patch_ids[:, k, bass.ds(n * PW, PW)],
                              a[bass.ds(row, PW * WIN)].rearrange("(p j) -> p j", j=PW)).then_inc(loaded, 16)

    with eng.If(eng.value_load(t.unsorted[0:1, 0:1], min_val=0, max_val=N_EDGES) > 0):
        load(in_order[0], in_order[1])
    with eng.Else():
        load(src, dst)


SHARE = (52, 87, NPATCH)


def count_edges(nc, t, y_dram, scaled_dram, pair_dram):
    with ExitStack() as ctx:
        sb = lambda n, s, d: ctx.enter_context(nc.sbuf_tensor(n, s, d))
        sem = lambda n: ctx.enter_context(nc.semaphore(n))
        NE = NPATCH * PW
        source = sb("source", [128, NE], FP32)
        first_i = sb("first_i", [128, NPATCH, PW], I32)
        local = sb("local", [128, NE], FP32)
        key = sb("key", [128, NE], FP32)
        part = sb("part", [128, NE], FP32)
        ok = source
        ys = sb("ys", [P, CH, HALF], FP32)
        ys_rest = sb("ys_rest", [P, CH, HALF], FP32)
        ys_pair = sb("ys_pair", [P, CH, 2 * HALF], FP16)
        cols_h = sb("cols_h", [128, KEYS], FP16)
        hot_part = sb("hot_part", [128, 2, PW, 128], FP16)
        hot_key = sb("hot_key", [128, 2, PW, KEYS], FP16)
        KH = (NT + 1) // 2
        ps = [ctx.enter_context(nc.psum_tensor(f"ps_count{i}", [128, 2, 512], FP32)) for i in range(2)]
        chain, made, part_ready, key_ready, window_done, taken = (
            sem("c_" + n) for n in ("chain", "made", "part_ready", "key_ready", "window_done", "taken"))
        tiles = lambda h: (0, KH) if h == 0 else (KH, NT)
        max_all, scale_set = sem("c_max_all"), sem("c_scale_set")
        ys_in, ys_scaled, ys_high, ys_left, ys_low, ys_out, pair_out = (
            sem("c_" + n) for n in ("ys_in", "ys_scaled", "ys_high", "ys_left", "ys_low", "ys_out", "pair_out"))
        by_half = lambda a: a.rearrange("(n p) (c d) -> c p n d", p=P, c=2)
        block = ctx.enter_context(nc.Block())
        parts = [(c, slice(k * CH, (k + 1) * CH)) for c in range(2) for k in range(NCHUNK)]

        @block.sync
        def _(sp):
            for i, (c, n) in enumerate(parts):
                if i > 0:
                    sp.wait_ge(ys_left, i)
                    sp.wait_ge(ys_out, 16 * i)
                sp.dma_start(ys[:, :, :], by_half(y_dram)[c][:, n, :]).then_inc(ys_in, 16)
                sp.wait_ge(ys_scaled, i + 1)
                sp.dma_start(by_half(scaled_dram)[c][:, n, :], ys[:, :, :]).then_inc(ys_out, 16)
                if c == 1:
                    sp.wait_ge(ys_low, i + 1)
                    sp.dma_start(pair_dram.rearrange("(n p) d -> p n d", p=P)[:, n, :], ys_pair[:, :, :]).then_inc(pair_out, 16)
            sp.wait_ge(ys_out, 16 * len(parts))
            sp.wait_ge(pair_out, 16 * NCHUNK)

        @block.gpsimd
        def _(pool):
            pool.iota(first_i[:, :, :], pattern=[[Q, NPATCH], [0, PW]], base=0, channel_multiplier=0).then_inc(made, 1)
            pool.iota(cols_h[:, :], pattern=[[1, KEYS]], base=0, channel_multiplier=0,
                      allow_small_or_imprecise_dtypes=True).then_inc(made, 1)
            pool.memset(t.counts[:, NT * N_NODES:NT * N_NODES + 8], 0.0).then_inc(made, 1)
            pool.partition_all_reduce(t.big[:, 1:2], t.big[:, 0:1], 128, bass.bass_isa.ReduceOp.max).then_inc(max_all, 1)
            pool.wait_ge(scale_set, 1)
            for i, (c, n) in enumerate(parts):
                pair = t.term[0][:, n, :] if c == 0 else ys_pair[:, :, :]
                pool.wait_ge(ys_in, 16 * (i + 1))
                pool.tensor_scalar(ys[:, :, :], ys[:, :, :], t.scale[0:P, 0:1], None, ALU.mult).then_inc(ys_scaled, 1)
                pool.wait_ge(ys_scaled, i + 1)
                if i > NCHUNK:
                    pool.wait_ge(pair_out, 16 * (i - NCHUNK))
                pool.tensor_copy(pair[:, :, 0:HALF], ys[:, :, :]).then_inc(ys_high, 1)
                pool.wait_ge(ys_high, i + 1)
                if i > 0:
                    pool.wait_ge(ys_low, i)
                pool.tensor_tensor(ys_rest[:, :, :], ys[:, :, :], pair[:, :, 0:HALF], ALU.subtract).then_inc(ys_left, 1)
                pool.wait_ge(ys_left, i + 1)
                pool.tensor_scalar(pair[:, :, HALF:2 * HALF], ys_rest[:, :, :], LOW, None, ALU.mult).then_inc(ys_low, 1)

        @block.tensor
        def _(pe):
            def step(back):
                g = back(0)
                if g is None:
                    return
                pe.wait_ge(part_ready, g.n + 1)
                need(pe, taken, g.n - 1)
                for j in range(PW):
                    pe.wait_ge(key_ready, g.n * PW + j + 1)
                    for h in range(2):
                        k0, k1 = tiles(h)
                        last = nc.tensor.matmul(ps[g.slot][:, h, 0:(k1 - k0) * Q], hot_part[:, g.slot, j, :],
                                                hot_key[:, g.slot, j, k0 * Q:k1 * Q], start=(j == 0), stop=(j == PW - 1))
                last.then_inc(window_done, 1)

            pipeline(pe, NPATCH, 0, step)

        @block.scalar
        def _(act):
            def take(b, c, slot):
                act.wait_ge(window_done, b * PPB + (c + 1))
                bucket = t.counts[0:P, bass.ds(b * N_NODES, N_NODES)].rearrange("p (k j) -> p k j", k=NT)
                for h in range(2):
                    k0, k1 = tiles(h)
                    last = nc.scalar.copy(bucket[:, k0:k1, c * Q:(c + 1) * Q],
                                          ps[slot][0:P, h, 0:(k1 - k0) * Q].rearrange("p (k j) -> p k j", j=Q))
                last.then_inc(taken, 1)

            with act.Fori(0, NT // 2) as pair:
                for n in range(2 * PPB):
                    take(pair * 2 + n // PPB, n % PPB, n % 2)
            for n in range((NT // 2) * 2 * PPB, NPATCH):
                take(n // PPB, n % PPB, n % 2)

        @block.vector
        def _(dve):
            link = Link(dve, chain)
            v = nc.vector
            flat = lambda a: a.rearrange("p n j -> p (n j)")
            dve.wait_ge(t.patches_in, 2 * 16 * SHARE[1])
            dve.wait_ge(t.patches_in_too, 2 * 16 * (SHARE[2] - SHARE[1]))
            link(v.tensor_copy(source[:, :], t.patch_ids[:, 0, :]))
            link(v.tensor_scalar(key[:, :], source[:, :], -float(P // 2), 1.0 / P, ALU.add, ALU.mult))
            link(v.tensor_scalar(key[:, :], key[:, :], MAGIC, None, ALU.add))
            link(v.tensor_scalar(key[:, :], key[:, :], MAGIC, None, ALU.subtract))
            link(v.scalar_tensor_tensor(out=part[:, :], in0=key[:, :], scalar=-float(P), in1=source[:, :],
                                        op0=ALU.mult, op1=ALU.add))
            dve.wait_ge(made, 3)
            link(v.tensor_tensor(local[:, :], t.patch_ids[:, 1, :], flat(first_i[:, :, :]), ALU.subtract))
            link(v.tensor_scalar(ok[:, :], local[:, :], 0.0, None, ALU.is_ge))
            link(v.scalar_tensor_tensor(out=ok[:, :], in0=local[:, :], scalar=float(Q), in1=ok[:, :],
                                        op0=ALU.is_lt, op1=ALU.mult))
            link(v.scalar_tensor_tensor(out=key[:, :], in0=key[:, :], scalar=float(Q), in1=local[:, :],
                                        op0=ALU.mult, op1=ALU.add))
            link(v.scalar_tensor_tensor(out=key[:, :], in0=key[:, :], scalar=1.0, in1=ok[:, :], op0=ALU.add, op1=ALU.mult))
            link(v.tensor_scalar(key[:, :], key[:, :], 1.0, None, ALU.subtract))
            dve.wait_ge(max_all, 1)
            bits = lambda c: t.big[:, c:c + 1].bitcast(I32)
            link(v.tensor_scalar(bits(2), bits(1), 0x7F800000, None, ALU.bitwise_and))
            link(v.tensor_scalar(t.scale[:, 0:1].bitcast(I32), bits(2), -1.0, float((254 + 13) << 23), ALU.mult, ALU.add))
            v.tensor_scalar(t.scale[:, 1:2].bitcast(I32), bits(2), float(13 << 23), None, ALU.subtract).then_inc(scale_set, 1)

            def step(back):
                g = back(0)
                if g is None:
                    return
                need(dve, window_done, g.n - 1)
                for j in range(PW):
                    last = v.tensor_scalar(hot_part[:, g.slot, j, :], t.cols[:, 0:128], part[:, bass.ds(g.n * PW + j, 1)],
                                           None, ALU.is_equal)
                last.then_inc(part_ready, 1)
                for j in range(PW):
                    v.tensor_scalar(hot_key[:, g.slot, j, :], cols_h[:, :], key[:, bass.ds(g.n * PW + j, 1)],
                                    None, ALU.is_equal).then_inc(key_ready, 1)

            pipeline(dve, NPATCH, 0, step)


def degrees(nc, t):
    with ExitStack() as ctx:
        sb = lambda n, s, d: ctx.enter_context(nc.sbuf_tensor(n, s, d))
        sem = lambda n: ctx.enter_context(nc.semaphore(n))
        deg = sb("deg", [P, NT], FP32)
        inv = sb("inv", [P, NT], FP32)
        place_i = sb("patch_place_i", [P, PPB], I32)
        place = sb("patch_place", [P, PPB], FP32)
        in_patch = sb("in_patch", [P, PPB], FP32)
        split = sb("deg_split", [P, NT, PPB], FP32)
        edges = sb("patch_edges", [128, NPATCH], FP32)
        start = sb("patch_start_f", [128, NPATCH], FP32)
        most = sb("most", [128, 1], FP32)
        ps = ctx.enter_context(nc.psum_tensor("ps_patch", [128, 512], FP32))
        chain, place_made, split_ready, summed = (sem("d_" + n) for n in ("chain", "place_made", "split_ready", "summed"))
        block = ctx.enter_context(nc.Block())

        @block.gpsimd
        def _(pool):
            pool.iota(place_i[:, :], pattern=[[-Q, PPB]], base=0, channel_multiplier=1).then_inc(place_made, 1)

        @block.tensor
        def _(pe):
            pe.wait_ge(split_ready, 1)
            nc.tensor.matmul(ps[:, 0:NPATCH], t.ones[0:P, :], split[:, :, :].rearrange("p b q -> p (b q)"),
                             start=True, stop=True).then_inc(summed, 1)

        @block.vector
        def _(dve):
            link = Link(dve, chain)
            v = nc.vector
            link(v.tensor_scalar(deg[:, :], t.sums[:, :, D], 1.0 / MSG_SCALE, None, ALU.mult))
            dve.wait_ge(place_made, 1)
            link(v.tensor_copy(place[:, :], place_i[:, :]))
            link(v.tensor_scalar(in_patch[:, :], place[:, :], 0.0, None, ALU.is_ge))
            link(v.scalar_tensor_tensor(out=in_patch[:, :], in0=place[:, :], scalar=float(Q), in1=in_patch[:, :],
                                        op0=ALU.is_lt, op1=ALU.mult))
            v.tensor_tensor(split[:, :, :], deg[:, :].rearrange("p (b o) -> p b o", o=1).to_broadcast([P, NT, PPB]),
                            in_patch[:, :].rearrange("p (o q) -> p o q", o=1).to_broadcast([P, NT, PPB]), ALU.mult).then_inc(split_ready, 1)
            link(v.tensor_scalar(inv[:, :], deg[:, :], 1.0, None, ALU.max))
            for i in range(NSTEPS):
                link(v.tensor_scalar(t.inv_deg[:, 1, i, :], inv[:, :], float(i + 1), None, ALU.mult))
                link(v.reciprocal(t.inv_deg[:, 0, i, :], t.inv_deg[:, 1, i, :]))
                link(v.tensor_scalar(t.inv_deg[:, 1, i, :], t.inv_deg[:, 0, i, :], 1.0 / LOW, None, ALU.mult))
            dve.wait_ge(summed, 1)
            link(v.tensor_copy(edges[:, :], ps[:, 0:NPATCH]))
            link(v.tensor_tensor_scan(start[:, :], t.ones[:, 0:NPATCH], edges[:, :], 0.0, ALU.mult, ALU.add))
            link(v.tensor_tensor(start[:, :], start[:, :], edges[:, :], ALU.subtract))
            link(v.tensor_scalar(t.patch_row[:, :], start[:, :], float(N_EDGES - PW * WIN), None, ALU.min))
            link(v.tensor_reduce(most[:, :], edges[:, :], AX.X, ALU.max))
            link(v.tensor_scalar(t.crowded[:, :], most[:, :], float(PW * WIN), None, ALU.is_gt))


def diffusion(nc, t, scaled_dram, pair_dram, d_dram):
    with ExitStack() as ctx:
        sb = lambda n, s, d: ctx.enter_context(nc.sbuf_tensor(n, s, d))
        sem = lambda n: ctx.enter_context(nc.semaphore(n))
        term = t.term
        acc = sb("acc", [P, NT, HALF], FP32)
        SL = 5
        low = sb("low_sum", [P, SL, HALF], FP32)
        rest = low
        val = sb("val", [P, SL, HALF], FP32)
        ps = [ctx.enter_context(nc.psum_tensor(f"ps_term{i}", [128, 512], FP32)) for i in range(SL)]
        names = ["turn_open", "pair_in", "y_in", "product", "low_ready", "val_ready", "high_ready", "rest_ready", "term_ready", "acc_ready", "stored"]
        turn_open, pair_in, y_in, product, low_ready, val_ready, high_ready, rest_ready, term_ready, acc_ready, stored = (
            sem("f_" + n) for n in names)
        y_v = scaled_dram.rearrange("(n p) (c d) -> c p n d", p=P, c=2)
        d_v = d_dram.rearrange("(n p) (c d) -> c p n d", p=P, c=2)
        PER = NT * NSTEPS
        PAIRS = NSTEPS // 2
        one = lambda a: a.rearrange("p (o d) -> p o d", o=1)
        block = ctx.enter_context(nc.Block())

        def steps(eng, do):
            for c in range(2):
                for i in range(NSTEPS):
                    at = (c * NSTEPS + i) * NT
                    for n in range(SL):
                        do(c, i, Turn(0, n, SL), at)
                    with eng.Fori(1, NT // SL) as k:
                        for n in range(SL):
                            do(c, i, Turn(k, n, SL), at)

        @block.sync
        def _(sp):
            sp.dma_start(acc[:, :, :], y_v[0]).then_inc(y_in, 16)
            sp.wait_ge(product, PER - NT)
            sp.dma_start(term[0][:, :, :], pair_dram.rearrange("(n p) d -> p n d", p=P)).then_inc(pair_in, 16)
            for c in range(2):
                for k in range(NCHUNK):
                    n = slice(k * CH, (k + 1) * CH)
                    sp.wait_ge(acc_ready, (c + 1) * PER - NT + (k + 1) * CH)
                    sp.dma_start(d_v[c][:, n, :], acc[:, n, :]).then_inc(stored, 16)
                    sp.wait_ge(stored, 16 * (c * NCHUNK + k + 1))
                    if c == 0:
                        sp.dma_start(acc[:, n, :], y_v[1][:, n, :]).then_inc(y_in, 16)

        @block.tensor
        def _(pe):
            with pe.Fori(0, 2 * PAIRS) as r:
                for odd in range(2):
                    if odd == 0:
                        pe.wait_ge(turn_open, r + 1)
                    for n in range(NT):
                        m = odd * NT + n
                        if m >= SL:
                            pe.wait_ge(val_ready, r * (2 * NT) + (m - SL + 1))
                        for k in range(NT):
                            if n == 0 and (k == 0 or k > NT - SL):
                                pe.wait_ge(term_ready, r * (2 * NT) + (m + max(k, NT - SL) + 1))
                            last = nc.tensor.matmul(ps[m % SL][:, 0:2 * HALF],
                                                    t.counts[0:P, n * N_NODES + k * P:n * N_NODES + k * P + 128],
                                                    term[odd][:, k, :], start=(k == 0), stop=(k == NT - 1))
                        last.then_inc(product, 1)

        @block.scalar
        def _(act):
            def do(c, i, g, at):
                n = g.n + at
                q = g.slot
                act.wait_ge(product, n + 1)
                need(act, val_ready, n - SL + 1)
                nc.scalar.activation(low[:, q, :], ps[q][0:P, HALF:2 * HALF], ACT.Copy,
                                     scale=t.inv_deg[:, 1, i, bass.ds(g.n, 1)]).then_inc(low_ready, 1)
                if i < NSTEPS - 1:
                    made = term[(i + 1) % 2]
                    act.wait_ge(val_ready, n + 1)
                    nc.scalar.copy(made[:, bass.ds(g.n, 1), 0:HALF], one(val[:, q, :])).then_inc(high_ready, 1)
                    act.wait_ge(rest_ready, n - c * NT + 1)
                    nc.scalar.mul(made[:, bass.ds(g.n, 1), HALF:2 * HALF], one(rest[:, q, :]), LOW).then_inc(term_ready, 1)

            steps(act, do)

        @block.vector
        def _(dve):
            v = nc.vector
            dve.sem_inc(term_ready, NT)

            def do(c, i, g, at):
                if i % 2 == 0 and isinstance(g.n, int) and g.n == 0:
                    if at > 0:
                        dve.wait_ge(val_ready, at)
                    dve.sem_inc(turn_open, 1)
                if i == 0 and isinstance(g.n, int) and g.n == 0:
                    dve.wait_ge(y_in, 16 * (1 + c * NCHUNK))
                n = g.n + at
                q = g.slot
                dve.wait_ge(low_ready, n + 1)
                if not isinstance(n, int) or n >= SL:
                    dve.wait_ge(acc_ready, n - SL + 1)
                v.scalar_tensor_tensor(out=val[:, q, :], in0=ps[q][0:P, 0:HALF], scalar=t.inv_deg[:, 0, i, bass.ds(g.n, 1)],
                                       in1=low[:, q, :], op0=ALU.mult, op1=ALU.add).then_inc(val_ready, 1)
                if i < NSTEPS - 1:
                    dve.wait_ge(high_ready, n - c * NT + 1)
                    v.tensor_tensor(rest[:, q, :], val[:, q, :], term[(i + 1) % 2][:, bass.ds(g.n, 1), 0:HALF].rearrange("p o d -> p (o d)"),
                                    ALU.subtract).then_inc(rest_ready, 1)
                else:
                    dve.wait_ge(val_ready, n + 1)
                a = acc[:, bass.ds(g.n, 1), :]
                v.tensor_tensor(a, a, one(val[:, q, :]), ALU.add).then_inc(acc_ready, 1)
                if c == 0 and i == NSTEPS - 1 and isinstance(g.n, int) and g.n == SL - 1:
                    dve.wait_ge(pair_in, 16)
                    dve.wait_ge(term_ready, PER)
                    dve.sem_inc(term_ready, NT)

            steps(dve, do)
            dve.wait_ge(acc_ready, 2 * PER)


def gathered_diffusion(nc, t, y_dram, term_dram, d_dram):
    with ExitStack() as ctx:
        sb = lambda n, s, d: ctx.enter_context(nc.sbuf_tensor(n, s, d))
        sem = lambda n: ctx.enter_context(nc.semaphore(n))
        acc = sb("acc_all", [P, NT, D], FP32)
        total = sb("total", [P, NT, D], FP32)
        rows = sb("rows", [128, 2, GW, D], FP32)
        idx = sb("row_idx", [128, 2, GW], I32)
        hot = sb("hot_row", [128, 2, GW, P], FP32)
        ps = [ctx.enter_context(nc.psum_tensor(f"ps_gather{i}", [128, 512], FP32)) for i in range(2)]
        names = ["chain", "acc_in", "ids_ready", "hot_ready", "product", "added", "term_ready", "stored", "passed", "scaled", "out_done"]
        chain, acc_in, ids_ready, hot_ready, product, added, term_ready, stored, passed, scaled, out_done = (sem("e_" + n) for n in names)
        rows_in = [sem("rows_in0"), sem("rows_in1")]
        tiled = lambda a: a.rearrange("(n p) d -> p n d", p=P)
        block = ctx.enter_context(nc.Block())
        crowded = lambda eng: eng.If(eng.value_load(t.crowded[0:1, 0:1], min_val=0, max_val=1) > 0)

        @block.sync
        def _(sp):
            with crowded(sp):
                sp.dma_start(acc[:, :, :], tiled(y_dram)).then_inc(acc_in, 16)
                for i in range(NSTEPS):
                    sp.wait_ge(term_ready, i + 1)
                    sp.dma_start(tiled(term_dram), total[:, :, :]).then_inc(stored, 16)
                sp.wait_ge(scaled, 1)
                sp.dma_start(tiled(d_dram), acc[:, :, :]).then_inc(out_done, 16)
                sp.wait_ge(stored, 16 * NSTEPS)
                sp.wait_ge(out_done, 16)

        @block.gpsimd
        def _(pool):
            with crowded(pool):
                pool.memset(t.gate_cell[:, :], 0.0).then_inc(passed, 1)
                for i in range(NSTEPS):
                    def step(back):
                        g = back(0)
                        if g is None:
                            return
                        n = g.n + i * NG
                        need(pool, product, n - 1)
                        pool.wait_ge(ids_ready, n + 1)
                        if i > 0 and isinstance(g.n, int):
                            pool.wait_ge(stored, 16 * i)
                        pool.wait_ge(passed, n + 1)
                        pool.tensor_tensor(t.gate_cell[:, 1:2], t.gate_cell[:, 0:1], t.gate_cell[:, 0:1], ALU.add).then_inc(passed, 1)
                        for j in range(GW):
                            pool.indirect_dma_start(
                                out=rows[:, g.slot, j, :], out_offset=None, in_=(term_dram if i else y_dram)[:, :],
                                in_offset=bass.IndirectOffsetOnAxis(ap=idx[:, g.slot, j:j + 1].bitcast(U32), axis=0)
                            ).then_inc(rows_in[g.slot], 16)

                    pipeline(pool, NG, 0, step)

        landed = lambda i, g: (g.half + i * (NG // 2)) * (16 * GW)

        @block.tensor
        def _(pe):
            with crowded(pe):
                for i in range(NSTEPS):
                    def step(back):
                        g = back(0)
                        if g is None:
                            return
                        n = g.n + i * NG
                        pe.wait_ge(rows_in[g.slot], landed(i, g) + 16 * GW)
                        pe.wait_ge(hot_ready, n + 1)
                        need(pe, added, n - 1 + (i + 1) if not isinstance(n, int) or n > 1 else 0)
                        for j in range(GW):
                            last = nc.tensor.matmul(ps[g.slot][0:P, 0:D], hot[:, g.slot, j, :], rows[:, g.slot, j, :],
                                                    start=(j == 0), stop=(j == GW - 1))
                        last.then_inc(product, 1)

                    pipeline(pe, NG, 0, step)

        @block.vector
        def _(dve):
            v = nc.vector
            with crowded(dve):
                for i in range(NSTEPS):
                    if i > 0:
                        dve.wait_ge(stored, 16 * i)
                    v.memset(total[:, :, :], 0.0).then_inc(added, 1)

                    def step(back):
                        g = back(0)
                        if g is not None:
                            n = g.n + i * NG
                            need(dve, rows_in[g.slot], landed(i, g))
                            v.tensor_copy(idx[:, g.slot, :], t.src_of[:, bass.ds(g.n * GW, GW)]).then_inc(ids_ready, 1)
                            need(dve, product, n - 1)
                            v.tensor_tensor(hot[:, g.slot, :, :], t.cols[:, 0:P].rearrange("p (o c) -> p o c", o=1).to_broadcast([128, GW, P]),
                                            t.local_of[:, bass.ds(g.n * GW, GW)].rearrange("p (j o) -> p j o", o=1).to_broadcast([128, GW, P]),
                                            ALU.is_equal).then_inc(hot_ready, 1)
                        g = back(1)
                        if g is not None:
                            n = g.n + i * NG
                            b = dve.value_load(t.group_bucket_i[0:1, bass.ds(g.n, 1)], min_val=0, max_val=NT - 1)
                            dve.wait_ge(product, n + 1)
                            dve.wait_ge(added, n + (i + 1))
                            at_b = total[:, bass.ds(b, 1), :]
                            v.tensor_tensor(at_b, at_b, ps[g.slot][0:P, 0:D].rearrange("p (o d) -> p o d", o=1), ALU.add).then_inc(added, 1)

                    pipeline(dve, NG, 1, step)
                    dve.wait_ge(added, (i + 1) * (NG + 1))
                    v.tensor_tensor(total[:, :, :], total[:, :, :],
                                    t.inv_deg[:, 0, i, :].rearrange("p (n o) -> p n o", o=1).to_broadcast([P, NT, D]),
                                    ALU.mult).then_inc(term_ready, 1)
                    dve.wait_ge(term_ready, i + 1)
                    if i == 0:
                        dve.wait_ge(acc_in, 16)
                    else:
                        dve.wait_ge(chain, i)
                    v.tensor_tensor(acc[:, :, :], acc[:, :, :], total[:, :, :], ALU.add).then_inc(chain, 1)
                    dve.wait_ge(chain, i + 1)
                v.tensor_scalar(acc[:, :, :], acc[:, :, :], t.scale[0:P, 0:1], None, ALU.mult).then_inc(scaled, 1)




def turn_chunk(nc, psT, src, ident):
    for u in range(2 * CH):
        last = nc.tensor.transpose(psT[:, u // 4, (u % 4) * P:(u % 4 + 1) * P],
                                   src[:, u // 2, (u % 2) * 128:(u % 2 + 1) * 128], ident[0:P, 0:P])
    return last


def turned(psT, out):
    full = 2 * CH // 4
    return [(psT[:, 0:full, 0:4 * P], out[:, 0:full * 4 * P].rearrange("p (b c) -> p b c", b=full)),
            (psT[:, full, 0:(2 * CH - 4 * full) * P], out[:, full * 4 * P:2 * CH * P])]


def multiply_chunk(nc, psO, xT, w, ones, bias_parts):
    for n in range(CH):
        to = psO[0:P, n // 2, (n % 2) * D:(n % 2 + 1) * D]
        for m in range(2):
            u = 2 * n + m
            nc.tensor.matmul(to, xT[:, u * P:(u + 1) * P], w[:, m, :], start=(m == 0), stop=False)
        last = nc.tensor.matmul(to, ones[0:3, 0:P], bias_parts[:, :], start=False, stop=True)
    return last


def products(psO, tiles):
    even = CH // 2
    return [(psO[0:P, 0:even, :].rearrange("p b (h d) -> p (b h) d", h=2), tiles[:, 0:2 * even, :]),
            (psO[0:P, even:even + 1, 0:D], tiles[:, 2 * even:CH, :])]


def node_output(nc, t, x1_dram, d_dram, Wout, bout, out):
    with ExitStack() as ctx:
        sb = lambda n, s, d: ctx.enter_context(nc.sbuf_tensor(n, s, d))
        pb = lambda n, s: ctx.enter_context(nc.psum_tensor(n, s, FP32))
        sem = lambda n: ctx.enter_context(nc.semaphore(n))
        wo = sb("wo", [128, 2, D], FP32)
        bor = sb("bor", [3, D], FP32)
        bow = sb("bow", [3, 3, D], FP32)
        bop = sb("bop", [3, D], BF16)
        acc = sb("acc_out", [P, NCHUNK, CH, D], FP32)
        x1 = sb("x1_out", [P, NCHUNK, CH, D], FP32)
        dT = sb("dT", [128, 2, 2 * CH * P], FP32)
        psT = pb("psT3", [128, 3, 512])
        psO = pb("psO", [128, 3, 512])
        names = ["w_in", "b_split", "chain", "turned", "copied", "out_done", "res_ready"]
        w_in, b_split, chain, turned_, copied, out_done, res_ready = (sem("o_" + n) for n in names)
        acc_in = [sem(f"acc_in{c}") for c in range(NCHUNK)]
        x1_in = [sem(f"x1_in{c}") for c in range(NCHUNK)]
        stored = sem("out_stored")
        block = ctx.enter_context(nc.Block())
        rows = lambda a, c: a.rearrange("(c n p) d -> c p n d", n=CH, p=P)[c]

        @block.sync
        def _(sp):
            for c in range(NCHUNK):
                sp.dma_start(acc[:, c, :, :], rows(d_dram, c)).then_inc(acc_in[c], 16)
                if c == 0:
                    sp.dma_start(wo[:, :, :], Wout.rearrange("(m p) n -> p m n", p=128)).then_inc(w_in, 16)
                sp.dma_start(x1[:, c, :, :], rows(x1_dram, c)).then_inc(x1_in[c], 16)
            for c in range(NCHUNK):
                sp.wait_ge(res_ready, c + 1)
                sp.dma_start(rows(out, c), x1[:, c, :, :]).then_inc(stored, 16)
            sp.wait_ge(stored, 16 * NCHUNK)

        @block.tensor
        def _(pe):
            for c in range(NCHUNK + 1):
                if c < NCHUNK:
                    pe.wait_ge(acc_in[c], 16)
                    if c > 0:
                        pe.wait_ge(copied, c)
                    turn_chunk(nc, psT, acc[:, c, :, :], t.ident).then_inc(turned_, 1)
                if c > 0:
                    if c == 1:
                        pe.wait_ge(w_in, 4 * 16)
                        pe.wait_ge(b_split, 1)
                    pe.wait_ge(copied, c)
                    if c > 1:
                        pe.wait_ge(res_ready, c - 1)
                    multiply_chunk(nc, psO, dT[:, (c - 1) % 2, :], wo, t.ones_h, bop).then_inc(out_done, 1)

        @block.scalar
        def _(act):
            for r in range(3):
                act.dma_start(bor[r:r + 1, :], bout.rearrange("(o n) -> o n", o=1)).then_inc(w_in, 16)
            for c in range(NCHUNK):
                act.wait_ge(turned_, c + 1)
                if c > 1:
                    act.wait_ge(out_done, c - 1)
                for of, to in turned(psT, dT[:, c % 2, :]):
                    last = nc.scalar.activation(to, of, ACT.Copy, scale=t.scale[:, 1:2])
                last.then_inc(copied, 1)

        @block.vector
        def _(dve):
            link = Link(dve, chain)
            dve.wait_ge(w_in, 4 * 16)
            split_row(nc, link, t, bop, bor, bow)
            dve.sem_inc(b_split, 1)
            for c in range(NCHUNK):
                dve.wait_ge(out_done, c + 1)
                dve.wait_ge(x1_in[c], 16)
                for of, to in products(psO, x1[:, c, :, :]):
                    last = nc.vector.tensor_tensor(to, to, of, ALU.add)
                last.then_inc(res_ready, 1)


class Tables:
    pass


def gnn_kernel(nc, x, src, dst, attr, W1, b1, W2, b2, U1, c1, U2, c2, Win, bin_, Wout, bout, out):
    dram = lambda n, s: nc.dram_tensor(n, s, FP32).ap()
    h_dram = dram("h_nodes", [N_NODES, D])
    in_order = (nc.dram_tensor("src_in_order", [N_EDGES], I32).ap(), nc.dram_tensor("dst_in_order", [N_EDGES], I32).ap(),
                dram("attr_in_order", [N_EDGES, R]))
    x1_dram = dram("x1_nodes", [N_NODES, D])
    y_dram = dram("y_nodes", [N_NODES, D])
    scaled_dram = dram("y_scaled", [N_NODES, D])
    pair_dram = nc.dram_tensor("y_pairs", [N_NODES, D], FP16).ap()
    d_dram = dram("diffused", [N_NODES, D])
    term_dram = dram("gathered_term", [N_NODES, D])
    t = Tables()
    with ExitStack() as ctx:
        keep = lambda scope: (lambda n, s, d: scope.enter_context(nc.sbuf_tensor(n, s, d)))
        sb = keep(ctx)
        t.ident = sb("ident", [128, 128], FP32)
        t.ones_h = sb("ones_h", [128, 128], BF16)
        t.gate_cell = sb("gate_cell", [1, 2], FP32)
        t.cols = sb("cols", [128, COLS], FP32)
        t.group_bucket_i = sb("group_bucket_i", [128, NG], I32)
        t.unsorted = sb("unsorted", [128, 1], I32)
        t.scale = sb("scale", [128, 2], FP32)
        t.big = sb("big", [128, 4], FP32)
        t.inv_deg = sb("inv_deg", [P, 2, NSTEPS, NT], FP32)
        t.crowded = sb("crowded", [128, 1], I32)
        t.patch_row = sb("patch_row", [128, NPATCH], I32)
        t.patch_ids = sb("patch_ids", [128, 2, NPATCH * PW], I32)
        t.src_of = sb("src_of", [128, NG * GW], FP32)
        t.local_of = sb("local_of", [128, NG * GW], FP32)
        t.patches_in = ctx.enter_context(nc.semaphore("patches_in"))
        t.patches_in_too = ctx.enter_context(nc.semaphore("patches_in_too"))
        with ExitStack() as nodes:
            sb = keep(nodes)
            t.before = sb("before", [128, 128], FP32)
            t.ones = sb("ones", [128, 128], FP32)
            t.place_i = sb("place_i", [128, TG, GW], I32)
            t.place = sb("place", [128, TG, GW], FP32)
            t.group_row = sb("group_row", [128, NG], I32)
            t.group_bucket = sb("group_bucket", [128, NG], FP32)
            t.group_skip = sb("group_skip", [128, NG], FP32)
            t.bucket_node = sb("bucket_node", [128, NG], FP32)
            with ExitStack() as edges:
                sb = keep(edges)
                t.dst_i = sb("dst_i", [P, EC], I32)
                t.dst_f = sb("dst_f", [P, EC], FP32)
                t.cols_i = sb("cols_i", [128, COLS], I32)
                prepare(nc, t, x, src, dst, h_dram)
                edge_sort(nc, t, src, attr, in_order)
            t.sums = nodes.enter_context(nc.sbuf_tensor("sums", [P, NT, D + 1], FP32))
            t.x1 = nodes.enter_context(nc.sbuf_tensor("x1", [P, NT, D], FP32))
            t.h = nodes.enter_context(nc.sbuf_tensor("h", [P, NT, D], FP32))
            edge_messages(nc, t, x, h_dram, src, dst, attr, in_order, W1, b1, W2, b2)
            t.moments = nodes.enter_context(nc.sbuf_tensor("moments", [P, NT, 6], FP32))
            degrees(nc, t)
            node_update(nc, t, src, dst, in_order, U1, c1, U2, c2)
            node_input(nc, t, x1_dram, y_dram, src, dst, in_order, Win, bin_)
        with ExitStack() as graph:
            t.counts = graph.enter_context(nc.sbuf_tensor("counts", [128, NT * N_NODES + 8], FP16))
            t.term = [graph.enter_context(nc.sbuf_tensor("term0", [P, NT, 2 * HALF], FP16))]
            count_edges(nc, t, y_dram, scaled_dram, pair_dram)
            t.term.append(graph.enter_context(nc.sbuf_tensor("term1", [P, NT, 2 * HALF], FP16)))
            diffusion(nc, t, scaled_dram, pair_dram, d_dram)
        gathered_diffusion(nc, t, y_dram, term_dram, d_dram)
        node_output(nc, t, x1_dram, d_dram, Wout, bout, out)


_INS = ["x", "src", "dst", "edge_attr_64", "L0_gnn_W1", "L0_gnn_b1", "L0_gnn_W2", "L0_gnn_b2", "L0_gnn_U1", "L0_gnn_c1",
        "L0_gnn_U2", "L0_gnn_c2", "L1_gnn_W_in", "L1_gnn_b_in", "L1_gnn_W_out", "L1_gnn_b_out"]


def kernel(**inputs):
    import numpy as _np
    import concourse.bacc as _bacc
    from concourse import mybir as _mybir
    from concourse.bass_utils import run_bass_kernel_spmd as _run

    nc = _bacc.Bacc("TRN2", target_bir_lowering=False, num_devices=1)
    arrays, args = {}, []
    for name in _INS:
        a = _np.asarray(inputs[name])
        if name in ("L1_gnn_W_in", "L1_gnn_W_out"):
            a = a.T
        a = _np.ascontiguousarray(a)
        arrays[f"in_{name}"] = a
        args.append(nc.dram_tensor(f"in_{name}", a.shape, _mybir.dt.from_np(a.dtype), kind="ExternalInput").ap())
    args.append(nc.dram_tensor("out_0", (N_NODES, D), FP32, kind="ExternalOutput").ap())
    gnn_kernel(nc, *args)
    r = _run(nc, [arrays], core_ids=[0])
    return r.results[0]["out_0"]
```
